# Optimizing a Trainium2 kernel written in Bass

```python
import numpy as np
import jax
import jax.numpy as jnp

def _softmax(x, axis=-1):
    return jax.nn.softmax(x, axis=axis)

def _gelu(x):
    return jax.nn.gelu(x, approximate=True)

def _silu(x):
    return jax.nn.silu(x)

def _sigmoid(x):
    return jax.nn.sigmoid(x)

def _layernorm(x, axis=-1, eps=1e-05):
    m = jnp.mean(x, axis=axis, keepdims=True)
    v = jnp.var(x, axis=axis, keepdims=True)
    return (x - m) / jnp.sqrt(v + eps)

def _scatter_add(tgt, idx, src, axis=0):
    return tgt.at[idx].add(src)

def _segment_sum(src, seg, n):
    return jax.ops.segment_sum(src, seg, n)
kernel_name = 'mk_flamingo_gated_d2_seqx_r8_62fad8'

def setup_inputs(seed: int=0):
    np.random.seed(seed)
    _w = jnp.asarray

    def _rec_inputs():
        import jax
        import jax.numpy as jnp
        _rk = jax.random.key(seed)
        x = -0.0002928 + 1 * jax.random.normal(jax.random.fold_in(_rk, 1), (128, 64, 128), jnp.float32)
        _lenS = 64 - jax.random.randint(jax.random.fold_in(_rk, 7), (128,), 0, max(1, 64 // 4) + 1, jnp.int32)
        _lenS2 = 64 - jax.random.randint(jax.random.fold_in(_rk, 8), (128,), 0, max(1, 64 // 4) + 1, jnp.int32)
        _ctx_1024P = jax.random.normal(jax.random.fold_in(_rk, 11), (128, 16, 128), jnp.float32)
        _ctx_1024c = jax.random.dirichlet(jax.random.fold_in(_rk, 511), 0.3 * jnp.ones((16,), jnp.float32), (128, 64))
        _ctx_1024t = jnp.einsum('bsk,bkd->bsd', _ctx_1024c, _ctx_1024P)
        _ctx_1024t = _ctx_1024t * jax.lax.rsqrt(jnp.mean(jnp.square(_ctx_1024t)) + 1e-12) * 0.953939
        ctx_1024 = -1.39393e-06 + 0.999914 * (_ctx_1024t + 0.3 * jax.random.normal(jax.random.fold_in(_rk, 611), (128, 64, 128), jnp.float32))
        _validS = jnp.arange(64)[None, :] < _lenS[:, None]
        _validS2 = jnp.arange(64)[None, :] < _lenS2[:, None]
        _causal = jnp.tril(jnp.ones((64, 64), dtype=bool))
        mask_BxS2_bf0 = jnp.logical_not(jnp.ones((128, 64), dtype=bool))
        _g = jax.random.normal(jax.random.fold_in(_rk, 9001), (2, 2), jnp.float32)
        _g = jnp.sign(_g) * jnp.maximum(jnp.abs(_g), 1.0) + (_g == 0) * 1.0
        g_xattn = _g[0]
        g_ffn = _g[1]
        return (x, ctx_1024, mask_BxS2_bf0, g_xattn, g_ffn)
    x, ctx_1024, mask_BxS2_bf0, g_xattn, g_ffn = _rec_inputs()

    def _L0_xattn_setup():
        import jax, jax.numpy as jnp
        import numpy as np
        B, S, D = (2, 256, 128)
        H = 16
        CHUNK = 32
        NEG_INF = -1000000000.0
        key = jax.random.key(seed)
        ks = jax.random.split(key, 11)
        std = 1.0 / np.sqrt(D)
        return {'query': jax.random.normal(ks[0], (B, S, D), jnp.float32), 'key': jax.random.normal(ks[1], (B, S, D), jnp.float32), 'value': jax.random.normal(ks[2], (B, S, D), jnp.float32), 'Wq': jax.random.normal(ks[3], (D, D), jnp.float32) * std, 'bq': jax.random.normal(ks[4], (D,), jnp.float32) * 0.01, 'Wk': jax.random.normal(ks[5], (D, D), jnp.float32) * std, 'bk': jax.random.normal(ks[6], (D,), jnp.float32) * 0.01, 'Wv': jax.random.normal(ks[7], (D, D), jnp.float32) * std, 'bv': jax.random.normal(ks[8], (D,), jnp.float32) * 0.01, 'Wo': jax.random.normal(ks[9], (D, D), jnp.float32) * std, 'bo': jax.random.normal(ks[10], (D,), jnp.float32) * 0.01}
    _L0_xattn_all = _L0_xattn_setup()
    _L0_xattn_in = {k: v for k, v in _L0_xattn_all.items() if k in ('Wq', 'bq', 'Wk', 'bk', 'Wv', 'bv', 'Wo', 'bo')}
    del _L0_xattn_all

    def _L0_ffn_setup():
        import jax, jax.numpy as jnp
        import numpy as np
        B, S, D, F, E = (4, 256, 128, 512, 8)
        key = jax.random.key(seed)
        ks = jax.random.split(key, 7)
        s1 = 1.0 / np.sqrt(D)
        s2 = 1.0 / np.sqrt(F)
        x = jax.random.normal(ks[0], (B, S, D), dtype=jnp.float32)
        W1 = jax.random.uniform(ks[1], (E, D, F), jnp.float32, -s1, s1)
        b1 = jax.random.uniform(ks[2], (E, F), jnp.float32, -s1, s1)
        W2 = jax.random.uniform(ks[3], (E, F, D), jnp.float32, -s2, s2)
        b2 = jax.random.uniform(ks[4], (E, D), jnp.float32, -s2, s2)
        Wr = jax.random.uniform(ks[5], (D, E), jnp.float32, -s1, s1)
        br = jax.random.uniform(ks[6], (E,), jnp.float32, -s1, s1)
        return {'x': x, 'W1': W1, 'b1': b1, 'W2': W2, 'b2': b2, 'Wr': Wr, 'br': br}
    _L0_ffn_all = _L0_ffn_setup()
    _L0_ffn_in = {k: v for k, v in _L0_ffn_all.items() if k in ('W1', 'b1', 'W2', 'b2', 'Wr', 'br')}
    del _L0_ffn_all

    def _L1_xattn_setup():
        import jax, jax.numpy as jnp
        import numpy as np
        EMBED_DIM = 128
        NUM_HEADS = 16
        HEAD_DIM = EMBED_DIM // NUM_HEADS
        B, T, S = (2, 256, 256)
        key = jax.random.key(seed)
        ks = jax.random.split(key, 12)
        xavier = lambda k: jax.random.uniform(k, (EMBED_DIM, EMBED_DIM), jnp.float32, -np.sqrt(6.0 / (2 * EMBED_DIM)), np.sqrt(6.0 / (2 * EMBED_DIM)))
        return {'query': jax.random.normal(ks[0], (B, T, EMBED_DIM), jnp.float32), 'key': jax.random.normal(ks[1], (B, S, EMBED_DIM), jnp.float32), 'value': jax.random.normal(ks[2], (B, S, EMBED_DIM), jnp.float32), 'key_padding_mask': jnp.zeros((B, S), dtype=bool), 'Wq': xavier(ks[3]), 'bq': jnp.zeros((EMBED_DIM,), jnp.float32), 'Wk': xavier(ks[4]), 'bk': jnp.zeros((EMBED_DIM,), jnp.float32), 'Wv': xavier(ks[5]), 'bv': jnp.zeros((EMBED_DIM,), jnp.float32), 'Wo': xavier(ks[6]), 'bo': jnp.zeros((EMBED_DIM,), jnp.float32)}
    _L1_xattn_all = _L1_xattn_setup()
    _L1_xattn_in = {k: v for k, v in _L1_xattn_all.items() if k in ('Wq', 'bq', 'Wk', 'bk', 'Wv', 'bv', 'Wo', 'bo')}
    del _L1_xattn_all

    def _L1_ffn_setup():
        import jax, jax.numpy as jnp
        import numpy as np
        B, T, C, H, E, MIN_E = (4, 256, 128, 128, 16, 2)
        IS_CAUSAL = False

        def _forward(hidden_states, sim_matrix, gates, q_proj, k_proj, v_proj, o_proj):
            b, t, c = hidden_states.shape
            n = b * t
            x = hidden_states.reshape(n, c)
            xn = x / jnp.maximum(jnp.linalg.norm(x, axis=-1, keepdims=True), 1e-12)
            sn = sim_matrix / jnp.maximum(jnp.linalg.norm(sim_matrix, axis=0, keepdims=True), 1e-12)
            logits = xn @ sn - jax.nn.sigmoid(gates)
            gated = jax.nn.relu(logits)
            hard = (gated > 0).astype(gated.dtype)
            mask = gated + jax.lax.stop_gradient(hard - gated)
            inactive = jnp.sum(hard, axis=1) == 0
            _, fb_idx = jax.lax.top_k(logits, MIN_E)
            fb = jnp.zeros((n, logits.shape[1]), gated.dtype).at[jnp.arange(n)[:, None], fb_idx].set(1.0)
            put = jax.lax.stop_gradient(inactive[:, None].astype(gated.dtype) * fb)
            mask = mask * (1.0 - put) + put
            masked = jnp.where(mask > 0, gated, -jnp.inf)
            w = jax.nn.softmax(masked, axis=-1)

            def moe_proj(p):
                y = jnp.einsum('nc,ech->neh', x, p)
                return jnp.einsum('ne,neh->nh', w, y)
            q = moe_proj(q_proj).reshape(b, t, -1)
            k = moe_proj(k_proj).reshape(b, t, -1)
            v = moe_proj(v_proj).reshape(b, t, -1)
            h = q.shape[-1]
            scores = jnp.einsum('bth,bsh->bts', q, k) / jnp.sqrt(jnp.asarray(h, q.dtype))
            if IS_CAUSAL and t > 1:
                causal = jnp.tril(jnp.ones((t, t), bool))
                scores = jnp.where(causal[None], scores, -jnp.inf)
            attn = jax.nn.softmax(scores, axis=-1)
            o = jnp.einsum('bts,bsh->bth', attn, v).reshape(n, h)
            z = jnp.einsum('ne,nh->enh', w, o)
            out = jnp.einsum('enh,ehc->nc', z, o_proj)
            return out.reshape(b, t, c)
        key = jax.random.key(seed)
        ks = jax.random.split(key, 6)
        lim_qkv = float(np.sqrt(6.0 / (C + H)))
        inp = {'hidden_states': jax.random.normal(ks[0], (B, T, C), jnp.float32), 'sim_matrix': jax.random.normal(ks[1], (C, E), jnp.float32), 'gates': jnp.zeros((E,), jnp.float32), 'q_proj': jax.random.uniform(ks[2], (E, C, H), jnp.float32, -lim_qkv, lim_qkv), 'k_proj': jax.random.uniform(ks[3], (E, C, H), jnp.float32, -lim_qkv, lim_qkv), 'v_proj': jax.random.uniform(ks[4], (E, C, H), jnp.float32, -lim_qkv, lim_qkv), 'o_proj': jax.random.uniform(ks[5], (E, H, C), jnp.float32, -lim_qkv, lim_qkv)}
        return inp
    _L1_ffn_all = _L1_ffn_setup()
    _L1_ffn_in = {k: v for k, v in _L1_ffn_all.items() if k in ('sim_matrix', 'gates', 'q_proj', 'k_proj', 'v_proj', 'o_proj')}
    del _L1_ffn_all
    return {'x': x, 'ctx_1024': ctx_1024, 'mask_BxS2_bf0': mask_BxS2_bf0, 'g_xattn': g_xattn, 'g_ffn': g_ffn, 'L0_xattn_Wq': _L0_xattn_in['Wq'], 'L0_xattn_bq': _L0_xattn_in['bq'], 'L0_xattn_Wk': _L0_xattn_in['Wk'], 'L0_xattn_bk': _L0_xattn_in['bk'], 'L0_xattn_Wv': _L0_xattn_in['Wv'], 'L0_xattn_bv': _L0_xattn_in['bv'], 'L0_xattn_Wo': _L0_xattn_in['Wo'], 'L0_xattn_bo': _L0_xattn_in['bo'], 'L0_ffn_W1': _L0_ffn_in['W1'], 'L0_ffn_b1': _L0_ffn_in['b1'], 'L0_ffn_W2': _L0_ffn_in['W2'], 'L0_ffn_b2': _L0_ffn_in['b2'], 'L0_ffn_Wr': _L0_ffn_in['Wr'], 'L0_ffn_br': _L0_ffn_in['br'], 'L1_xattn_Wq': _L1_xattn_in['Wq'], 'L1_xattn_bq': _L1_xattn_in['bq'], 'L1_xattn_Wk': _L1_xattn_in['Wk'], 'L1_xattn_bk': _L1_xattn_in['bk'], 'L1_xattn_Wv': _L1_xattn_in['Wv'], 'L1_xattn_bv': _L1_xattn_in['bv'], 'L1_xattn_Wo': _L1_xattn_in['Wo'], 'L1_xattn_bo': _L1_xattn_in['bo'], 'L1_ffn_sim_matrix': _L1_ffn_in['sim_matrix'], 'L1_ffn_gates': _L1_ffn_in['gates'], 'L1_ffn_q_proj': _L1_ffn_in['q_proj'], 'L1_ffn_k_proj': _L1_ffn_in['k_proj'], 'L1_ffn_v_proj': _L1_ffn_in['v_proj'], 'L1_ffn_o_proj': _L1_ffn_in['o_proj']}

def reference(x, ctx_1024, mask_BxS2_bf0, g_xattn, g_ffn, L0_xattn_Wq, L0_xattn_bq, L0_xattn_Wk, L0_xattn_bk, L0_xattn_Wv, L0_xattn_bv, L0_xattn_Wo, L0_xattn_bo, L0_ffn_W1, L0_ffn_b1, L0_ffn_W2, L0_ffn_b2, L0_ffn_Wr, L0_ffn_br, L1_xattn_Wq, L1_xattn_bq, L1_xattn_Wk, L1_xattn_bk, L1_xattn_Wv, L1_xattn_bv, L1_xattn_Wo, L1_xattn_bo, L1_ffn_sim_matrix, L1_ffn_gates, L1_ffn_q_proj, L1_ffn_k_proj, L1_ffn_v_proj, L1_ffn_o_proj):
    import jax
    import jax.numpy as jnp

    def _L0_xattn_ref(query, key, value, Wq, bq, Wk, bk, Wv, bv, Wo, bo):
        import jax, jax.numpy as jnp
        import numpy as np
        B, S, D = (2, 256, 128)
        H = 16
        CHUNK = 32
        NEG_INF = -1000000000.0
        b, s, d = query.shape
        hd = d // H
        scale = 1.0 / jnp.sqrt(jnp.asarray(hd, query.dtype))
        q = (query @ Wq + bq).reshape(b, s, H, hd)
        k = (key @ Wk + bk).reshape(b, s, H, hd)
        v = (value @ Wv + bv).reshape(b, s, H, hd)
        scores = jnp.einsum('bqhd,bkhd->bhqk', q, k) * scale
        pos = jnp.arange(s)
        block_end = (pos // CHUNK + 1) * CHUNK
        mask = pos[None, :] < block_end[:, None]
        scores = jnp.where(mask[None, None], scores, NEG_INF)
        attn = jax.nn.softmax(scores, axis=-1)
        out = jnp.einsum('bhqk,bkhd->bqhd', attn, v).reshape(b, s, d)
        return out @ Wo + bo

    def _L0_ffn_ref(x, W1, b1, W2, b2, Wr, br):
        import jax, jax.numpy as jnp
        import numpy as np
        B, S, D, F, E = (4, 256, 128, 512, 8)
        b, s, d = x.shape
        e = Wr.shape[1]
        logits = x @ Wr + br
        idx = jnp.argmax(logits, axis=-1)
        probs = jax.nn.softmax(logits, axis=-1)
        gates = jnp.take_along_axis(probs, idx[..., None], axis=-1)[..., 0]
        xf = x.reshape(-1, d)
        idxf = idx.reshape(-1)
        gf = gates.reshape(-1)
        out = jnp.zeros_like(xf)
        for ei in range(e):
            h = jax.nn.gelu(xf @ W1[ei] + b1[ei], approximate=False)
            y = h @ W2[ei] + b2[ei]
            mask = (idxf == ei).astype(xf.dtype)
            out = out + y * (gf * mask)[:, None]
        return out.reshape(b, s, d)

    def _L1_xattn_ref(query, key, value, key_padding_mask, Wq, bq, Wk, bk, Wv, bv, Wo, bo):
        import jax, jax.numpy as jnp
        import numpy as np
        EMBED_DIM = 128
        NUM_HEADS = 16
        HEAD_DIM = EMBED_DIM // NUM_HEADS
        B, T, S = (2, 256, 256)
        bsz, tgt_len, _ = query.shape
        src_len = key.shape[1]
        q = (query @ Wq.T + bq).reshape(bsz, tgt_len, NUM_HEADS, HEAD_DIM).transpose(0, 2, 1, 3)
        k = (key @ Wk.T + bk).reshape(bsz, src_len, NUM_HEADS, HEAD_DIM).transpose(0, 2, 1, 3)
        v = (value @ Wv.T + bv).reshape(bsz, src_len, NUM_HEADS, HEAD_DIM).transpose(0, 2, 1, 3)
        scale = HEAD_DIM ** (-0.5)
        scores = jnp.einsum('bhtd,bhsd->bhts', q, k) * scale
        causal_mask = jnp.triu(jnp.ones((tgt_len, src_len), dtype=bool), k=1)
        neg_inf = jnp.finfo(scores.dtype).min
        scores = jnp.where(causal_mask[None, None], neg_inf, scores)
        scores = jnp.where(key_padding_mask[:, None, None, :], neg_inf, scores)
        attn = jax.nn.softmax(scores, axis=-1)
        out = jnp.einsum('bhts,bhsd->bhtd', attn, v)
        out = out.transpose(0, 2, 1, 3).reshape(bsz, tgt_len, EMBED_DIM)
        return out @ Wo.T + bo

    def _L1_ffn_ref(hidden_states, sim_matrix, gates, q_proj, k_proj, v_proj, o_proj):
        import jax, jax.numpy as jnp
        import numpy as np
        B, T, C, H, E, MIN_E = (4, 256, 128, 128, 16, 2)
        IS_CAUSAL = False

        def _forward(hidden_states, sim_matrix, gates, q_proj, k_proj, v_proj, o_proj):
            b, t, c = hidden_states.shape
            n = b * t
            x = hidden_states.reshape(n, c)
            xn = x / jnp.maximum(jnp.linalg.norm(x, axis=-1, keepdims=True), 1e-12)
            sn = sim_matrix / jnp.maximum(jnp.linalg.norm(sim_matrix, axis=0, keepdims=True), 1e-12)
            logits = xn @ sn - jax.nn.sigmoid(gates)
            gated = jax.nn.relu(logits)
            hard = (gated > 0).astype(gated.dtype)
            mask = gated + jax.lax.stop_gradient(hard - gated)
            inactive = jnp.sum(hard, axis=1) == 0
            _, fb_idx = jax.lax.top_k(logits, MIN_E)
            fb = jnp.zeros((n, logits.shape[1]), gated.dtype).at[jnp.arange(n)[:, None], fb_idx].set(1.0)
            put = jax.lax.stop_gradient(inactive[:, None].astype(gated.dtype) * fb)
            mask = mask * (1.0 - put) + put
            masked = jnp.where(mask > 0, gated, -jnp.inf)
            w = jax.nn.softmax(masked, axis=-1)

            def moe_proj(p):
                y = jnp.einsum('nc,ech->neh', x, p)
                return jnp.einsum('ne,neh->nh', w, y)
            q = moe_proj(q_proj).reshape(b, t, -1)
            k = moe_proj(k_proj).reshape(b, t, -1)
            v = moe_proj(v_proj).reshape(b, t, -1)
            h = q.shape[-1]
            scores = jnp.einsum('bth,bsh->bts', q, k) / jnp.sqrt(jnp.asarray(h, q.dtype))
            if IS_CAUSAL and t > 1:
                causal = jnp.tril(jnp.ones((t, t), bool))
                scores = jnp.where(causal[None], scores, -jnp.inf)
            attn = jax.nn.softmax(scores, axis=-1)
            o = jnp.einsum('bts,bsh->bth', attn, v).reshape(n, h)
            z = jnp.einsum('ne,nh->enh', w, o)
            out = jnp.einsum('enh,ehc->nc', z, o_proj)
            return out.reshape(b, t, c)
        return _forward(hidden_states, sim_matrix, gates, q_proj, k_proj, v_proj, o_proj)
    x = x + jnp.tanh(g_xattn[0]) * _L0_xattn_ref(_layernorm(x, axis=-1), ctx_1024, ctx_1024, L0_xattn_Wq, L0_xattn_bq, L0_xattn_Wk, L0_xattn_bk, L0_xattn_Wv, L0_xattn_bv, L0_xattn_Wo, L0_xattn_bo)
    x = x + jnp.tanh(g_ffn[0]) * _L0_ffn_ref(_layernorm(x, axis=-1), L0_ffn_W1, L0_ffn_b1, L0_ffn_W2, L0_ffn_b2, L0_ffn_Wr, L0_ffn_br)
    x = x + jnp.tanh(g_xattn[1]) * _L1_xattn_ref(_layernorm(x, axis=-1), ctx_1024, ctx_1024, mask_BxS2_bf0, L1_xattn_Wq, L1_xattn_bq, L1_xattn_Wk, L1_xattn_bk, L1_xattn_Wv, L1_xattn_bv, L1_xattn_Wo, L1_xattn_bo)
    x = x + jnp.tanh(g_ffn[1]) * _L1_ffn_ref(_layernorm(x, axis=-1), L1_ffn_sim_matrix, L1_ffn_gates, L1_ffn_q_proj, L1_ffn_k_proj, L1_ffn_v_proj, L1_ffn_o_proj)
    return x

_drawn_inputs = setup_inputs


def setup_inputs(seed=0):
    import zlib

    import numpy as np

    out = dict(_drawn_inputs(seed))
    spreads = {'g_ffn': (-1.0, 0.6),
     'L1_xattn_bq': (0.0, 0.289),
     'L1_xattn_bk': (0.0, 0.8),
     'L1_xattn_bv': (0.0, 0.1),
     'L1_xattn_bo': (0.0, 0.1),
     'L1_ffn_gates': (0.0, 0.1)}
    factors = {'L0_xattn_bq': 8.0,
     'L0_xattn_bk': 8.0,
     'L0_xattn_bv': 4.445,
     'L0_xattn_bo': 4.457,
     'L0_ffn_b1': 7.295,
     'L0_ffn_b2': 6.247,
     'L0_ffn_br': 4.771}
    for name, (base, spread) in spreads.items():
        noise = np.random.default_rng([zlib.crc32(name.encode()), seed]).standard_normal(out[name].shape)
        drawn = base * np.exp(spread * noise) if base else spread * noise
        out[name] = jnp.asarray(drawn.astype(out[name].dtype))
    for name, factor in factors.items():
        out[name] = (out[name] * factor).astype(out[name].dtype)
    return out
```

```python
from contextlib import ExitStack

import numpy as np
import concourse.bass as bass
from concourse import mybir

ALU = mybir.AluOpType
ACT = mybir.ActivationFunctionType
AX_X = mybir.AxisListType.X
F32 = mybir.dt.float32
BF16 = mybir.dt.bfloat16
I32 = mybir.dt.int32
U32 = mybir.dt.uint32
U8 = mybir.dt.uint8

P = 128
SEQS, LEN, D = 128, 64, 128
N = SEQS * LEN
HEADS, HD = 16, 8
UNIT = 256
UNITS = N // UNIT
QUADS = 4
E0, F0 = 8, 512
E1 = 16
FJ = F0 // P
SLOTS = N // P + E0
REGION = N + (E0 + 2) * P
ROWW = 2 * D + 1
CHUNK = 32
MASKED = -(2.0 ** 126)
EPS = 1e-5
SCALE = float(np.float32(1.0) / np.sqrt(np.float32(HD)))
SCALE_H = float(1.0 / np.sqrt(np.float32(D)))
VW = 17


class Steps:

    def __init__(self, eng, sem, unit, per_unit):
        self.eng, self.sem, self.unit, self.per_unit, self.n = eng, sem, unit, per_unit, 0

    def free(self, ins):
        self.n += 1
        ins.then_inc(self.sem, 1)

    def __call__(self, ins):
        self.free(ins)
        self.eng.wait_ge(self.sem, self.unit * self.per_unit + self.n)

    def end(self):
        assert self.n == self.per_unit, (self.n, self.per_unit)


def bcast(ap, n, at):
    return ap.unsqueeze(at).broadcast_to(list(ap.shape[:at]) + [n] + list(ap.shape[at:]))


def flamingo(nc, a, out):
    ctx = ExitStack()
    with ctx:
        ctx.enter_context(nc.allow_non_contiguous_dma("small constant loads"))

        def sb(name, shape, dt=F32):
            return ctx.enter_context(nc.sbuf_tensor(name, shape, dt))

        def bank(name):
            return ctx.enter_context(nc.psum_tensor(name, [P, 512], F32))

        def sem(name):
            return ctx.enter_context(nc.semaphore(name))

        sorted_in = nc.dram_tensor("sorted_in", (E0 * REGION, ROWW), F32, kind="Internal").ap()
        sorted_out = nc.dram_tensor("sorted_out", (SLOTS * P, D), F32, kind="Internal").ap()

        ident = sb("ident", [P, P])
        identb = sb("identb", [P, P], BF16)
        onesf = sb("onesf", [P, P])
        onesb = sb("onesb", [P, P], BF16)
        earlier = sb("earlier", [P, P], BF16)
        mask_rows = sb("mask_rows", [LEN + 1, 2, LEN], BF16)
        mask_chunk = sb("mask_chunk", [LEN, 8, LEN], BF16)
        mask_causal = [sb(f"mask_causal{b}", [LEN + 1, 8, LEN], BF16) for b in range(2)]
        head_blk = sb("head_blk", [P, HEADS])
        head_of = sb("head_of", [P, 4])
        term_sel = sb("term_sel", [3 * E1, E1, P], BF16)
        iota = sb("iota", [P, 2, E1])
        region0 = sb("region0", [P, E0])
        slot_no = sb("slot_no", [1, SLOTS])
        half_neg = sb("half_neg", [P, 2])
        eps = sb("eps", [P, 2])
        masked = sb("masked", [LEN + 1, UNIT])
        half_pos = sb("half_pos", [P, E1])
        pad_u8 = sb("pad_u8", [LEN + 1, N], U8)
        pad_unit = sb("pad_unit", [LEN + 1, UNIT])
        wraw = sb("wraw", [P, 10, P])
        wq = [sb(f"wq{l}", [P, P]) for l in range(2)]
        wk = [sb(f"wk{l}", [P, P]) for l in range(2)]
        wv = [sb(f"wv{l}", [P, P]) for l in range(2)]
        wo = [sb(f"wo{l}", [P, P]) for l in range(2)]
        wo_swap = [sb(f"wo_swap{l}", [P, P]) for l in range(2)]
        brow = sb("brow", [1, 4, P])
        browp = sb("browp", [1, 4, P])
        bcol = sb("bcol", [P, 4])
        bvcol = sb("bvcol", [P, 2])
        bvb = sb("bvb", [P, 2, P])
        bo_b = sb("bo_b", [P, 2, P])
        gbo = sb("gbo", [P, 2, P])
        graw = sb("graw", [P, 4])
        tg = sb("tg", [P, 4])
        w1 = sb("w1", [P, E0 * F0])
        w2 = sb("w2", [P, E0 * FJ * D])
        b1b = sb("b1b", [P, E0 * F0])
        b2b = sb("b2b", [P, E0 * D])
        wr = sb("wr", [P, E0])
        brb = sb("brb", [P, E0])
        proj = sb("proj", [P, 4, E1, D])
        simm = sb("simm", [P, E1])
        simq = sb("simq", [P, E1])
        simn = sb("simn", [P, E1])
        sgate = sb("sgate", [P, E1])

        xin = [sb(f"xin{b}", [P, 2, D]) for b in range(2)]
        cin = [sb(f"cin{b}", [P, 2, D]) for b in range(2)]
        st6 = sb("st6", [P, 2, 6])
        mv = sb("mv", [P, 2, 2])
        rstd = sb("rstd", [P, 2])
        vare = sb("vare", [P, 2])
        xn = sb("xn", [P, 2, D])
        xb = [sb(f"xb{b}", [P, 2, D]) for b in range(2)]
        xcT = sb("xcT", [P, 4, P])
        qx = sb("qx", [P, 4, 4, LEN])
        kT = sb("kT", [P, UNIT])
        vb = [sb(f"vb{b}", [P, 2, 8, 2, VW]) for b in range(2)]
        mx = sb("mx", [P, QUADS, 8])
        prob = [sb(f"prob{j}", [P, 2, 4, LEN]) for j in range(QUADS)]
        pT = [sb(f"pT{b}", [P, 2, 2, P]) for b in range(2)]
        rden = sb("rden", [P, 4, 4])
        on = sb("on", [P, 4, 8, HD])
        oT = sb("oT", [P, 2, P])
        xr = [sb(f"xr{b}", [P, 2, ROWW + 7]) for b in range(2)]
        st6b = sb("st6b", [P, 2, 6])
        mvb = sb("mvb", [P, 2, 2])
        vareb = sb("vareb", [P, 2])
        rstdb = sb("rstdb", [P, 2])
        x1T = sb("x1T", [P, 2, P])
        lg = sb("lg", [P, 2, E1])
        top = sb("top", [P, 2, 8])
        topi = sb("topi", [P, 2, 8], U32)
        topf = sb("topf", [P, 2, 8])
        onehot = sb("onehot", [P, 2, E0], BF16)
        seen = sb("seen", [P, 2, E0], BF16)
        ex = sb("ex", [P, 2, E1])
        den = sb("den", [P, 2])
        gate = sb("gate", [P, 2])
        rank = sb("rank", [P, 2, E0])
        rsel = sb("rsel", [P, 2, E0])
        posf = sb("posf", [P, 2])
        posi = [sb(f"posi{b}", [P, 2], I32) for b in range(2)]
        place = sb("place", [P, UNITS, 2])
        beyond = sb("beyond", [P, UNITS, 2])
        placed = sb("placed", [P, UNITS, 2])
        move = sb("move", [P, E0 - 1])
        placei = sb("placei", [P, UNITS, 2], I32)
        gidx = [sb(f"gidx{b}", [P, 2], I32) for b in range(2)]
        count = sb("count", [P, E0])
        tiles = sb("tiles", [P, E0])
        tilesi = sb("tilesi", [P, E0], I32)
        tend = sb("tend", [1, E0])
        full = sb("full", [1, SLOTS, E0 - 1])
        fullt = sb("fullt", [1, SLOTS, E0 - 1])
        slotf = sb("slotf", [1, 5, SLOTS])
        slot_e = sb("slot_e", [1, SLOTS], I32)
        slot_row = sb("slot_row", [1, SLOTS], I32)
        padf = sb("padf", [P, 2 * E0])
        padi = sb("padi", [P, 2 * E0 + 2], I32)
        zrow = sb("zrow", [P, ROWW])
        xs = [sb(f"xs{b}", [P, ROWW]) for b in range(2)]
        xsT = [sb(f"xsT{b}", [P, P]) for b in range(2)]
        hb = [sb(f"hb{b}", [P, F0]) for b in range(2)]
        hT = [sb(f"hT{b}", [P, F0]) for b in range(2)]
        yb = [sb(f"yb{b}", [P, D]) for b in range(2)]
        yo = [sb(f"yo{b}", [P, D]) for b in range(2)]
        x3 = sb("x3", [P, 2, D])
        hn = sb("hn", [P, 2, D])
        sq = sb("sq", [P, 2, D])
        ss = sb("ss", [P, 2])
        nrm = sb("nrm", [P, 2])
        hnT = sb("hnT", [P, UNIT])
        gm = sb("gm", [P, 2, E1])
        fb = sb("fb", [P, 2, 2, E1])
        idle = sb("idle", [P, 2])
        gtop = sb("gtop", [P, 2])
        wg = sb("wg", [P, 2, E1])
        wres = sb("wres", [P, 2, E1])
        w3 = sb("w3", [P, 2, 3, E1], BF16)
        w3T = sb("w3T", [3 * E1, UNIT], BF16)
        z = w1[:, :].rearrange("p (e n) -> p e n", e=E1)
        qkT = sb("qkT", [P, 2, UNIT])
        vh = sb("vh", [P, 2, D])
        smx = sb("smx", [P, 2])
        sd = sb("sd", [P, 2, LEN])
        pbd = sb("pbd", [P, 2, 2, LEN])
        srs = sb("srs", [P, 2])
        pbT = sb("pbT", [P, UNIT])
        ohT = sb("ohT", [P, UNIT])
        res = [sb(f"res{b}", [P, 2, D]) for b in range(2)]

        m0 = bank("m0")
        m1 = bank("m1")
        s_bank = [bank(f"s_bank{j}") for j in range(QUADS)]
        tb = bank("tb")
        po = bank("po")
        m0_bf = m0[:, :].bitcast(BF16)

        names = ("vec_ln", "pool_ln", "rstd_ready", "xn_ready", "residual_ready",
                 "xc_in_psum", "xcT_ready", "qk_in_psum", "qk_ready", "v_in_psum", "v_ready", "scores_in_psum",
                 "vec_max", "scores_ready", "exp_ready", "probT_in_psum", "probT_ready", "pv_in_psum",
                 "vec_rden", "heads_ready", "oT_in_psum", "oT_ready", "y_in_psum", "x_mid_ready", "pad_row_ready",
                 "vec_ln2", "var2_ready", "pool_ln2", "rstd2_ready", "xn2_ready", "x1T_in_psum", "x1T_ready",
                 "logits_in_psum", "vec_logits", "logits_ready", "exp8_ready", "onehot_ready", "rank_in_psum",
                 "vec_rank", "pos_ready", "idx_ready", "pool_pad")
        s = [{n: sem(f"{n}_{l}") for n in names} for l in range(2)]
        x_loaded = [[sem(f"x_loaded_{l}_{par}") for par in range(2)] for l in range(2)]
        ctx_loaded = [[sem(f"ctx_loaded_{l}_{par}") for par in range(2)] for l in range(2)]
        slot_loaded = [sem(f"slot_loaded_{par}") for par in range(2)]
        ring_filled = sem("ring_filled")
        ring_used = sem("ring_used")
        fnames = ("norm_ready", "pool_nrm", "nrm_ready", "vec_gate", "wexp_ready", "w3_ready", "w3T_in_psum", "w3T_ready",
                  "qk1_in_psum", "qk1_ready", "v1_in_psum", "v1_ready", "s1_in_psum", "s1_ready", "p1_ready",
                  "vec_p1", "pn_ready", "pT_in_psum", "pT_ready", "o1_in_psum", "o1_ready", "y1_in_psum",
                  "res_ready", "vec_res")
        f = {n: sem(f"f_{n}") for n in fnames}
        load = {n: sem(f"load_{n}") for n in ("attn", "moe", "experts1", "small", "swap")}
        setup = {n: sem(f"setup_{n}") for n in ("pool", "tensor", "scalar", "vector", "consts", "vec_done")}
        routed = {n: sem(f"routed_{n}") for n in ("scattered", "count_in_psum", "vector", "table", "padded", "zero")}
        passed = sem("passed")
        out_sem = sem("out_sem")
        b = {n: sem(f"moe_{n}") for n in ("xT_in_psum", "xT_ready", "h_in_psum", "h_ready", "gelu_ready",
                                          "hT_in_psum", "hT_ready", "y_in_psum", "vec_y", "y_ready", "stored")}

        def apart(eng):
            eng.sem_inc(passed, 1)

        block = ctx.enter_context(nc.Block())

        def units(eng, body):
            body(0, 0, False)
            body(1, 1, False)
            with eng.Fori(1, UNITS // 2 - 1) as i:
                for parity in range(2):
                    body(i * 2 + parity, parity, False)
            body(UNITS - 2, 0, False)
            body(UNITS - 1, 1, True)

        @block.sync
        def _(sp):
            def tokens(ap, u):
                return ap[bass.ds(u * UNIT, UNIT), :].rearrange("(t p) d -> p t d", p=P)

            def load_unit(layer, u, par):
                if layer == 0:
                    sp.dma_start(xin[par][:, :, :], tokens(a["x"], u)).then_inc(x_loaded[0][par], 16)
                sp.dma_start(cin[par][:, :, :], tokens(a["ctx_1024"], u)).then_inc(ctx_loaded[layer][par], 16)

            def attention_loads(layer):
                q = s[layer]

                def body(u, par):
                    sp.wait_ge(q["residual_ready"], u + 1)
                    sp.wait_ge(q["xc_in_psum"], u + 1)
                    load_unit(layer, u + 2, par)

                with sp.Fori(0, (UNITS - 2) // 2) as i:
                    for par in range(2):
                        body(i * 2 + par, par)

            load_unit(0, 0, 0)
            for k, n in enumerate(("L0_xattn_Wq", "L0_xattn_Wk", "L0_xattn_Wv", "L1_xattn_Wq", "L1_xattn_Wk",
                                   "L1_xattn_Wv", "L1_xattn_Wo")):
                sp.dma_start(wraw[:, k, :], a[n]).then_inc(load["attn"], 16)
            sp.dma_start(wraw[:, 7, 0:64], a["L1_xattn_Wo"][:, 64:128]).then_inc(load["attn"], 16)
            sp.dma_start(wraw[:, 7, 64:128], a["L1_xattn_Wo"][:, 0:64]).then_inc(load["attn"], 16)
            sp.dma_start(wo[0][:, :], a["L0_xattn_Wo"]).then_inc(load["attn"], 16)
            sp.dma_start(wo_swap[0][0:64, :], a["L0_xattn_Wo"][64:128, :]).then_inc(load["attn"], 16)
            sp.dma_start(wo_swap[0][64:128, :], a["L0_xattn_Wo"][0:64, :]).then_inc(load["attn"], 16)
            for k, n in enumerate(("L0_xattn_bq", "L0_xattn_bk", "L1_xattn_bq", "L1_xattn_bk")):
                sp.dma_start(brow[0:1, k, :], a[n].unsqueeze(0)).then_inc(load["small"], 16)
            for l in range(2):
                sp.dma_start(bvcol[:, l:l + 1], a[f"L{l}_xattn_bv"].unsqueeze(1)).then_inc(load["small"], 16)
                sp.dma_start(bo_b[:, l, :], a[f"L{l}_xattn_bo"].partition_broadcast(P)).then_inc(load["small"], 16)
            sp.dma_start(graw[:, 0:2], a["g_xattn"].partition_broadcast(P)).then_inc(load["small"], 16)
            sp.dma_start(graw[:, 2:4], a["g_ffn"].partition_broadcast(P)).then_inc(load["small"], 16)
            sp.dma_start(wr[:, :], a["L0_ffn_Wr"]).then_inc(load["small"], 16)
            sp.dma_start(brb[:, :], a["L0_ffn_br"].partition_broadcast(P)).then_inc(load["small"], 16)
            sp.dma_start(simm[:, :], a["L1_ffn_sim_matrix"]).then_inc(load["small"], 16)
            sp.dma_start(sgate[:, :], a["L1_ffn_gates"].partition_broadcast(P)).then_inc(load["small"], 16)
            sp.dma_start(pad_u8[LEN:LEN + 1, :], a["mask_BxS2_bf0"].rearrange("b s -> (b s)").unsqueeze(0))\
                .then_inc(load["small"], 16)
            load_unit(0, 1, 1)
            sp.dma_start(w1[:, :].rearrange("c (e n) -> c e n", e=E0), a["L0_ffn_W1"].rearrange("e c n -> c e n"))\
                .then_inc(load["moe"], 16)
            sp.dma_start(w2[:, :].rearrange("c (e n) -> c e n", n=D),
                         a["L0_ffn_W2"].rearrange("e (j c) n -> c (e j) n", c=P)).then_inc(load["moe"], 16)
            sp.dma_start(b1b[:, :], a["L0_ffn_b1"].rearrange("e n -> (e n)").partition_broadcast(P))\
                .then_inc(load["moe"], 16)
            sp.dma_start(b2b[:, :], a["L0_ffn_b2"].rearrange("e n -> (e n)").partition_broadcast(P))\
                .then_inc(load["moe"], 16)
            for k, n in enumerate("qkvo"):
                sp.dma_start(proj[:, k, :, :], a[f"L1_ffn_{n}_proj"].rearrange("e c n -> c e n"))\
                    .then_inc(load["experts1"], 16)
            attention_loads(0)

            sp.wait_ge(routed["table"], 2)
            sp.wait_ge(routed["padded"], 16 * 2 * (E0 + 1))
            sp.wait_ge(routed["scattered"], 16 * 2 * UNITS)

            def load_slot(sl, par):
                row = sp.value_load(slot_row[0:1, bass.ds(sl, 1)], min_val=0, max_val=E0 * REGION - P)
                sp.dma_start(xs[par][:, :], sorted_in[bass.ds(row, P), :]).then_inc(slot_loaded[par], 16)

            def store_slot(sl, par):
                sp.wait_ge(b["y_ready"], sl + 1)
                sp.dma_start(sorted_out[bass.ds(sl * P, P), :], yo[par][:, :]).then_inc(b["stored"], 16)

            load_slot(0, 0)
            load_slot(1, 1)
            with sp.Fori(0, SLOTS // 2 - 1) as i:
                for par in range(2):
                    store_slot(i * 2 + par, par)
                    load_slot(i * 2 + par + 2, par)
            store_slot(SLOTS - 2, 0)
            store_slot(SLOTS - 1, 1)

            load_unit(1, 0, 0)
            load_unit(1, 1, 1)
            with sp.Fori(0, UNITS // 2 - 1) as i:
                for par in range(2):
                    u = i * 2 + par
                    sp.wait_ge(s[1]["xc_in_psum"], u + 1)
                    load_unit(1, u + 2, par)
                    sp.wait_ge(f["res_ready"], u + 1)
                    sp.dma_start(tokens(out, u), res[par][:, :, :]).then_inc(out_sem, 16)
            for u in range(UNITS - 2, UNITS):
                sp.wait_ge(f["res_ready"], u + 1)
                sp.dma_start(tokens(out, u), res[u % 2][:, :, :]).then_inc(out_sem, 16)
            sp.wait_ge(out_sem, 16 * UNITS)

        @block.gpsimd
        def _(g):
            done = Steps(g, setup["pool"], 0, 0)
            for t, v in ((ident[:, :], 0.0), (identb[:, :], 0.0), (onesf[:, :], 1.0), (onesb[:, :], 1.0),
                         (earlier[:, :], 1.0), (mask_rows[:, :, :], 0.0), (mask_chunk[:, :, :], 0.0),
                         (mask_causal[0][:, :, :], 0.0), (mask_causal[1][:, :, :], 0.0), (head_blk[:, :], 1.0),
                         (term_sel[:, :, :], 0.0), (half_neg[:, :], -0.5), (half_pos[:, :], 0.5),
                         (eps[:, :], EPS), (masked[:, :], MASKED),
                         (zrow[:, :], 0.0), (pbd[:, :, :, :], 0.0), (vb[0][:, :, :, :, :], 0.0),
                         (vb[1][:, :, :, :, :], 0.0), (seen[:, 0, :], 0.0)):
                done(g.memset(t, v))
            for t in (ident, identb):
                done(g.affine_select(out=t[:, :], in_=t[:, :], compare_op=ALU.not_equal, fill=1.0, base=0,
                                     pattern=[[-1, P]], channel_multiplier=1))
            done(g.affine_select(out=earlier[:, :], in_=earlier[:, :], compare_op=ALU.is_gt, fill=0.0, base=0,
                                 pattern=[[1, P]], channel_multiplier=-1))
            done(g.affine_select(out=mask_rows[0:LEN], in_=mask_rows[0:LEN], compare_op=ALU.not_equal, fill=1.0,
                                 base=0, pattern=[[0, 2], [-1, LEN]], channel_multiplier=1))
            done(g.memset(mask_rows[LEN:LEN + 1], 1.0))
            done(g.memset(mask_chunk[0:CHUNK, :, CHUNK:LEN], MASKED))
            for m in mask_causal:
                done(g.affine_select(out=m[0:LEN], in_=m[0:LEN], compare_op=ALU.is_ge, fill=MASKED, base=0,
                                     pattern=[[0, 8], [-1, LEN]], channel_multiplier=1))
            done(g.affine_select(out=head_blk[:, :], in_=head_blk[:, :], compare_op=ALU.is_ge, fill=0.0, base=0,
                                 pattern=[[-HD, HEADS]], channel_multiplier=1))
            done(g.affine_select(out=head_blk[:, :], in_=head_blk[:, :], compare_op=ALU.is_ge, fill=0.0,
                                 base=HD - 1, pattern=[[HD, HEADS]], channel_multiplier=-1))
            for t in range(3):
                done(g.affine_select(out=term_sel[:, :, :], in_=term_sel[:, :, :], compare_op=ALU.not_equal,
                                     fill=1.0, base=-E1 * t, pattern=[[-1, E1], [0, P]], channel_multiplier=1))
            for v in vb:
                done(g.memset(v[0:64, :, :, 0, VW - 1:VW], 1.0))
                done(g.memset(v[64:128, :, :, 1, VW - 1:VW], 1.0))
            done(g.iota(iota[:, :, :], pattern=[[0, 2], [1, E1]], base=0, channel_multiplier=0,
                        allow_small_or_imprecise_dtypes=True))
            done(g.iota(slot_no[:, :], pattern=[[1, SLOTS]], base=0, channel_multiplier=0,
                        allow_small_or_imprecise_dtypes=True))
            done(g.tensor_scalar(region0[:, :], iota[:, 0, 0:E0], float(REGION), None, ALU.mult))
            g.memset(half_neg[:, :], -0.5).then_inc(setup["consts"], 1)
            g.wait_ge(setup["vector"], 1)
            g.tensor_tensor(simn[:, :], simq[:, :], half_pos[:, :], ALU.pow).then_inc(setup["consts"], 1)
            g.wait_ge(setup["vec_done"], 6)

            def front(layer, u, par):
                q = s[layer]
                if layer == 1:
                    step = Steps(g, q["pool_pad"], u, 1)
                    step(g.tensor_copy(pad_unit[LEN:LEN + 1, :], pad_u8[LEN:LEN + 1, bass.ds(u * UNIT, UNIT)]))
                    step.end()
                    g.tensor_tensor(mask_causal[par][LEN:LEN + 1, :, :].rearrange("p (r k) n -> p r (k n)", r=2),
                                    bcast(pad_unit[LEN:LEN + 1, :], 2, 1),
                                    bcast(masked[LEN:LEN + 1, :], 2, 1), ALU.mult).then_inc(q["pad_row_ready"], 1)
                    g.wait_ge(q["pad_row_ready"], u + 1)
                    apart(g)
                    for t in range(2):
                        g.indirect_dma_start(
                            out=xin[par][:, t, :], out_offset=None, in_=sorted_out[:, :],
                            in_offset=bass.IndirectOffsetOnAxis(ap=gidx[par][:, t:t + 1], axis=0),
                            bounds_check=SLOTS * P - 1, oob_is_err=True).then_inc(x_loaded[1][par], 16)
                g.wait_ge(x_loaded[layer][par], (8 + 8 * layer) * (u - par + 2))
                g.tensor_tensor(xb[par][:, :, :], xin[par][:, :, :], bcast(gbo[:, layer, :], 2, 1), ALU.add)\
                    .then_inc(q["residual_ready"], 1)
                g.wait_ge(q["vec_ln"], 4 * u + 4)
                step = Steps(g, q["pool_ln"], u, 1)
                step(g.tensor_tensor(vare[:, :], mv[:, :, 1], eps[:, :], ALU.add))
                step.end()
                g.tensor_tensor(rstd[:, :], vare[:, :], half_neg[:, :], ALU.pow).then_inc(q["rstd_ready"], 1)

            def second_norm(q, u):
                g.wait_ge(q["vec_ln2"], 4 * u + 4)
                step = Steps(g, q["pool_ln2"], u, 1)
                step(g.tensor_tensor(vareb[:, :], mvb[:, :, 1], eps[:, :], ALU.add))
                step.end()
                g.tensor_tensor(rstdb[:, :], vareb[:, :], half_neg[:, :], ALU.pow).then_inc(q["rstd2_ready"], 1)

            def body0(u, par, last):
                if not last:
                    front(0, u + 1, 1 - par)
                second_norm(s[0], u)
                g.wait_ge(s[0]["pos_ready"], u + 1)
                apart(g)
                for t in range(2):
                    g.indirect_dma_start(
                        out=sorted_in[:, :], out_offset=bass.IndirectOffsetOnAxis(ap=posi[par][:, t:t + 1], axis=0),
                        in_=xr[par][:, t, 0:ROWW], in_offset=None,
                        bounds_check=E0 * REGION - 1, oob_is_err=True).then_inc(routed["scattered"], 16)

            front(0, 0, 0)
            units(g, body0)

            g.wait_ge(routed["zero"], 1)
            for k in range(2 * E0 + 2):
                g.indirect_dma_start(
                    out=sorted_in[:, :], out_offset=bass.IndirectOffsetOnAxis(ap=padi[:, k:k + 1], axis=0),
                    in_=zrow[:, :], in_offset=None,
                    bounds_check=E0 * REGION - 1, oob_is_err=True).then_inc(routed["padded"], 16)

            g.wait_ge(routed["table"], 3)
            g.wait_ge(b["stored"], 16 * SLOTS)

            def take_index(u, par):
                g.tensor_copy(gidx[par][:, :], placei[:, bass.ds(u, 1), :].rearrange("p a t -> p (a t)"))\
                    .then_inc(s[1]["idx_ready"], 1)
                g.wait_ge(s[1]["idx_ready"], u + 1)
                apart(g)

            def body1(u, par, last):
                if not last:
                    g.wait_ge(s[1]["xn_ready"], u + 1)
                    take_index(u + 1, 1 - par)
                    front(1, u + 1, 1 - par)
                second_norm(s[1], u)
                g.wait_ge(f["norm_ready"], u + 1)
                g.tensor_tensor(nrm[:, :], ss[:, :], half_pos[:, 0:2], ALU.pow).then_inc(f["pool_nrm"], 1)

            take_index(0, 0)
            front(1, 0, 0)
            units(g, body1)

        @block.scalar
        def _(act):
            act.wait_ge(load["small"], 16 * 15)
            act.activation(tg[:, :], graw[:, :], ACT.Tanh).then_inc(setup["scalar"], 1)
            act.activation(sgate[:, :], sgate[:, :], ACT.Exp, scale=-1.0).then_inc(setup["scalar"], 1)

            def copy_xcT(q, u):
                act.wait_ge(q["xc_in_psum"], u + 1)
                if not (isinstance(u, int) and u == 0):
                    act.wait_ge(q["v_in_psum"], u)
                act.activation(xcT[:, :, :], m0[:, :].rearrange("p (a b) -> p a b", a=4), ACT.Copy)\
                    .then_inc(q["xcT_ready"], 1)

            def copy_v(q, u, par):
                act.wait_ge(q["v_in_psum"], u + 1)
                if not (isinstance(u, int) and u == 0):
                    act.wait_ge(q["pv_in_psum"], 4 * u - 4)
                for half in range(2):
                    rows = slice(64 * half, 64 * half + 64)
                    ins = act.activation(vb[par][rows, :, :, half, 0:16],
                                         m0[rows, 0:256].rearrange("p (t h d) -> p t h d", t=2, h=8), ACT.Copy)
                ins.then_inc(q["v_ready"], 2)

            def exp_quad(q, u, j):
                act.wait_ge(q["scores_ready"], 4 * u + j + 1)
                act.activation(prob[j][:, :, :, :], prob[j][:, :, :, :], ACT.Exp, scale=SCALE)\
                    .then_inc(q["exp_ready"], 1)

            def copy_pT(q, u, j):
                act.wait_ge(q["probT_in_psum"], 4 * u + j + 1)
                act.wait_ge(q["pv_in_psum"], 4 * u + max(j - 1, 0))
                act.activation(pT[j % 2][:, :, :, :], tb[:, :].rearrange("p (r t n) -> p r t n", r=2, t=2),
                               ACT.Copy).then_inc(q["probT_ready"], 1)

            def copy_oT(q, u):
                act.wait_ge(q["oT_in_psum"], u + 1)
                act.wait_ge(q["y_in_psum"], u)
                act.activation(oT[:, :, :], m0[:, 0:256].rearrange("p (t n) -> p t n", t=2), ACT.Copy)\
                    .then_inc(q["oT_ready"], 1)

            def attention(layer, u, par, last):
                q = s[layer]
                copy_pT(q, u, 0)
                copy_pT(q, u, 1)
                if not last:
                    copy_xcT(q, u + 1)
                copy_pT(q, u, 2)
                if not last:
                    copy_v(q, u + 1, 1 - par)
                copy_pT(q, u, 3)
                if not last:
                    exp_quad(q, u + 1, 0)
                copy_oT(q, u)
                if not last:
                    for j in range(1, QUADS):
                        exp_quad(q, u + 1, j)

            def start(layer):
                copy_xcT(s[layer], 0)
                copy_v(s[layer], 0, 0)
                for j in range(QUADS):
                    exp_quad(s[layer], 0, j)

            def body0(u, par, last):
                q = s[0]
                attention(0, u, par, last)
                act.wait_ge(q["x1T_in_psum"], u + 1)
                act.activation(x1T[:, :, :], m0[:, 0:256].rearrange("p (t n) -> p t n", t=2), ACT.Copy)\
                    .then_inc(q["x1T_ready"], 1)
                act.wait_ge(q["logits_ready"], u + 1)
                act.activation(ex[:, :, 0:E0], lg[:, :, 0:E0], ACT.Exp).then_inc(q["exp8_ready"], 1)

            start(0)
            units(act, body0)

            def copy_xsT(sl, par):
                act.wait_ge(b["xT_in_psum"], sl + 1)
                act.activation(xsT[par][:, :], m0[:, 0:P], ACT.Copy).then_inc(b["xT_ready"], 1)

            def gelu(sl, par):
                act.wait_ge(b["h_ready"], sl + 1)
                act.activation(hb[par][:, :], hb[par][:, :], ACT.Gelu).then_inc(b["gelu_ready"], 1)

            def copy_hT(sl, par):
                act.wait_ge(b["hT_in_psum"], sl + 1)
                act.activation(hT[par][:, :], tb[:, :], ACT.Copy).then_inc(b["hT_ready"], 1)

            def slot(sl, par, last):
                if not last:
                    copy_xsT(sl + 1, 1 - par)
                copy_hT(sl, par)
                if not last:
                    gelu(sl + 1, 1 - par)

            copy_xsT(0, 0)
            gelu(0, 0)
            slot(0, 0, False)
            slot(1, 1, False)
            with act.Fori(1, SLOTS // 2 - 1) as i:
                for par in range(2):
                    slot(i * 2 + par, par, False)
            slot(SLOTS - 2, 0, False)
            slot(SLOTS - 1, 1, True)

            def body1(u, par, last):
                q = s[1]
                attention(1, u, par, last)
                act.wait_ge(q["x1T_in_psum"], u + 1)
                act.activation(hnT[:, :], m0[:, 0:256], ACT.Copy).then_inc(q["x1T_ready"], 1)
                act.wait_ge(q["logits_ready"], u + 1)
                act.activation(ex[:, :, :], lg[:, :, :], ACT.Exp).then_inc(f["wexp_ready"], 1)
                act.wait_ge(f["w3T_in_psum"], u + 1)
                act.activation(w3T[:, :], m0_bf[0:3 * E1, 0:256], ACT.Copy).then_inc(f["w3T_ready"], 1)
                act.wait_ge(f["v1_in_psum"], u + 1)
                act.activation(vh[:, :, :], m0[:, 0:256].rearrange("p (t n) -> p t n", t=2), ACT.Copy)\
                    .then_inc(f["v1_ready"], 1)
                act.wait_ge(f["s1_ready"], u + 1)
                for half in range(2):
                    rows = slice(64 * half, 64 * half + 64)
                    ins = act.activation(pbd[rows, :, half, :], sd[rows, :, :], ACT.Exp, scale=SCALE_H)
                ins.then_inc(f["p1_ready"], 2)
                act.wait_ge(f["pT_in_psum"], u + 1)
                act.activation(pbT[:, :], tb[:, 0:256], ACT.Copy).then_inc(f["pT_ready"], 1)
                act.wait_ge(f["o1_in_psum"], u + 1)
                act.activation(ohT[:, :], m0[:, 0:256], ACT.Copy).then_inc(f["o1_ready"], 1)

            start(1)
            units(act, body1)

        @block.vector
        def _(v):
            def by_pair(ap):
                return ap.rearrange("c (h p d) -> c p h d", h=2, p=8)

            def to_pairs(dst):
                return dst.rearrange("c (p h d) -> c p h d", p=8, h=2)

            v.wait_ge(setup["consts"], 1)
            v.wait_ge(load["attn"], 16 * 12)
            v.wait_ge(load["small"], 16 * 15)
            v.tensor_reduce(head_of[:, :], head_blk[:, :].rearrange("p (j r) -> p r j", r=4), AX_X, ALU.add)
            for k, w in enumerate((wq[0], wk[0], wv[0])):
                v.tensor_copy(to_pairs(w[:, :]), by_pair(wraw[:, k, :]))
            for k in range(4):
                v.tensor_copy(browp[0:1, k, :].rearrange("c (p h d) -> c p h d", p=8, h=2),
                              brow[0:1, k, :].rearrange("c (h p d) -> c p h d", h=2, p=8))
            for l in range(2):
                v.tensor_scalar(bvb[:, l, :], onesf[:, :], bvcol[:, l:l + 1], None, ALU.mult)
            v.tensor_tensor(simq[:, :], simm[:, :], simm[:, :], ALU.mult).then_inc(setup["vec_done"], 1)
            v.wait_ge(setup["tensor"], 1)
            for k, w in enumerate((wq[1], wk[1], wv[1])):
                v.tensor_copy(to_pairs(w[:, :]), by_pair(s_bank[k][:, 0:P]))
            v.tensor_copy(wo[1][:, :], s_bank[3][:, 0:P])
            v.tensor_copy(wo_swap[1][:, :], po[:, 0:P]).then_inc(setup["vec_done"], 1)
            v.wait_ge(setup["tensor"], 2)
            v.tensor_copy(simq[:, :], m1[:, 256:256 + E1]).then_inc(setup["vector"], 1)
            v.wait_ge(setup["scalar"], 2)
            step = Steps(v, setup["vec_done"], 0, 0)
            step.n = 2
            step(v.tensor_copy(bcol[:, :], m1[:, 300:304]))
            step(v.tensor_tensor(bo_b[:, :, :], m1[:, 0:256].rearrange("p (l n) -> p l n", l=2), bo_b[:, :, :], ALU.add))
            for l in range(2):
                step(v.tensor_scalar(gbo[:, l, :], bo_b[:, l, :], tg[:, l:l + 1], None, ALU.mult))
            step(v.tensor_scalar(sgate[:, :], sgate[:, :], 1.0, None, ALU.add))
            step(v.reciprocal(sgate[:, :], sgate[:, :]))
            v.wait_ge(setup["consts"], 2)
            step(v.tensor_scalar(simn[:, :], simn[:, :], 1e-12, None, ALU.max))
            step(v.reciprocal(simn[:, :], simn[:, :]))
            step(v.tensor_tensor(simn[:, :], simm[:, :], simn[:, :], ALU.mult))

            def stats(sm, u, x, six, two):
                step = Steps(v, sm, u, 4)
                step.free(v.bn_stats(six[:, 0, :], x[:, 0, 0:D]))
                step(v.bn_stats(six[:, 1, :], x[:, 1, 0:D]))
                apart(v)
                for t in range(2):
                    step.free(v.bn_aggr(two[:, t, :], six[:, t, :]))
                step.end()

            def norm(layer, u, par):
                q = s[layer]
                v.wait_ge(x_loaded[layer][par], (8 + 8 * layer) * (u - par + 2))
                stats(q["vec_ln"], u, xin[par], st6, mv)
                v.wait_ge(q["rstd_ready"], u + 1)
                if not (isinstance(u, int) and u == 0):
                    v.wait_ge(q["xc_in_psum"], u)
                for t in range(2):
                    ins = v.tensor_scalar(xn[:, t, :], xin[par][:, t, :], mv[:, t, 0:1], rstd[:, t:t + 1],
                                          ALU.subtract, ALU.mult)
                ins.then_inc(q["xn_ready"], 1)

            def copy_qk(layer, u):
                q = s[layer]
                v.wait_ge(q["qk_in_psum"], u + 1)
                if not (isinstance(u, int) and u == 0):
                    v.wait_ge(q["scores_in_psum"], 4 * u)
                v.tensor_scalar(kT[:, :], m1[:, 256:512], bcol[:, 2 * layer + 1:2 * layer + 2], None, ALU.add)
                for r in range(4):
                    ins = v.tensor_scalar(qx[:, :, r, :], m1[:, 0:256].rearrange("p (s k) -> p s k", s=4),
                                          bcol[:, 2 * layer:2 * layer + 1], head_of[:, r:r + 1], ALU.add, ALU.mult)
                ins.then_inc(q["qk_ready"], 1)

            def shift_quad(q, u, j):
                v.wait_ge(q["scores_in_psum"], 4 * u + j + 1)
                step = Steps(v, q["vec_max"], u * QUADS + j, 1)
                sc = s_bank[j][:, :].rearrange("p (a k) -> p a k", k=LEN)
                step(v.tensor_reduce(mx[:, j, :], sc, AX_X, ALU.max))
                if not (isinstance(u, int) and u == 0):
                    v.wait_ge(q["probT_in_psum"], 4 * u - 3 + j)
                v.scalar_tensor_tensor(out=prob[j][:, :, :, :].rearrange("p r t k -> p (r t) k"), in0=sc,
                                       scalar=MASKED, in1=bcast(mx[:, j, :], LEN, 2),
                                       op0=ALU.max, op1=ALU.subtract).then_inc(q["scores_ready"], 1)

            def normalise(q, u, half):
                v.wait_ge(q["pv_in_psum"], 4 * u + 2 * half + 2)
                step = Steps(v, q["vec_rden"], u * 2 + half, 1)
                o = po[:, 0:4 * 4 * VW].rearrange("p (a t c) -> p a t c", a=4, t=4)
                step(v.reciprocal(rden[:, :, :], o[:, :, :, VW - 1]))
                if half == 0:
                    v.wait_ge(q["oT_in_psum"], u)
                for h in range(2):
                    rows = slice(64 * h, 64 * h + 64)
                    ins = v.tensor_tensor(
                        on[rows, :, 4 * half:4 * half + 4, :].rearrange("p t a d -> p a t d"),
                        o[rows, :, :, HD * h:HD * h + HD], bcast(rden[rows, :, :], HD, 3), ALU.mult)
                ins.then_inc(q["heads_ready"], 1)

            def add_residual(layer, u, par, dst):
                q = s[layer]
                v.wait_ge(q["y_in_psum"], u + 1)
                v.scalar_tensor_tensor(out=dst, in0=m1[:, 0:256].rearrange("p (t n) -> p t n", t=2),
                                       scalar=tg[:, layer:layer + 1], in1=xb[par][:, :, :],
                                       op0=ALU.mult, op1=ALU.add).then_inc(q["x_mid_ready"], 1)

            def attention(layer, u, par, last, dst):
                q = s[layer]
                if not last:
                    norm(layer, u + 1, 1 - par)
                    copy_qk(layer, u + 1)
                normalise(q, u, 0)
                if not last:
                    shift_quad(q, u + 1, 0)
                normalise(q, u, 1)
                if not last:
                    shift_quad(q, u + 1, 1)
                    shift_quad(q, u + 1, 2)
                if layer == 0:
                    v.wait_ge(routed["scattered"], 32 * u)
                add_residual(layer, u, par, dst)
                if not last:
                    shift_quad(q, u + 1, 3)

            def start(layer):
                norm(layer, 0, 0)
                copy_qk(layer, 0)
                for j in range(QUADS):
                    shift_quad(s[layer], 0, j)

            def body0(u, par, last):
                q = s[0]
                attention(0, u, par, last, xr[par][:, :, 0:D])
                v.wait_ge(q["x_mid_ready"], u + 1)
                stats(q["vec_ln2"], u, xr[par], st6b, mvb)
                v.wait_ge(q["rstd2_ready"], u + 1)
                for t in range(2):
                    ins = v.tensor_scalar(xr[par][:, t, D:2 * D], xr[par][:, t, 0:D], mvb[:, t, 0:1],
                                          rstdb[:, t:t + 1], ALU.subtract, ALU.mult)
                ins.then_inc(q["xn2_ready"], 1)
                v.wait_ge(q["logits_in_psum"], u + 1)
                step = Steps(v, q["vec_logits"], u, 7)
                step(v.tensor_tensor(lg[:, :, 0:E0], m1[:, 0:2 * E0].rearrange("p (t e) -> p t e", t=2),
                                     bcast(brb[:, :], 2, 1), ALU.add))
                apart(v)
                step.free(v.max(top[:, 0, :], lg[:, 0, 0:E0]))
                step(v.max(top[:, 1, :], lg[:, 1, 0:E0]))
                apart(v)
                step.free(v.max_index(topi[:, 0, :], top[:, 0, :], lg[:, 0, 0:E0]))
                step(v.max_index(topi[:, 1, :], top[:, 1, :], lg[:, 1, 0:E0]))
                step(v.tensor_copy(topf[:, :, :], topi[:, :, :]))
                step(v.tensor_tensor(onehot[:, :, :], iota[:, :, 0:E0], topf[:, :, 0:1].broadcast_to([P, 2, E0]),
                                     ALU.is_equal))
                step.end()
                step = Steps(v, q["onehot_ready"], u, 1)
                step(v.tensor_tensor(seen[:, 1, :], seen[:, 0, :], onehot[:, 0, :], ALU.add))
                step.end()
                v.tensor_tensor(lg[:, :, 0:E0], lg[:, :, 0:E0], top[:, :, 0:1].broadcast_to([P, 2, E0]),
                                ALU.subtract).then_inc(q["logits_ready"], 1)
                v.wait_ge(q["rank_in_psum"], u + 1)
                step = Steps(v, q["vec_rank"], u, 7)
                step(v.tensor_tensor(seen[:, 0, :], seen[:, 1, :], onehot[:, 1, :], ALU.add))
                step(v.tensor_tensor(rank[:, :, :], m1[:, 0:2 * E0].rearrange("p (t e) -> p t e", t=2),
                                     bcast(region0[:, :], 2, 1), ALU.add))
                step(v.tensor_tensor(rsel[:, :, :], rank[:, :, :], onehot[:, :, :], ALU.mult))
                step(v.tensor_reduce(posf[:, :], rsel[:, :, :], AX_X, ALU.add))
                step(v.tensor_copy(place[:, bass.ds(u, 1), :], posf[:, :].unsqueeze(1)))
                v.wait_ge(q["exp8_ready"], u + 1)
                step(v.tensor_reduce(den[:, :], ex[:, :, 0:E0], AX_X, ALU.add))
                step(v.reciprocal(gate[:, :], den[:, :]))
                step.end()
                v.tensor_scalar(xr[par][:, :, 2 * D], gate[:, :], tg[:, 2:3], None, ALU.mult)
                v.tensor_copy(posi[par][:, :], posf[:, :]).then_inc(q["pos_ready"], 1)

            start(0)
            units(v, body0)

            v.wait_ge(routed["count_in_psum"], 1)
            step = Steps(v, routed["vector"], 0, 0)
            step(v.tensor_copy(count[:, :], m1[:, 0:E0]))
            step(v.tensor_tensor(padf[:, 0:E0], count[:, :], region0[:, :], ALU.add))
            step(v.tensor_scalar(padf[:, 0:E0], padf[:, 0:E0], m1[:, 64:65], None, ALU.add))
            step(v.tensor_copy(padi[:, 0:E0], padf[:, 0:E0]))
            for k in range(E0 + 2):
                step(v.tensor_scalar(padi[:, E0 + k:E0 + k + 1], padf[:, E0 - 1:E0], float(P * (k + 1)), None, ALU.add))
            v.tensor_copy(padi[:, 0:E0], padf[:, 0:E0]).then_inc(routed["zero"], 1)
            step(v.tensor_scalar(tilesi[:, :], count[:, :], P / 2 - 0.5, 1.0 / P, ALU.add, ALU.mult))
            step(v.tensor_copy(tiles[:, :], tilesi[:, :]))
            step(v.tensor_copy(tend[:, 0:1], tiles[0:1, 0:1]))
            for e in range(1, E0):
                step(v.tensor_tensor(tend[:, e:e + 1], tend[:, e - 1:e], tiles[0:1, e:e + 1], ALU.add))
            step(v.tensor_tensor(full[:, :, :], bcast(tend[:, 0:E0 - 1], SLOTS, 1), bcast(slot_no[:, :], E0 - 1, 2),
                                 ALU.is_le))
            step(v.tensor_reduce(slotf[:, 0, :], full[:, :, :], AX_X, ALU.add))
            step(v.tensor_tensor(fullt[:, :, :], full[:, :, :], bcast(tend[:, 0:E0 - 1], SLOTS, 1), ALU.mult))
            step(v.tensor_reduce(slotf[:, 1, :], fullt[:, :, :], AX_X, ALU.max))
            step(v.tensor_tensor(slotf[:, 2, :], slot_no[:, :], slotf[:, 1, :], ALU.subtract))
            step(v.tensor_scalar(slotf[:, 3, :], slotf[:, 2, :], float(P), None, ALU.mult))
            step(v.scalar_tensor_tensor(out=slotf[:, 4, :], in0=slotf[:, 0, :], scalar=float(REGION),
                                        in1=slotf[:, 3, :], op0=ALU.mult, op1=ALU.add))
            v.tensor_copy(slot_e[:, :], slotf[:, 0, :]).then_inc(routed["table"], 1)
            v.tensor_copy(slot_row[:, :], slotf[:, 4, :]).then_inc(routed["table"], 1)
            v.wait_ge(routed["table"], 2)
            step(v.tensor_scalar(move[:, :], tiles[:, 0:E0 - 1], float(P), -float(REGION), ALU.mult, ALU.add))
            src = place
            for e in range(1, E0):
                step(v.tensor_scalar(beyond[:, :, :], place[:, :, :], float(e * REGION), move[:, e - 1:e],
                                     ALU.is_ge, ALU.mult))
                step(v.tensor_tensor(placed[:, :, :], src[:, :, :], beyond[:, :, :], ALU.add))
                src = placed
            v.tensor_copy(placei[:, :, :], placed[:, :, :]).then_inc(routed["table"], 1)
            v.wait_ge(load["moe"], 16 * 4)

            def expert_of(sl):
                return v.value_load(slot_e[0:1, bass.ds(sl, 1)], min_val=0, max_val=E0 - 1)

            def add_b1(sl, par, first=False):
                e = expert_of(sl)
                v.wait_ge(b["h_in_psum"], sl + 1)
                if not first:
                    v.wait_ge(b["hT_in_psum"], sl - 1)
                v.tensor_tensor(hb[par][:, :], s_bank[par][:, :], b1b[:, bass.ds(e * F0, F0)], ALU.add)\
                    .then_inc(b["h_ready"], 1)

            def finish_slot(sl, par):
                e = expert_of(sl)
                v.wait_ge(b["y_in_psum"], sl + 1)
                step = Steps(v, b["vec_y"], sl, 1)
                step(v.tensor_tensor(yb[par][:, :], po[:, 0:D], b2b[:, bass.ds(e * D, D)], ALU.add))
                v.wait_ge(b["stored"], 16 * sl)
                v.scalar_tensor_tensor(out=yo[par][:, :], in0=yb[par][:, :], scalar=xs[par][:, 2 * D:2 * D + 1],
                                       in1=xs[par][:, 0:D], op0=ALU.mult, op1=ALU.add).then_inc(b["y_ready"], 1)

            add_b1(0, 0, True)

            def slot(sl, par, last):
                if not last:
                    add_b1(sl + 1, 1 - par)
                finish_slot(sl, par)

            slot(0, 0, False)
            slot(1, 1, False)
            with v.Fori(1, SLOTS // 2 - 1) as i:
                for par in range(2):
                    slot(i * 2 + par, par, False)
            slot(SLOTS - 2, 0, False)
            slot(SLOTS - 1, 1, True)

            def body1(u, par, last):
                q = s[1]
                attention(1, u, par, last, x3[:, :, :])
                v.wait_ge(q["x_mid_ready"], u + 1)
                stats(q["vec_ln2"], u, x3, st6b, mvb)
                v.wait_ge(q["rstd2_ready"], u + 1)
                for t in range(2):
                    ins = v.tensor_scalar(hn[:, t, :], x3[:, t, :], mvb[:, t, 0:1], rstdb[:, t:t + 1],
                                          ALU.subtract, ALU.mult)
                    ins.then_inc(q["xn2_ready"], 1)
                v.wait_ge(q["xn2_ready"], 2 * u + 2)
                step = Steps(v, f["vec_gate"], u, 25)
                step(v.tensor_tensor(sq[:, :, :], hn[:, :, :], hn[:, :, :], ALU.mult))
                v.tensor_reduce(ss[:, :], sq[:, :, :], AX_X, ALU.add).then_inc(f["norm_ready"], 1)
                v.wait_ge(f["pool_nrm"], u + 1)
                step(v.tensor_scalar(nrm[:, :], nrm[:, :], 1e-12, None, ALU.max))
                step(v.reciprocal(nrm[:, :], nrm[:, :]))
                v.wait_ge(q["logits_in_psum"], u + 1)
                for t in range(2):
                    step.free(v.scalar_tensor_tensor(out=lg[:, t, :], in0=m1[:, E1 * t:E1 * t + E1],
                                                     scalar=nrm[:, t:t + 1], in1=sgate[:, :],
                                                     op0=ALU.mult, op1=ALU.subtract))
                v.wait_ge(f["vec_gate"], 25 * u + step.n)
                apart(v)
                step.free(v.max(top[:, 0, :], lg[:, 0, :]))
                step(v.max(top[:, 1, :], lg[:, 1, :]))
                apart(v)
                step.free(v.max_index(topi[:, 0, :], top[:, 0, :], lg[:, 0, :]))
                step(v.max_index(topi[:, 1, :], top[:, 1, :], lg[:, 1, :]))
                step(v.tensor_copy(topf[:, :, :], topi[:, :, :]))
                for k in range(2):
                    step(v.tensor_tensor(fb[:, k, :, :], iota[:, :, :], topf[:, :, k:k + 1].broadcast_to([P, 2, E1]),
                                         ALU.is_equal))
                step(v.tensor_tensor(fb[:, 0, :, :], fb[:, 0, :, :], fb[:, 1, :, :], ALU.add))
                step(v.tensor_scalar(idle[:, :], top[:, :, 0], 0.0, None, ALU.is_le))
                step(v.tensor_scalar(gtop[:, :], top[:, :, 0], 0.0, None, ALU.max))
                step(v.tensor_tensor(fb[:, 0, :, :], fb[:, 0, :, :], bcast(idle[:, :], E1, 2), ALU.mult))
                step(v.tensor_scalar(gm[:, :, :], lg[:, :, :], 0.0, None, ALU.is_gt))
                step(v.tensor_tensor(gm[:, :, :], gm[:, :, :], fb[:, 0, :, :], ALU.add))
                v.scalar_tensor_tensor(out=lg[:, :, :], in0=lg[:, :, :], scalar=0.0, in1=bcast(gtop[:, :], E1, 2),
                                       op0=ALU.max, op1=ALU.subtract).then_inc(q["logits_ready"], 1)
                v.wait_ge(f["wexp_ready"], u + 1)
                step(v.tensor_tensor(wg[:, :, :], ex[:, :, :], gm[:, :, :], ALU.mult))
                step(v.tensor_reduce(den[:, :], wg[:, :, :], AX_X, ALU.add))
                step(v.reciprocal(gate[:, :], den[:, :]))
                step(v.tensor_tensor(wg[:, :, :], wg[:, :, :], bcast(gate[:, :], E1, 2), ALU.mult))
                step(v.tensor_copy(w3[:, :, 0, :], wg[:, :, :]))
                step(v.tensor_tensor(wres[:, :, :], wg[:, :, :], w3[:, :, 0, :], ALU.subtract))
                step(v.tensor_copy(w3[:, :, 1, :], wres[:, :, :]))
                step.end()
                v.tensor_tensor(w3[:, :, 2, :], wres[:, :, :], w3[:, :, 1, :], ALU.subtract)\
                    .then_inc(f["w3_ready"], 1)

                def weigh(src, done, base):
                    v.wait_ge(done, u + 1)
                    for k in range(E1 // 2):
                        v.wait_ge(ring_filled, u * E1 + base + k + 1)
                        v.tensor_tensor(z[:, 2 * k:2 * k + 2, :],
                                        s_bank[k % QUADS][:, :].rearrange("p (e n) -> p e n", e=2),
                                        bcast(src, 2, 1), ALU.mult).then_inc(ring_used, 1)

                v.wait_ge(f["y1_in_psum"], u)
                weigh(hnT[:, :], q["x1T_ready"], 0)
                v.wait_ge(f["qk1_in_psum"], u + 1)
                v.tensor_copy(qkT[:, :, :], m1[:, :].rearrange("p (a n) -> p a n", a=2)).then_inc(f["qk1_ready"], 1)
                v.wait_ge(f["s1_in_psum"], u + 1)
                step = Steps(v, f["vec_p1"], u, 3)
                sc = po[:, 0:2 * LEN].rearrange("p (t k) -> p t k", t=2)
                step(v.tensor_reduce(smx[:, :], sc, AX_X, ALU.max))
                v.tensor_tensor(sd[:, :, :], sc, bcast(smx[:, :], LEN, 2), ALU.subtract).then_inc(f["s1_ready"], 1)
                v.wait_ge(f["p1_ready"], 2 * u + 2)
                pb = pbd[:, :, :, :].rearrange("p t h k -> p t (h k)")
                step(v.tensor_reduce(srs[:, :], pb, AX_X, ALU.add))
                step(v.reciprocal(srs[:, :], srs[:, :]))
                step.end()
                v.tensor_tensor(pb, pb, bcast(srs[:, :], P, 2), ALU.mult).then_inc(f["pn_ready"], 1)
                v.wait_ge(f["v1_in_psum"], u + 1)
                weigh(ohT[:, :], f["o1_ready"], E1 // 2)
                v.wait_ge(f["y1_in_psum"], u + 1)
                v.wait_ge(out_sem, 16 * u)
                v.scalar_tensor_tensor(out=res[par][:, :, :], in0=m1[:, 0:256].rearrange("p (t n) -> p t n", t=2),
                                       scalar=tg[:, 3:4], in1=x3[:, :, :],
                                       op0=ALU.mult, op1=ALU.add).then_inc(f["res_ready"], 1)

            start(1)
            units(v, body1)

        @block.tensor
        def _(pe):
            pe.wait_ge(setup["consts"], 1)
            pe.wait_ge(load["attn"], 16 * 12)
            pe.wait_ge(load["small"], 16 * 15)
            for k in range(4):
                pe.transpose(s_bank[k][:, 0:P], wraw[:, 3 + k, :], ident[:, :])
            pe.transpose(po[:, 0:P], wraw[:, 7, :], ident[:, :]).then_inc(setup["tensor"], 1)
            pe.wait_ge(setup["vec_done"], 2)
            for l in range(2):
                pe.matmul(m1[:, P * l:P * l + P], bvb[:, l, :], wo[l][:, :], start=True, stop=True)
            for k in range(4):
                pe.matmul(m1[:, 300 + k:301 + k], browp[0:1, k, :], onesf[0:1, 0:1], start=True, stop=True)
            pe.matmul(m1[:, 256:256 + E1], onesf[:, :], simq[:, :], start=True, stop=True)\
                .then_inc(setup["tensor"], 1)
            pe.wait_ge(setup["vec_done"], 4)

            def transpose_in(layer, u, par):
                q = s[layer]
                if not (isinstance(u, int) and u == 0):
                    pe.wait_ge(q["v_ready"], 2 * u)
                    pe.wait_ge(q["x1T_ready"], u - 1)
                pe.wait_ge(q["xn_ready"], u + 1)
                pe.wait_ge(ctx_loaded[layer][par], 8 * (u - par + 2))
                for t in range(2):
                    pe.transpose(m0[:, P * t:P * t + P], xn[:, t, :], ident[:, :])
                for t in range(2):
                    ins = pe.transpose(m0[:, P * (2 + t):P * (3 + t)], cin[par][:, t, :], ident[:, :])
                ins.then_inc(q["xc_in_psum"], 1)

            def queries_keys(layer, u):
                q = s[layer]
                pe.wait_ge(q["xcT_ready"], u + 1)
                if not (isinstance(u, int) and u == 0):
                    pe.wait_ge((q["pos_ready"] if layer == 0 else f["res_ready"]), u - 1)
                pe.matmul(m1[:, 0:256], wq[layer][:, :], xcT[:, 0:2, :], start=True, stop=True)
                pe.matmul(m1[:, 256:512], wk[layer][:, :], xcT[:, 2:4, :], start=True, stop=True)\
                    .then_inc(q["qk_in_psum"], 1)

            def values(layer, u):
                q = s[layer]
                for t in range(2):
                    ins = pe.matmul(m0[:, P * t:P * t + P], xcT[:, 2 + t, :], wv[layer][:, :], start=True, stop=True)
                ins.then_inc(q["v_in_psum"], 1)

            def scores(layer, u, par, j):
                q = s[layer]
                if j == 0:
                    pe.wait_ge(q["qk_ready"], u + 1)
                    if layer == 1:
                        pe.wait_ge(q["pad_row_ready"], u + 1)
                        if not (isinstance(u, int) and u == 0):
                            pe.wait_ge(ring_used, u * E1 - E1)
                if not (isinstance(u, int) and u == 0):
                    pe.wait_ge(q["scores_ready"], 4 * u - 3 + j)
                if layer == 0:
                    mask, rows = mask_chunk, LEN
                else:
                    mask, rows = mask_causal[par], LEN + 1
                pe.matmul(s_bank[j][:, :], mask_rows[0:rows, :, :], mask[0:rows, :, :], start=True, stop=False,
                          skip_group_check=True)
                quad = slice(32 * j, 32 * j + 32)
                for r in range(2):
                    for t in range(4):
                        seq = slice(LEN * t, LEN * t + LEN)
                        col = LEN * (4 * r + t)
                        ins = pe.matmul(s_bank[j][:, col:col + LEN], qx[quad, t, 2 * r:2 * r + 2, :], kT[quad, seq],
                                        start=False, stop=True, skip_group_check=True)
                ins.then_inc(q["scores_in_psum"], 1)

            def transpose_probs(q, u, j):
                pe.wait_ge(q["exp_ready"], 4 * u + j + 1)
                pe.wait_ge(q["probT_ready"], 4 * u + j)
                for r in range(2):
                    for t in range(2):
                        col = P * (2 * r + t)
                        ins = pe.transpose(tb[:, col:col + P], prob[j][:, r, 2 * t:2 * t + 2, :], ident[:, :])
                ins.then_inc(q["probT_in_psum"], 1)

            def weigh_values(q, u, par, j):
                pe.wait_ge(q["probT_ready"], 4 * u + j + 1)
                if j == 0:
                    pe.wait_ge(q["v_ready"], 2 * u + 2)
                if j % 2 == 0:
                    pe.wait_ge(q["heads_ready"], 2 * u + j // 2)
                for r in range(2):
                    for t in range(2):
                        col = 2 * VW * (2 * (2 * (j % 2) + r) + t)
                        ins = pe.matmul(po[:, col:col + 2 * VW], pT[j % 2][:, r, t, :], vb[par][:, t, 2 * j + r, :, :],
                                        start=True, stop=True, skip_group_check=True)
                ins.then_inc(q["pv_in_psum"], 1)

            def transpose_heads(q, u, last):
                pe.wait_ge(q["heads_ready"], 2 * u + 2)
                pe.wait_ge(q["v_ready"], 2 * u + (2 if last else 4))
                for t in range(2):
                    ins = pe.transpose(m0[:, P * t:P * t + P], on[:, 2 * t:2 * t + 2, :, :], ident[:, :])
                ins.then_inc(q["oT_in_psum"], 1)

            def output(layer, u, last):
                q = s[layer]
                pe.wait_ge(q["oT_ready"], u + 1)
                pe.wait_ge(q["qk_ready"], u + (1 if last else 2))
                apart(pe)
                for half in range(2):
                    rows = slice(64 * half, 64 * half + 64)
                    for t in range(2):
                        for h in range(2):
                            w = wo[layer] if h == half else wo_swap[layer]
                            ins = pe.matmul(m1[rows, P * t:P * t + P], oT[rows, t, 64 * h:64 * h + 64], w[rows, :],
                                            start=(h == 0), stop=(h == 1), skip_group_check=True)
                ins.then_inc(q["y_in_psum"], 1)

            def attention(layer, u, par, last):
                q = s[layer]
                transpose_probs(q, u, 0)
                transpose_probs(q, u, 1)
                if not last:
                    transpose_in(layer, u + 1, 1 - par)
                weigh_values(q, u, par, 0)
                if not last:
                    queries_keys(layer, u + 1)
                transpose_probs(q, u, 2)
                weigh_values(q, u, par, 1)
                if not last:
                    values(layer, u + 1)
                transpose_probs(q, u, 3)
                weigh_values(q, u, par, 2)
                if not last:
                    scores(layer, u + 1, 1 - par, 0)
                weigh_values(q, u, par, 3)
                if not last:
                    scores(layer, u + 1, 1 - par, 1)
                transpose_heads(q, u, last)
                if not last:
                    scores(layer, u + 1, 1 - par, 2)
                output(layer, u, last)
                if not last:
                    scores(layer, u + 1, 1 - par, 3)

            def start(layer):
                transpose_in(layer, 0, 0)
                queries_keys(layer, 0)
                pe.wait_ge(s[layer]["xcT_ready"], 1)
                values(layer, 0)
                for j in range(QUADS):
                    scores(layer, 0, 0, j)

            def body0(u, par, last):
                q = s[0]
                attention(0, u, par, last)
                pe.wait_ge(q["oT_ready"], u + 1)
                pe.wait_ge(q["xn2_ready"], u + 1)
                for t in range(2):
                    ins = pe.transpose(m0[:, P * t:P * t + P], xr[par][:, t, D:2 * D], ident[:, :])
                ins.then_inc(q["x1T_in_psum"], 1)
                pe.wait_ge(q["x1T_ready"], u + 1)
                pe.wait_ge(q["x_mid_ready"], u + 1)
                for t in range(2):
                    ins = pe.matmul(m1[:, E0 * t:E0 * t + E0], x1T[:, t, :], wr[:, :], start=True, stop=True)
                ins.then_inc(q["logits_in_psum"], 1)
                pe.wait_ge(q["onehot_ready"], u + 1)
                for t in range(2):
                    pe.matmul(m1[:, E0 * t:E0 * t + E0], earlier[:, :], onehot[:, t, :], start=True, stop=False)
                    ins = pe.matmul(m1[:, E0 * t:E0 * t + E0], onesb[:, :], seen[:, t, :], start=False, stop=True)
                ins.then_inc(q["rank_in_psum"], 1)

            start(0)
            units(pe, body0)

            pe.wait_ge(s[0]["pos_ready"], UNITS)
            pe.matmul(m1[:, 0:E0], onesb[:, :], seen[:, 0, :], start=True, stop=True)
            pe.matmul(m1[:, 64:65], earlier[:, :], onesb[:, 0:1], start=True, stop=True)\
                .then_inc(routed["count_in_psum"], 1)
            pe.wait_ge(routed["table"], 2)
            pe.wait_ge(load["moe"], 16 * 4)

            def expert_of(sl):
                return pe.value_load(slot_e[0:1, bass.ds(sl, 1)], min_val=0, max_val=E0 - 1)

            def hidden(sl, par, first=False):
                pe.wait_ge(slot_loaded[par], 8 * (sl - par + 2))
                pe.transpose(m0[:, 0:P], xs[par][:, D:2 * D], ident[:, :]).then_inc(b["xT_in_psum"], 1)
                e = expert_of(sl)
                pe.wait_ge(b["xT_ready"], sl + 1)
                if not first:
                    pe.wait_ge(b["h_ready"], sl - 1)
                pe.matmul(s_bank[par][:, :], xsT[par][:, :], w1[:, bass.ds(e * F0, F0)], start=True, stop=True)\
                    .then_inc(b["h_in_psum"], 1)

            def transpose_h(sl, par):
                pe.wait_ge(b["gelu_ready"], sl + 1)
                pe.wait_ge(b["hT_ready"], sl)
                for j in range(FJ):
                    ins = pe.transpose(tb[:, P * j:P * j + P], hb[par][:, P * j:P * j + P], ident[:, :])
                ins.then_inc(b["hT_in_psum"], 1)

            def down(sl, par):
                e = expert_of(sl)
                pe.wait_ge(b["hT_ready"], sl + 1)
                pe.wait_ge(b["vec_y"], sl)
                for j in range(FJ):
                    ins = pe.matmul(po[:, 0:D], hT[par][:, P * j:P * j + P], w2[:, bass.ds((e * FJ + j) * D, D)],
                                    start=(j == 0), stop=(j == FJ - 1))
                ins.then_inc(b["y_in_psum"], 1)

            def slot(sl, par, last):
                transpose_h(sl, par)
                if not last:
                    hidden(sl + 1, 1 - par)
                down(sl, par)

            hidden(0, 0, True)
            slot(0, 0, False)
            slot(1, 1, False)
            with pe.Fori(1, SLOTS // 2 - 1) as i:
                for par in range(2):
                    slot(i * 2 + par, par, False)
            slot(SLOTS - 2, 0, False)
            slot(SLOTS - 1, 1, True)
            pe.wait_ge(load["experts1"], 16 * 4)
            pe.wait_ge(setup["vec_done"], 11)
            pe.wait_ge(b["y_ready"], SLOTS)

            def body1(u, par, last):
                q = s[1]
                attention(1, u, par, last)
                pe.wait_ge(q["xn2_ready"], 2 * u + 2)
                pe.wait_ge(q["oT_ready"], u + 1)
                for t in range(2):
                    ins = pe.transpose(m0[:, P * t:P * t + P], hn[:, t, :], ident[:, :])
                ins.then_inc(q["x1T_in_psum"], 1)
                pe.wait_ge(q["x1T_ready"], u + 1)
                pe.wait_ge(q["x_mid_ready"], u + 1)
                for t in range(2):
                    ins = pe.matmul(m1[:, E1 * t:E1 * t + E1], hnT[:, P * t:P * t + P], simn[:, :],
                                    start=True, stop=True)
                ins.then_inc(q["logits_in_psum"], 1)
                pe.wait_ge(f["w3_ready"], u + 1)
                apart(pe)
                for t in range(2):
                    ins = pe.transpose(m0_bf[0:3 * E1, P * t:P * t + P], w3[:, t, :, :], identb[:, :])
                ins.then_inc(f["w3T_in_psum"], 1)
                pe.wait_ge(f["w3T_ready"], u + 1)
                pe.wait_ge(q["scores_ready"], 4 * u + (4 if last else 8))

                def spread(base):
                    for k in range(E1 // 2):
                        if k >= QUADS:
                            pe.wait_ge(ring_used, u * E1 + base + k - QUADS + 1)
                        for e in range(2):
                            ins = pe.matmul(s_bank[k % QUADS][:, 256 * e:256 * e + 256], term_sel[:, 2 * k + e, :],
                                            w3T[:, :], start=True, stop=True)
                        ins.then_inc(ring_filled, 1)

                spread(0)
                for k in range(2):
                    for e in range(E1):
                        if k == 0 and e % 2 == 0:
                            pe.wait_ge(ring_used, u * E1 + e // 2 + 1)
                        ins = pe.matmul(m1[:, 256 * k:256 * k + 256], proj[:, k, e, :], z[:, e, :],
                                        start=(e == 0), stop=(e == E1 - 1))
                ins.then_inc(f["qk1_in_psum"], 1)
                for t in range(2):
                    for e in range(E1):
                        ins = pe.matmul(m0[:, P * t:P * t + P], z[:, e, P * t:P * t + P], proj[:, 2, e, :],
                                        start=(e == 0), stop=(e == E1 - 1))
                ins.then_inc(f["v1_in_psum"], 1)
                pe.wait_ge(f["qk1_ready"], u + 1)
                pe.wait_ge(q["heads_ready"], 2 * u + 2)
                apart(pe)
                for t in range(2):
                    for half in range(2):
                        seq = slice(LEN * (2 * t + half), LEN * (2 * t + half) + LEN)
                        ins = pe.matmul(po[64 * half:64 * half + 64, LEN * t:LEN * t + LEN], qkT[:, 0, seq],
                                        qkT[:, 1, seq], start=True, stop=True, skip_group_check=True)
                ins.then_inc(f["s1_in_psum"], 1)
                pe.wait_ge(f["pn_ready"], u + 1)
                pe.wait_ge(q["probT_ready"], 4 * u + 4)
                for t in range(2):
                    ins = pe.transpose(tb[:, P * t:P * t + P], pbd[:, t, :, :], ident[:, :])
                ins.then_inc(f["pT_in_psum"], 1)
                pe.wait_ge(f["pT_ready"], u + 1)
                pe.wait_ge(f["v1_ready"], u + 1)
                for t in range(2):
                    ins = pe.matmul(m0[:, P * t:P * t + P], vh[:, t, :], pbT[:, P * t:P * t + P],
                                    start=True, stop=True)
                ins.then_inc(f["o1_in_psum"], 1)
                spread(E1 // 2)
                for t in range(2):
                    for e in range(E1):
                        if t == 0 and e % 2 == 0:
                            pe.wait_ge(ring_used, u * E1 + E1 // 2 + e // 2 + 1)
                        ins = pe.matmul(m1[:, P * t:P * t + P], z[:, e, P * t:P * t + P], proj[:, 3, e, :],
                                        start=(e == 0), stop=(e == E1 - 1))
                ins.then_inc(f["y1_in_psum"], 1)

            start(1)
            units(pe, body1)


def kernel(**inputs):
    import numpy as _np
    import concourse.bacc as _bacc
    from concourse import mybir as _mybir
    from concourse.bass_utils import run_bass_kernel_spmd as _run

    nc = _bacc.Bacc("TRN2", target_bir_lowering=False, num_devices=1)
    arrays, args = {}, {}
    for name in inputs:
        x = _np.ascontiguousarray(inputs[name])
        if name in ("x", "ctx_1024"):
            x = x.reshape(-1, x.shape[-1])
        arrays[f"in_{name}"] = x
        args[name] = nc.dram_tensor(f"in_{name}", x.shape, _mybir.dt.from_np(x.dtype), kind="ExternalInput").ap()
    shape = _np.shape(inputs["x"])
    out = nc.dram_tensor("out_x", (shape[0] * shape[1], shape[2]), _mybir.dt.float32, kind="ExternalOutput").ap()
    flamingo(nc, args, out)
    r = _run(nc, [arrays], core_ids=[0])
    return r.results[0]["out_x"].reshape(shape)
```

```python
from contextlib import ExitStack

import numpy as np
import concourse.bass as bass
from concourse import mybir

ALU = mybir.AluOpType
ACT = mybir.ActivationFunctionType
AX_X = mybir.AxisListType.X
F32 = mybir.dt.float32
BF16 = mybir.dt.bfloat16
I32 = mybir.dt.int32
U32 = mybir.dt.uint32
U8 = mybir.dt.uint8

P = 128
SEQS, LEN, D = 128, 64, 128
N = SEQS * LEN
HEADS, HD = 16, 8
UNIT = 256
UNITS = N // UNIT
QUADS = 4
E0, F0 = 8, 512
E1 = 16
FJ = F0 // P
RING0 = 6
SLOTS = N // P + E0
REGION = N + (E0 + 2) * P
ROWW = 2 * D + 1
CHUNK = 32
MASKED = -(2.0 ** 126)
EPS = 1e-5
SCALE = float(np.float32(1.0) / np.sqrt(np.float32(HD)))
SCALE_H = float(1.0 / np.sqrt(np.float32(D)))
VW = 17


class Steps:

    def __init__(self, eng, sem, unit, per_unit):
        self.eng, self.sem, self.unit, self.per_unit, self.n = eng, sem, unit, per_unit, 0

    def free(self, ins):
        self.n += 1
        ins.then_inc(self.sem, 1)

    def wait(self):
        self.eng.wait_ge(self.sem, self.unit * self.per_unit + self.n)

    def __call__(self, ins):
        self.free(ins)
        self.wait()

    def end(self):
        assert self.n == self.per_unit, (self.n, self.per_unit)


def bcast(ap, n, at):
    return ap.unsqueeze(at).broadcast_to(list(ap.shape[:at]) + [n] + list(ap.shape[at:]))


def flamingo(nc, a, out):
    ctx = ExitStack()
    with ctx:
        ctx.enter_context(nc.allow_non_contiguous_dma("small constant loads"))

        def sb(name, shape, dt=F32):
            return ctx.enter_context(nc.sbuf_tensor(name, shape, dt))

        def bank(name):
            return ctx.enter_context(nc.psum_tensor(name, [P, 512], F32))

        def sem(name):
            return ctx.enter_context(nc.semaphore(name))

        sorted_in = nc.dram_tensor("sorted_in", (E0 * REGION, ROWW), F32, kind="Internal").ap()
        sorted_out = nc.dram_tensor("sorted_out", (SLOTS * P, D), F32, kind="Internal").ap()

        ident = sb("ident", [P, P])
        identb = sb("identb", [P, P], BF16)
        onesf = sb("onesf", [P, P])
        onesb = sb("onesb", [P, P], BF16)
        earlier = sb("earlier", [P, P], BF16)
        mask_rows = sb("mask_rows", [LEN + 1, 2, LEN], BF16)
        mask_chunk = sb("mask_chunk", [LEN, 8, LEN], BF16)
        mask_causal = [sb(f"mask_causal{b}", [LEN + 1, 8, LEN], BF16) for b in range(2)]
        head_blk = sb("head_blk", [P, HEADS])
        head_of = sb("head_of", [P, 4])
        head_bq = sb("head_bq", [P, 2, 4])
        term_sel = sb("term_sel", [3 * E1, E1, P], BF16)
        iota = sb("iota", [P, 2, E1])
        region0 = sb("region0", [P, E0])
        slot_no = sb("slot_no", [1, SLOTS])
        half_neg = sb("half_neg", [P, 2])
        eps = sb("eps", [P, 2])
        masked = sb("masked", [LEN + 1, UNIT])
        half_pos = sb("half_pos", [P, E1])
        pad_u8 = sb("pad_u8", [LEN + 1, N], U8)
        pad_unit = sb("pad_unit", [LEN + 1, UNIT])
        wraw = sb("wraw", [P, 10, P])
        wq = [sb(f"wq{l}", [P, P]) for l in range(2)]
        wk = [sb(f"wk{l}", [P, P]) for l in range(2)]
        wv = [sb(f"wv{l}", [P, P]) for l in range(2)]
        wo = [sb(f"wo{l}", [P, P]) for l in range(2)]
        wos = [sb(f"wos{l}", [P, 2, P]) for l in range(2)]
        brow = sb("brow", [1, 4, P])
        browp = sb("browp", [1, 4, P])
        bcol = sb("bcol", [P, 4])
        bvcol = sb("bvcol", [P, 2])
        bvb = sb("bvb", [P, 2, P])
        bo_b = sb("bo_b", [P, 2, P])
        gbo = sb("gbo", [P, 2, P])
        graw = sb("graw", [P, 4])
        tg = sb("tg", [P, 4])
        w1 = sb("w1", [P, E0 * F0])
        w2 = sb("w2", [P, E0 * FJ * D])
        b1b = sb("b1b", [P, E0 * F0])
        b2b = sb("b2b", [P, E0 * D])
        wr = sb("wr", [P, E0])
        brb = sb("brb", [P, E0])
        proj = sb("proj", [P, 4, E1, D])
        simm = sb("simm", [P, E1])
        simq = sb("simq", [P, E1])
        simn = sb("simn", [P, E1])
        sgate = sb("sgate", [P, E1])

        xin = [sb(f"xin{b}", [P, 2, D]) for b in range(2)]
        cin = [sb(f"cin{b}", [P, 2, D]) for b in range(2)]
        st6 = sb("st6", [P, 2, 6])
        mv = sb("mv", [P, 2, 2])
        rstd = sb("rstd", [P, 2])
        vare = sb("vare", [P, 2])
        xn = sb("xn", [P, 2, D])
        xb = [sb(f"xb{b}", [P, 2, D]) for b in range(2)]
        xcT = sb("xcT", [P, 4, P])
        qx = sb("qx", [P, 4, 4, LEN])
        kT = sb("kT", [P, UNIT])
        vb = [sb(f"vb{b}", [P, 2, 8, 2, VW]) for b in range(2)]
        mx = sb("mx", [P, QUADS, 8])
        prob = [sb(f"prob{j}", [P, 2, 4, LEN]) for j in range(QUADS)]
        pT = [sb(f"pT{b}", [P, 2, 2, P]) for b in range(2)]
        rden = sb("rden", [P, 4, 4])
        on = sb("on", [P, 4, 8, HD])
        oT = sb("oT", [P, 2, 2, 2, LEN])
        xr = [sb(f"xr{b}", [P, 2, ROWW + 7]) for b in range(2)]
        st6b = sb("st6b", [P, 2, 6])
        mvb = sb("mvb", [P, 2, 2])
        vareb = sb("vareb", [P, 2])
        rstdb = sb("rstdb", [P, 2])
        x1T = sb("x1T", [P, 2, P])
        lg = sb("lg", [P, 2, E1])
        top = sb("top", [P, 2, 8])
        topi = sb("topi", [P, 2, 8], U32)
        onehot = sb("onehot", [P, 2, E0], BF16)
        seen = sb("seen", [P, 2, E0], BF16)
        ex = sb("ex", [P, 2, E1])
        den = sb("den", [P, 2])
        gate = sb("gate", [P, 2])
        rank = sb("rank", [P, 2, E0])
        rsel = sb("rsel", [P, 2, E0])
        posf = sb("posf", [P, 2])
        posi = [sb(f"posi{b}", [P, 2], I32) for b in range(2)]
        place = sb("place", [P, UNITS, 2])
        beyond = sb("beyond", [P, UNITS, 2])
        placed = sb("placed", [P, UNITS, 2])
        move = sb("move", [P, E0 - 1])
        placei = sb("placei", [P, UNITS, 2], I32)
        gidx = [sb(f"gidx{b}", [P, 2], I32) for b in range(2)]
        count = sb("count", [P, E0])
        tiles = sb("tiles", [P, E0])
        tilesi = sb("tilesi", [P, E0], I32)
        tend = sb("tend", [1, E0])
        full = sb("full", [1, SLOTS, E0 - 1])
        fullt = sb("fullt", [1, SLOTS, E0 - 1])
        slotf = sb("slotf", [1, 5, SLOTS])
        slot_e = sb("slot_e", [1, SLOTS], I32)
        slot_row = sb("slot_row", [1, SLOTS], I32)
        padf = sb("padf", [P, 2 * E0])
        padi = sb("padi", [P, 2 * E0 + 2], I32)
        zrow = sb("zrow", [P, ROWW])
        xs = [sb(f"xs{b}", [P, ROWW]) for b in range(RING0)]
        xsT = [sb(f"xsT{b}", [P, P]) for b in range(2)]
        hb = [sb(f"hb{b}", [P, F0]) for b in range(2)]
        hT = [sb(f"hT{b}", [P, F0]) for b in range(2)]
        yb = [sb(f"yb{b}", [P, D]) for b in range(2)]
        yo = [sb(f"yo{b}", [P, D]) for b in range(2)]
        x3 = [sb(f"x3{b}", [P, 2, D]) for b in range(2)]
        hn = sb("hn", [P, 2, D])
        width = sb("width", [P, 2])
        dvar = sb("dvar", [P, 2])
        dnorm = sb("dnorm", [P, 2])
        nrm = sb("nrm", [P, 2])
        rnrm = sb("rnrm", [P, 2])
        hnT = sb("hnT", [P, UNIT])
        gm = sb("gm", [P, 2, E1])
        fb = sb("fb", [P, 2, 2, E1])
        idle = sb("idle", [P, 2])
        gtop = sb("gtop", [P, 2])
        wg = sb("wg", [P, 2, E1])
        wres = sb("wres", [P, 2, E1])
        w3 = sb("w3", [P, 2, 3, E1], BF16)
        w3T = sb("w3T", [3 * E1, UNIT], BF16)
        z = w1[:, :].rearrange("p (e n) -> p e n", e=E1)
        qkT = sb("qkT", [P, 2, UNIT])
        vh = sb("vh", [P, 2, D])
        smx = sb("smx", [P, 2])
        sd = sb("sd", [P, 2, LEN])
        pbd = sb("pbd", [P, 2, 2, LEN])
        srs = sb("srs", [P, 2])
        pbT = sb("pbT", [P, UNIT])
        ohT = sb("ohT", [P, UNIT])
        res = [sb(f"res{b}", [P, 2, D]) for b in range(2)]

        m0 = bank("m0")
        m1 = bank("m1")
        s_bank = [bank(f"s_bank{j}") for j in range(QUADS)]
        tb = bank("tb")
        po = bank("po")
        m0_bf = m0[:, :].bitcast(BF16)

        names = ("vec_ln", "pool_ln", "rstd_ready", "xn_ready", "residual_ready",
                 "xc_in_psum", "xcT_ready", "qk_in_psum", "qk_ready", "v_in_psum", "v_ready", "scores_in_psum",
                 "vec_max", "scores_ready", "exp_ready", "probT_in_psum", "probT_ready", "pv_in_psum",
                 "vec_rden", "heads_ready", "oT_in_psum", "oT_ready", "y_in_psum", "x_mid_ready", "pad_row_ready",
                 "pool_pad", "vec_ln2", "pool_ln2", "rstd2_ready", "xn2_ready", "x1T_in_psum", "x1T_ready",
                 "logits_in_psum", "logits_ready", "exp8_ready", "idx_ready")
        s = [{n: sem(f"{n}_{l}") for n in names} for l in range(2)]
        rnames = ("router_steps", "onehot_ready", "rank_in_psum", "rank_steps", "pos_ready")
        route = {n: sem(n) for n in rnames}
        x_loaded = [[sem(f"x_loaded_{l}_{par}") for par in range(2)] for l in range(2)]
        ctx_loaded = [[sem(f"ctx_loaded_{l}_{par}") for par in range(2)] for l in range(2)]
        slot_loaded = [sem(f"slot_loaded_{n}") for n in range(RING0)]
        stored = [sem(f"stored_{par}") for par in range(2)]
        scattered = [sem(f"scattered_{par}") for par in range(2)]
        ring_filled = sem("ring_filled")
        ring_used = sem("ring_used")
        z_used = sem("z_used")
        fnames = ("nrm_steps", "nrm_ready", "gate_steps", "gate_logits", "wexp_ready", "w3_ready",
                  "w3T_in_psum", "w3T_ready", "qk1_ready", "v1_ready", "s1_in_psum", "s1_ready",
                  "p1_ready", "vec_s1", "vec_p1", "pn_ready", "pT_in_psum", "pT_ready", "o1_in_psum", "o1_ready",
                  "res_ready")
        f = {n: sem(f"f_{n}") for n in fnames}
        load = {n: sem(f"load_{n}") for n in ("attn", "moe", "experts1", "small", "swap")}
        setup = {n: sem(f"setup_{n}") for n in ("pool", "tensor", "scalar", "vector", "consts", "vec_done")}
        routed = {n: sem(f"routed_{n}") for n in ("count_in_psum", "vector", "table", "padded", "zero")}
        passed = sem("passed")
        out_sem = [sem(f"out_sem_{par}") for par in range(2)]
        b = {n: sem(f"moe_{n}") for n in ("xT_in_psum", "xT_ready", "h_in_psum", "h_ready", "gelu_ready",
                                          "hT_in_psum", "hT_ready", "y_in_psum", "vec_y", "y_ready")}

        def apart(eng):
            eng.sem_inc(passed, 1)

        block = ctx.enter_context(nc.Block())

        def exists(unit):
            return not isinstance(unit, int) or 0 <= unit < UNITS

        def wait(eng, semaphore, count):
            if not isinstance(count, int) or count > 0:
                eng.wait_ge(semaphore, count)

        def units(eng, body):
            for u in range(-2, 2):
                body(u, u % 2)
            with eng.Fori(1, UNITS // 2 - 2) as i:
                for par in range(2):
                    body(i * 2 + par, par)
            for u in range(UNITS - 4, UNITS + 1):
                body(u, u % 2)

        def slots(eng, body):
            for sl in range(-3, RING0):
                body(sl, sl % RING0, sl % 2, sl // RING0)
            with eng.Fori(1, SLOTS // RING0 - 1) as i:
                for n in range(RING0):
                    body(i * RING0 + n, n, n % 2, i)
            for sl in range(SLOTS - RING0, SLOTS):
                body(sl, sl % RING0, sl % 2, sl // RING0)

        def slot_exists(sl):
            return not isinstance(sl, int) or 0 <= sl < SLOTS

        @block.sync
        def _(sp):
            def tokens(ap, u):
                return ap[bass.ds(u * UNIT, UNIT), :].rearrange("(t p) d -> p t d", p=P)

            def load_unit(layer, v, par):
                if layer == 0:
                    sp.dma_start(xin[par][:, :, :], tokens(a["x"], v)).then_inc(x_loaded[0][par], 16)
                sp.dma_start(cin[par][:, :, :], tokens(a["ctx_1024"], v)).then_inc(ctx_loaded[layer][par], 16)

            def body(layer, u, par):
                q = s[layer]
                if exists(u + 3) and not (isinstance(u, int) and u < -1):
                    if layer == 0:
                        wait(sp, q["residual_ready"], u + 2)
                    wait(sp, q["xc_in_psum"], u + 2)
                    load_unit(layer, u + 3, 1 - par)
                if layer == 1 and exists(u - 1):
                    wait(sp, f["res_ready"], u)
                    sp.dma_start(tokens(out, u - 1), res[1 - par][:, :, :]).then_inc(out_sem[1 - par], 16)

            load_unit(0, 0, 0)
            for k, n in enumerate(("L0_xattn_Wq", "L0_xattn_Wk", "L0_xattn_Wv", "L1_xattn_Wq", "L1_xattn_Wk",
                                   "L1_xattn_Wv", "L1_xattn_Wo")):
                sp.dma_start(wraw[:, k, :], a[n]).then_inc(load["attn"], 16)
            sp.dma_start(wraw[:, 7, 0:64], a["L1_xattn_Wo"][:, 64:128]).then_inc(load["attn"], 16)
            sp.dma_start(wraw[:, 7, 64:128], a["L1_xattn_Wo"][:, 0:64]).then_inc(load["attn"], 16)
            sp.dma_start(wo[0][:, :], a["L0_xattn_Wo"]).then_inc(load["attn"], 16)
            for h in range(2):
                for half in range(2):
                    sp.dma_start(wos[0][64 * half:64 * half + 64, h, :], a["L0_xattn_Wo"][64 * h:64 * h + 64, :])\
                        .then_inc(load["attn"], 16)
            for k, n in enumerate(("L0_xattn_bq", "L0_xattn_bk", "L1_xattn_bq", "L1_xattn_bk")):
                sp.dma_start(brow[0:1, k, :], a[n].unsqueeze(0)).then_inc(load["small"], 16)
            for l in range(2):
                sp.dma_start(bvcol[:, l:l + 1], a[f"L{l}_xattn_bv"].unsqueeze(1)).then_inc(load["small"], 16)
                sp.dma_start(bo_b[:, l, :], a[f"L{l}_xattn_bo"].partition_broadcast(P)).then_inc(load["small"], 16)
            sp.dma_start(graw[:, 0:2], a["g_xattn"].partition_broadcast(P)).then_inc(load["small"], 16)
            sp.dma_start(graw[:, 2:4], a["g_ffn"].partition_broadcast(P)).then_inc(load["small"], 16)
            sp.dma_start(wr[:, :], a["L0_ffn_Wr"]).then_inc(load["small"], 16)
            sp.dma_start(brb[:, :], a["L0_ffn_br"].partition_broadcast(P)).then_inc(load["small"], 16)
            sp.dma_start(simm[:, :], a["L1_ffn_sim_matrix"]).then_inc(load["small"], 16)
            sp.dma_start(sgate[:, :], a["L1_ffn_gates"].partition_broadcast(P)).then_inc(load["small"], 16)
            sp.dma_start(pad_u8[LEN:LEN + 1, :], a["mask_BxS2_bf0"].rearrange("b s -> (b s)").unsqueeze(0))\
                .then_inc(load["small"], 16)
            load_unit(0, 1, 1)
            sp.dma_start(w1[:, :].rearrange("c (e n) -> c e n", e=E0), a["L0_ffn_W1"].rearrange("e c n -> c e n"))\
                .then_inc(load["moe"], 16)
            sp.dma_start(w2[:, :].rearrange("c (e n) -> c e n", n=D),
                         a["L0_ffn_W2"].rearrange("e (j c) n -> c (e j) n", c=P)).then_inc(load["moe"], 16)
            sp.dma_start(b1b[:, :], a["L0_ffn_b1"].rearrange("e n -> (e n)").partition_broadcast(P))\
                .then_inc(load["moe"], 16)
            sp.dma_start(b2b[:, :], a["L0_ffn_b2"].rearrange("e n -> (e n)").partition_broadcast(P))\
                .then_inc(load["moe"], 16)
            for k, n in enumerate("qkvo"):
                sp.dma_start(proj[:, k, :, :], a[f"L1_ffn_{n}_proj"].rearrange("e c n -> c e n"))\
                    .then_inc(load["experts1"], 16)
            units(sp, lambda u, par: body(0, u, par))

            sp.wait_ge(routed["table"], 2)
            sp.wait_ge(routed["padded"], 16 * 2 * (E0 + 1))
            for par in range(2):
                sp.wait_ge(scattered[par], 16 * UNITS)

            def load_slot(sl, n):
                row = sp.value_load(slot_row[0:1, bass.ds(sl, 1)], min_val=0, max_val=E0 * REGION - P)
                sp.dma_start(xs[n][:, :], sorted_in[bass.ds(row, P), :]).then_inc(slot_loaded[n], 16)

            def slot(sl, n, par, rnd):
                if slot_exists(sl):
                    sp.wait_ge(b["y_ready"], sl + 1)
                    sp.dma_start(sorted_out[bass.ds(sl * P, P), :], yo[par][:, :]).then_inc(stored[par], 16)
                    if slot_exists(sl + RING0):
                        load_slot(sl + RING0, n)

            for sl in range(RING0):
                load_slot(sl, sl)
            slots(sp, slot)

            load_unit(1, 0, 0)
            load_unit(1, 1, 1)
            units(sp, lambda u, par: body(1, u, par))
            for par in range(2):
                sp.wait_ge(out_sem[par], 8 * UNITS)

        @block.gpsimd
        def _(g):
            done = Steps(g, setup["pool"], 0, 0)
            for t, v in ((ident[:, :], 0.0), (identb[:, :], 0.0), (onesf[:, :], 1.0), (onesb[:, :], 1.0),
                         (earlier[:, :], 1.0), (mask_rows[:, :, :], 0.0), (mask_chunk[:, :, :], 0.0),
                         (mask_causal[0][:, :, :], 0.0), (mask_causal[1][:, :, :], 0.0), (head_blk[:, :], 1.0),
                         (term_sel[:, :, :], 0.0), (half_neg[:, :], -0.5), (half_pos[:, :], 0.5),
                         (eps[:, :], EPS), (masked[:, :], MASKED), (width[:, :], float(D)),
                         (zrow[:, :], 0.0), (pbd[:, :, :, :], 0.0), (vb[0][:, :, :, :, :], 0.0),
                         (vb[1][:, :, :, :, :], 0.0), (seen[:, 0, :], 0.0), (oT[:, :, :, :, :], 0.0)):
                done.free(g.memset(t, v))
            g.wait_ge(setup["pool"], done.n)
            for t in (ident, identb):
                done.free(g.affine_select(out=t[:, :], in_=t[:, :], compare_op=ALU.not_equal, fill=1.0, base=0,
                                          pattern=[[-1, P]], channel_multiplier=1))
            done.free(g.affine_select(out=earlier[:, :], in_=earlier[:, :], compare_op=ALU.is_gt, fill=0.0, base=0,
                                      pattern=[[1, P]], channel_multiplier=-1))
            done.free(g.affine_select(out=mask_rows[0:LEN], in_=mask_rows[0:LEN], compare_op=ALU.not_equal,
                                      fill=1.0, base=0, pattern=[[0, 2], [-1, LEN]], channel_multiplier=1))
            done.wait()
            done(g.memset(mask_rows[LEN:LEN + 1], 1.0))
            done(g.memset(mask_chunk[0:CHUNK, :, CHUNK:LEN], MASKED))
            for m in mask_causal:
                done.free(g.affine_select(out=m[0:LEN], in_=m[0:LEN], compare_op=ALU.is_ge, fill=MASKED, base=0,
                                          pattern=[[0, 8], [-1, LEN]], channel_multiplier=1))
            done(g.affine_select(out=head_blk[:, :], in_=head_blk[:, :], compare_op=ALU.is_ge, fill=0.0, base=0,
                                 pattern=[[-HD, HEADS]], channel_multiplier=1))
            done(g.affine_select(out=head_blk[:, :], in_=head_blk[:, :], compare_op=ALU.is_ge, fill=0.0,
                                 base=HD - 1, pattern=[[HD, HEADS]], channel_multiplier=-1))
            for t in range(3):
                done(g.affine_select(out=term_sel[:, :, :], in_=term_sel[:, :, :], compare_op=ALU.not_equal,
                                     fill=1.0, base=-E1 * t, pattern=[[-1, E1], [0, P]], channel_multiplier=1))
            for v in vb:
                done(g.memset(v[0:64, :, :, 0, VW - 1:VW], 1.0))
                done(g.memset(v[64:128, :, :, 1, VW - 1:VW], 1.0))
            done(g.iota(iota[:, :, :], pattern=[[0, 2], [1, E1]], base=0, channel_multiplier=0,
                        allow_small_or_imprecise_dtypes=True))
            done(g.iota(slot_no[:, :], pattern=[[1, SLOTS]], base=0, channel_multiplier=0,
                        allow_small_or_imprecise_dtypes=True))
            done(g.tensor_scalar(region0[:, :], iota[:, 0, 0:E0], float(REGION), None, ALU.mult))
            g.memset(half_neg[:, :], -0.5).then_inc(setup["consts"], 1)
            g.wait_ge(setup["vector"], 1)
            g.tensor_tensor(simn[:, :], simq[:, :], half_pos[:, :], ALU.pow).then_inc(setup["consts"], 1)
            g.wait_ge(setup["vec_done"], 6)

            def gather(v, par):
                q = s[1]
                if exists(v - 2):
                    g.wait_ge(q["residual_ready"], v - 1)
                wait(g, q["pad_row_ready"], v)
                apart(g)
                g.tensor_copy(gidx[par][:, :], placei[:, bass.ds(v, 1), :].rearrange("p a t -> p (a t)"))\
                    .then_inc(q["idx_ready"], 1)
                g.wait_ge(q["idx_ready"], v + 1)
                apart(g)
                for t in range(2):
                    g.indirect_dma_start(
                        out=xin[par][:, t, :], out_offset=None, in_=sorted_out[:, :],
                        in_offset=bass.IndirectOffsetOnAxis(ap=gidx[par][:, t:t + 1], axis=0),
                        bounds_check=SLOTS * P - 1, oob_is_err=True).then_inc(x_loaded[1][par], 16)

            def pad_row(v, par):
                q = s[1]
                wait(g, q["scores_in_psum"], 4 * v - 4)
                g.wait_ge(x_loaded[1][par], 16 * (v - par + 2))
                wait(g, q["residual_ready"], v)
                step = Steps(g, q["pool_pad"], v, 1)
                step(g.tensor_copy(pad_unit[LEN:LEN + 1, :], pad_u8[LEN:LEN + 1, bass.ds(v * UNIT, UNIT)]))
                step.end()
                g.tensor_tensor(mask_causal[par][LEN:LEN + 1, :, :].rearrange("p (r k) n -> p r (k n)", r=2),
                                bcast(pad_unit[LEN:LEN + 1, :], 2, 1),
                                bcast(masked[LEN:LEN + 1, :], 2, 1), ALU.mult).then_inc(q["pad_row_ready"], 1)

            def norm(layer, v, par):
                q = s[layer]
                g.wait_ge(q["vec_ln"], 4 * v + 4)
                if layer == 1:
                    g.wait_ge(q["pad_row_ready"], v + 1)
                step = Steps(g, q["pool_ln"], v, 2)
                step(g.tensor_tensor(vare[:, :], mv[:, :, 1], eps[:, :], ALU.add))
                step(g.tensor_tensor(rstd[:, :], vare[:, :], half_neg[:, :], ALU.pow))
                step.end()
                wait(g, q["xc_in_psum"], v)
                apart(g)
                for t in range(2):
                    ins = g.tensor_scalar(xn[:, t, :], xin[par][:, t, :], mv[:, t, 0:1], rstd[:, t:t + 1],
                                          ALU.subtract, ALU.mult)
                ins.then_inc(q["xn_ready"], 1)

            def residual(layer, v, par):
                q = s[layer]
                g.wait_ge(x_loaded[layer][par], (8 + 8 * layer) * (v - par + 2))
                wait(g, q["x_mid_ready"], v - 1)
                g.tensor_tensor(xb[par][:, :, :], xin[par][:, :, :], bcast(gbo[:, layer, :], 2, 1), ALU.add)\
                    .then_inc(q["residual_ready"], 1)

            def second_norm(layer, u, src, dst):
                q = s[layer]
                g.wait_ge(q["vec_ln2"], 4 * u + 4)
                step = Steps(g, q["pool_ln2"], u, 2)
                step(g.tensor_tensor(vareb[:, :], mvb[:, :, 1], eps[:, :], ALU.add))
                step(g.tensor_tensor(rstdb[:, :], vareb[:, :], half_neg[:, :], ALU.pow))
                step.end()
                if layer == 1:
                    wait(g, q["x1T_in_psum"], u)
                apart(g)
                for t in range(2):
                    ins = g.tensor_scalar(dst(t), src(t), mvb[:, t, 0:1], rstdb[:, t:t + 1], ALU.subtract, ALU.mult)
                ins.then_inc(q["xn2_ready"], 1)

            def body0(u, par):
                if exists(u + 2):
                    norm(0, u + 2, par)
                if exists(u - 1):
                    g.wait_ge(route["pos_ready"], u)
                    apart(g)
                    for t in range(2):
                        g.indirect_dma_start(
                            out=sorted_in[:, :],
                            out_offset=bass.IndirectOffsetOnAxis(ap=posi[1 - par][:, t:t + 1], axis=0),
                            in_=xr[1 - par][:, t, 0:ROWW], in_offset=None,
                            bounds_check=E0 * REGION - 1, oob_is_err=True).then_inc(scattered[1 - par], 16)
                if exists(u):
                    second_norm(0, u, lambda t: xr[par][:, t, 0:D], lambda t: xr[par][:, t, D:2 * D])
                if exists(u + 2):
                    residual(0, u + 2, par)

            units(g, body0)

            g.wait_ge(routed["zero"], 1)
            for k in range(2 * E0 + 2):
                g.indirect_dma_start(
                    out=sorted_in[:, :], out_offset=bass.IndirectOffsetOnAxis(ap=padi[:, k:k + 1], axis=0),
                    in_=zrow[:, :], in_offset=None,
                    bounds_check=E0 * REGION - 1, oob_is_err=True).then_inc(routed["padded"], 16)

            g.wait_ge(routed["table"], 3)
            for par in range(2):
                g.wait_ge(stored[par], 8 * SLOTS)

            def body1(u, par):
                q = s[1]
                if exists(u + 2):
                    pad_row(u + 2, par)
                if exists(u + 3):
                    gather(u + 3, 1 - par)
                if exists(u + 2):
                    norm(1, u + 2, par)
                if exists(u):
                    second_norm(1, u, lambda t: x3[par][:, t, :], lambda t: hn[:, t, :])
                    step = Steps(g, f["nrm_steps"], u, 2)
                    step(g.tensor_tensor(dvar[:, :], mvb[:, :, 1], width[:, :], ALU.mult))
                    step(g.tensor_tensor(dnorm[:, :], dvar[:, :], half_pos[:, 0:2], ALU.pow))
                    step.end()
                    g.tensor_tensor(nrm[:, :], dnorm[:, :], rstdb[:, :], ALU.mult).then_inc(f["nrm_ready"], 1)
                if exists(u + 2):
                    residual(1, u + 2, par)

            gather(0, 0)
            units(g, body1)

        @block.scalar
        def _(act):
            act.wait_ge(load["small"], 16 * 15)
            act.activation(tg[:, :], graw[:, :], ACT.Tanh).then_inc(setup["scalar"], 1)
            act.activation(sgate[:, :], sgate[:, :], ACT.Exp, scale=-1.0).then_inc(setup["scalar"], 1)
            act.wait_ge(setup["vec_done"], 12)

            def copy_xcT(q, v):
                if exists(v):
                    act.wait_ge(q["xc_in_psum"], v + 1)
                    wait(act, q["v_in_psum"], v)
                    act.activation(xcT[:, :, :], m0[:, :].rearrange("p (a b) -> p a b", a=4), ACT.Copy)\
                        .then_inc(q["xcT_ready"], 1)

            def copy_qk(layer, v):
                q = s[layer]
                if exists(v):
                    act.wait_ge(q["qk_in_psum"], v + 1)
                    wait(act, q["scores_in_psum"], 4 * v)
                    for r in range(4):
                        act.activation(qx[:, :, r, :], m1[:, 0:256].rearrange("p (s k) -> p s k", s=4), ACT.Identity,
                                       bias=head_bq[:, layer, r:r + 1], scale=head_of[:, r:r + 1])
                    act.activation(kT[:, :], m1[:, 256:512], ACT.Identity,
                                   bias=bcol[:, 2 * layer + 1:2 * layer + 2]).then_inc(q["qk_ready"], 1)

            def copy_v(q, v, par):
                if exists(v):
                    act.wait_ge(q["v_in_psum"], v + 1)
                    wait(act, q["pv_in_psum"], 4 * v - 4)
                    for half in range(2):
                        rows = slice(64 * half, 64 * half + 64)
                        ins = act.activation(vb[par][rows, :, :, half, 0:16],
                                             m0[rows, 0:256].rearrange("p (t h d) -> p t h d", t=2, h=8), ACT.Copy)
                    ins.then_inc(q["v_ready"], 1)

            def exp_quad(q, v, j):
                if exists(v):
                    act.wait_ge(q["scores_ready"], 4 * v + j + 1)
                    act.activation(prob[j][:, :, :, :], prob[j][:, :, :, :], ACT.Exp, scale=SCALE)\
                        .then_inc(q["exp_ready"], 1)

            def copy_pT(q, u, j):
                if exists(u):
                    act.wait_ge(q["probT_in_psum"], 4 * u + j + 1)
                    wait(act, q["pv_in_psum"], 4 * u + j - 1)
                    act.activation(pT[j % 2][:, :, :, :], tb[:, :].rearrange("p (r t n) -> p r t n", r=2, t=2),
                                   ACT.Copy).then_inc(q["probT_ready"], 1)

            def copy_oT(q, u):
                if exists(u):
                    act.wait_ge(q["oT_in_psum"], u + 1)
                    wait(act, q["y_in_psum"], u)
                    for half in range(2):
                        rows = slice(64 * half, 64 * half + 64)
                        ins = act.activation(oT[rows, :, :, half, :],
                                             m0[rows, 0:256].rearrange("p (t h n) -> p t h n", t=2, h=2), ACT.Copy)
                    ins.then_inc(q["oT_ready"], 1)

            def body0(u, par):
                q = s[0]
                copy_pT(q, u, 0)
                exp_quad(q, u + 1, 0)
                copy_pT(q, u, 1)
                if exists(u - 1):
                    act.wait_ge(q["x1T_in_psum"], u)
                    act.activation(x1T[:, :, :], m0[:, 0:256].rearrange("p (t n) -> p t n", t=2), ACT.Copy)\
                        .then_inc(q["x1T_ready"], 1)
                exp_quad(q, u + 1, 1)
                copy_pT(q, u, 2)
                exp_quad(q, u + 1, 2)
                copy_pT(q, u, 3)
                if exists(u - 1):
                    act.wait_ge(q["logits_ready"], u)
                    act.activation(ex[:, :, 0:E0], lg[:, :, 0:E0], ACT.Exp).then_inc(q["exp8_ready"], 1)
                copy_xcT(q, u + 2)
                exp_quad(q, u + 1, 3)
                copy_oT(q, u)
                copy_qk(0, u + 2)
                copy_v(q, u + 2, par)

            units(act, body0)

            def slot(sl, n, par, rnd):
                if slot_exists(sl):
                    act.wait_ge(b["hT_in_psum"], sl + 1)
                    act.activation(hT[par][:, :], tb[:, :], ACT.Copy).then_inc(b["hT_ready"], 1)
                if slot_exists(sl + 2):
                    act.wait_ge(b["h_ready"], sl + 3)
                    act.activation(hb[par][:, :], hb[par][:, :], ACT.Gelu).then_inc(b["gelu_ready"], 1)
                if slot_exists(sl + 3):
                    act.wait_ge(b["xT_in_psum"], sl + 4)
                    act.activation(xsT[1 - par][:, :], m0[:, 0:P], ACT.Copy).then_inc(b["xT_ready"], 1)

            slots(act, slot)

            def body1(u, par):
                q = s[1]
                w = u - 1
                if exists(w):
                    act.wait_ge(z_used, 16 * w + 8)
                    act.activation(vh[:, :, :], m0[:, 0:256].rearrange("p (t n) -> p t n", t=2), ACT.Copy)\
                        .then_inc(f["v1_ready"], 1)
                copy_pT(q, u, 0)
                exp_quad(q, u + 1, 0)
                if exists(w):
                    act.wait_ge(f["s1_ready"], w + 1)
                    for half in range(2):
                        rows = slice(64 * half, 64 * half + 64)
                        ins = act.activation(pbd[rows, :, half, :], sd[rows, :, :], ACT.Exp, scale=SCALE_H)
                    ins.then_inc(f["p1_ready"], 1)
                copy_pT(q, u, 1)
                exp_quad(q, u + 1, 1)
                if exists(w):
                    act.wait_ge(f["pT_in_psum"], w + 1)
                    act.activation(pbT[:, :], tb[:, 0:256], ACT.Copy).then_inc(f["pT_ready"], 1)
                copy_pT(q, u, 2)
                exp_quad(q, u + 1, 2)
                if exists(w):
                    act.wait_ge(f["o1_in_psum"], w + 1)
                    act.activation(ohT[:, :], m0[:, 0:256], ACT.Copy).then_inc(f["o1_ready"], 1)
                copy_pT(q, u, 3)
                copy_xcT(q, u + 2)
                exp_quad(q, u + 1, 3)
                copy_oT(q, u)
                copy_qk(1, u + 2)
                copy_v(q, u + 2, par)
                if exists(u):
                    act.wait_ge(q["x1T_in_psum"], u + 1)
                    act.activation(hnT[:, :], m0[:, 0:256], ACT.Copy).then_inc(q["x1T_ready"], 1)
                    act.wait_ge(q["logits_ready"], u + 1)
                    act.activation(ex[:, :, :], lg[:, :, :], ACT.Exp).then_inc(f["wexp_ready"], 1)
                    act.wait_ge(f["w3T_in_psum"], u + 1)
                    act.activation(w3T[:, :], m0_bf[0:3 * E1, 0:256], ACT.Copy).then_inc(f["w3T_ready"], 1)

            units(act, body1)

        @block.vector
        def _(v):
            def by_pair(ap):
                return ap.rearrange("c (h p d) -> c p h d", h=2, p=8)

            def to_pairs(dst):
                return dst.rearrange("c (p h d) -> c p h d", p=8, h=2)

            v.wait_ge(setup["consts"], 1)
            v.wait_ge(load["attn"], 16 * 14)
            v.wait_ge(load["small"], 16 * 15)
            v.tensor_reduce(head_of[:, :], head_blk[:, :].rearrange("p (j r) -> p r j", r=4), AX_X, ALU.add)
            for k, w in enumerate((wq[0], wk[0], wv[0])):
                v.tensor_copy(to_pairs(w[:, :]), by_pair(wraw[:, k, :]))
            for k in range(4):
                v.tensor_copy(to_pairs(browp[0:1, k, :]), by_pair(brow[0:1, k, :]))
            for l in range(2):
                v.tensor_scalar(bvb[:, l, :], onesf[:, :], bvcol[:, l:l + 1], None, ALU.mult)
            v.tensor_tensor(simq[:, :], simm[:, :], simm[:, :], ALU.mult).then_inc(setup["vec_done"], 1)
            v.wait_ge(setup["tensor"], 1)
            for k, w in enumerate((wq[1], wk[1], wv[1])):
                v.tensor_copy(to_pairs(w[:, :]), by_pair(s_bank[k][:, 0:P]))
            v.tensor_copy(wo[1][:, :], s_bank[3][:, 0:P])
            for h in range(2):
                for half in range(2):
                    rows = slice(64 * half, 64 * half + 64)
                    ins = v.tensor_copy(wos[1][rows, h, :], (s_bank[3] if h == half else po)[rows, 0:P])
            ins.then_inc(setup["vec_done"], 1)
            v.wait_ge(setup["tensor"], 2)
            v.tensor_copy(simq[:, :], m1[:, 256:256 + E1]).then_inc(setup["vector"], 1)
            v.wait_ge(setup["scalar"], 2)
            step = Steps(v, setup["vec_done"], 0, 0)
            step.n = 2
            step(v.tensor_copy(bcol[:, :], m1[:, 300:304]))
            step(v.tensor_tensor(bo_b[:, :, :], m1[:, 0:256].rearrange("p (l n) -> p l n", l=2), bo_b[:, :, :], ALU.add))
            for l in range(2):
                step(v.tensor_scalar(gbo[:, l, :], bo_b[:, l, :], tg[:, l:l + 1], None, ALU.mult))
            for l in range(2):
                ins = v.tensor_scalar(head_bq[:, l, :], head_of[:, :], bcol[:, 2 * l:2 * l + 1], None, ALU.mult)
            step(ins)
            step(v.tensor_scalar(sgate[:, :], sgate[:, :], 1.0, None, ALU.add))
            step(v.reciprocal(sgate[:, :], sgate[:, :]))
            v.wait_ge(setup["consts"], 2)
            step(v.tensor_scalar(simn[:, :], simn[:, :], 1e-12, None, ALU.max))
            step(v.reciprocal(simn[:, :], simn[:, :]))
            step(v.tensor_tensor(simn[:, :], simm[:, :], simn[:, :], ALU.mult))

            def stats(sm, u, x, six, two):
                step = Steps(v, sm, u, 4)
                step.free(v.bn_stats(six[:, 0, :], x[:, 0, 0:D]))
                step(v.bn_stats(six[:, 1, :], x[:, 1, 0:D]))
                apart(v)
                for t in range(2):
                    step.free(v.bn_aggr(two[:, t, :], six[:, t, :]))
                step.end()

            def first_stats(layer, w, par):
                q = s[layer]
                if exists(w):
                    v.wait_ge(x_loaded[layer][par], (8 + 8 * layer) * (w - par + 2))
                    wait(v, q["xn_ready"], w)
                    apart(v)
                    stats(q["vec_ln"], w, xin[par], st6, mv)

            def second_stats(layer, u, x):
                q = s[layer]
                v.wait_ge(q["x_mid_ready"], u + 1)
                wait(v, q["xn2_ready"] if layer == 0 else f["nrm_ready"], u)
                apart(v)
                stats(q["vec_ln2"], u, x, st6b, mvb)

            def shift_quad(q, w, j):
                if exists(w):
                    v.wait_ge(q["scores_in_psum"], 4 * w + j + 1)
                    step = Steps(v, q["vec_max"], w * QUADS + j, 1)
                    sc = s_bank[j][:, :].rearrange("p (a k) -> p a k", k=LEN)
                    step(v.tensor_reduce(mx[:, j, :], sc, AX_X, ALU.max))
                    wait(v, q["probT_in_psum"], 4 * w - 3 + j)
                    v.scalar_tensor_tensor(out=prob[j][:, :, :, :].rearrange("p r t k -> p (r t) k"), in0=sc,
                                           scalar=MASKED, in1=bcast(mx[:, j, :], LEN, 2),
                                           op0=ALU.max, op1=ALU.subtract).then_inc(q["scores_ready"], 1)

            def normalise(q, u, half):
                if exists(u):
                    v.wait_ge(q["pv_in_psum"], 4 * u + 2 * half + 2)
                    step = Steps(v, q["vec_rden"], u * 2 + half, 1)
                    o = po[:, 0:4 * 4 * VW].rearrange("p (a t c) -> p a t c", a=4, t=4)
                    step(v.reciprocal(rden[:, :, :], o[:, :, :, VW - 1]))
                    if half == 0:
                        wait(v, q["oT_in_psum"], u)
                    for h in range(2):
                        rows = slice(64 * h, 64 * h + 64)
                        ins = v.tensor_tensor(
                            on[rows, :, 4 * half:4 * half + 4, :].rearrange("p t a d -> p a t d"),
                            o[rows, :, :, HD * h:HD * h + HD], bcast(rden[rows, :, :], HD, 3), ALU.mult)
                    ins.then_inc(q["heads_ready"], 1)

            def add_residual(layer, u, par, dst):
                q = s[layer]
                v.wait_ge(q["y_in_psum"], u + 1)
                v.wait_ge(q["residual_ready"], u + 1)
                v.scalar_tensor_tensor(out=dst, in0=m1[:, 0:256].rearrange("p (t n) -> p t n", t=2),
                                       scalar=tg[:, layer:layer + 1], in1=xb[par][:, :, :],
                                       op0=ALU.mult, op1=ALU.add).then_inc(q["x_mid_ready"], 1)

            ROUTER, RANK = 5, 6

            def router_logits(w):
                if exists(w):
                    v.wait_ge(s[0]["logits_in_psum"], w + 1)
                    step = Steps(v, route["router_steps"], w, ROUTER)
                    step(v.tensor_tensor(lg[:, :, 0:E0], m1[:, 0:2 * E0].rearrange("p (t e) -> p t e", t=2),
                                         bcast(brb[:, :], 2, 1), ALU.add))
                    apart(v)
                    for t in range(2):
                        step.free(v.max(top[:, t, :], lg[:, t, 0:E0]))

            def router_choice(w):
                if exists(w):
                    v.wait_ge(route["router_steps"], ROUTER * w + 3)
                    apart(v)
                    for t in range(2):
                        ins = v.max_index(topi[:, t, :], top[:, t, :], lg[:, t, 0:E0])
                        ins.then_inc(route["router_steps"], 1)

            def router_onehot(w):
                if exists(w):
                    v.wait_ge(route["router_steps"], ROUTER * w + ROUTER)
                    v.tensor_tensor(onehot[:, :, :], iota[:, :, 0:E0], topi[:, :, 0:1].broadcast_to([P, 2, E0]),
                                    ALU.is_equal).then_inc(route["onehot_ready"], 1)
                    v.tensor_tensor(lg[:, :, 0:E0], lg[:, :, 0:E0], top[:, :, 0:1].broadcast_to([P, 2, E0]),
                                    ALU.subtract).then_inc(s[0]["logits_ready"], 1)
                    v.wait_ge(route["onehot_ready"], 2 * w + 1)
                    v.tensor_tensor(seen[:, 1, :], seen[:, 0, :], onehot[:, 0, :], ALU.add)\
                        .then_inc(route["onehot_ready"], 1)

            def router_rank(w):
                if exists(w):
                    v.wait_ge(route["rank_in_psum"], w + 1)
                    v.wait_ge(s[0]["exp8_ready"], w + 1)
                    step = Steps(v, route["rank_steps"], w, RANK)
                    step.free(v.tensor_tensor(seen[:, 0, :], seen[:, 1, :], onehot[:, 1, :], ALU.add))
                    step.free(v.tensor_tensor(rank[:, :, :], m1[:, 0:2 * E0].rearrange("p (t e) -> p t e", t=2),
                                              bcast(region0[:, :], 2, 1), ALU.add))
                    step(v.tensor_reduce(den[:, :], ex[:, :, 0:E0], AX_X, ALU.add))
                    step.free(v.tensor_tensor(rsel[:, :, :], rank[:, :, :], onehot[:, :, :], ALU.mult))
                    step(v.reciprocal(gate[:, :], den[:, :]))
                    step.free(v.tensor_reduce(posf[:, :], rsel[:, :, :], AX_X, ALU.add))
                    step.end()

            def router_place(w, par):
                if exists(w):
                    v.tensor_scalar(xr[par][:, :, 2 * D], gate[:, :], tg[:, 2:3], None, ALU.mult)
                    v.wait_ge(route["rank_steps"], RANK * w + RANK)
                    v.tensor_copy(place[:, bass.ds(w, 1), :], posf[:, :].unsqueeze(1))
                    v.tensor_copy(posi[par][:, :], posf[:, :]).then_inc(route["pos_ready"], 1)

            def body0(u, par):
                q = s[0]
                shift_quad(q, u + 1, 0)
                first_stats(0, u + 2, par)
                shift_quad(q, u + 1, 1)
                router_logits(u - 1)
                shift_quad(q, u + 1, 2)
                router_choice(u - 1)
                normalise(q, u, 0)
                router_onehot(u - 1)
                shift_quad(q, u + 1, 3)
                normalise(q, u, 1)
                router_rank(u - 1)
                router_place(u - 1, 1 - par)
                if exists(u):
                    wait(v, scattered[par], 16 * (u - par))
                    add_residual(0, u, par, xr[par][:, :, 0:D])
                    second_stats(0, u, xr[par])

            units(v, body0)

            v.wait_ge(routed["count_in_psum"], 1)
            step = Steps(v, routed["vector"], 0, 0)
            step(v.tensor_copy(count[:, :], m1[:, 0:E0]))
            step(v.tensor_tensor(padf[:, 0:E0], count[:, :], region0[:, :], ALU.add))
            step(v.tensor_scalar(padf[:, 0:E0], padf[:, 0:E0], m1[:, 64:65], None, ALU.add))
            for k in range(E0 + 2):
                step.free(v.tensor_scalar(padi[:, E0 + k:E0 + k + 1], padf[:, E0 - 1:E0], float(P * (k + 1)), None,
                                          ALU.add))
            v.wait_ge(routed["vector"], step.n)
            v.tensor_copy(padi[:, 0:E0], padf[:, 0:E0]).then_inc(routed["zero"], 1)
            step(v.tensor_scalar(tilesi[:, :], count[:, :], P / 2 - 0.5, 1.0 / P, ALU.add, ALU.mult))
            step(v.tensor_copy(tiles[:, :], tilesi[:, :]))
            step(v.tensor_copy(tend[:, 0:1], tiles[0:1, 0:1]))
            for e in range(1, E0):
                step(v.tensor_tensor(tend[:, e:e + 1], tend[:, e - 1:e], tiles[0:1, e:e + 1], ALU.add))
            step(v.tensor_tensor(full[:, :, :], bcast(tend[:, 0:E0 - 1], SLOTS, 1), bcast(slot_no[:, :], E0 - 1, 2),
                                 ALU.is_le))
            step(v.tensor_reduce(slotf[:, 0, :], full[:, :, :], AX_X, ALU.add))
            step(v.tensor_tensor(fullt[:, :, :], full[:, :, :], bcast(tend[:, 0:E0 - 1], SLOTS, 1), ALU.mult))
            step(v.tensor_reduce(slotf[:, 1, :], fullt[:, :, :], AX_X, ALU.max))
            step(v.tensor_tensor(slotf[:, 2, :], slot_no[:, :], slotf[:, 1, :], ALU.subtract))
            step(v.tensor_scalar(slotf[:, 3, :], slotf[:, 2, :], float(P), None, ALU.mult))
            step(v.scalar_tensor_tensor(out=slotf[:, 4, :], in0=slotf[:, 0, :], scalar=float(REGION),
                                        in1=slotf[:, 3, :], op0=ALU.mult, op1=ALU.add))
            v.tensor_copy(slot_e[:, :], slotf[:, 0, :]).then_inc(routed["table"], 1)
            v.tensor_copy(slot_row[:, :], slotf[:, 4, :]).then_inc(routed["table"], 1)
            v.wait_ge(routed["table"], 2)
            v.wait_ge(load["moe"], 16 * 4)

            def expert_of(sl):
                return v.value_load(slot_e[0:1, bass.ds(sl, 1)], min_val=0, max_val=E0 - 1)

            def slot(sl, n, par, rnd):
                if slot_exists(sl + 2):
                    e = expert_of(sl + 2)
                    v.wait_ge(b["h_in_psum"], sl + 3)
                    wait(v, b["hT_in_psum"], sl + 1)
                    v.tensor_tensor(hb[par][:, :], s_bank[par][:, :], b1b[:, bass.ds(e * F0, F0)], ALU.add)\
                        .then_inc(b["h_ready"], 1)
                if slot_exists(sl):
                    e = expert_of(sl)
                    v.wait_ge(b["y_in_psum"], sl + 1)
                    step = Steps(v, b["vec_y"], sl, 1)
                    step(v.tensor_tensor(yb[par][:, :], po[:, 0:D], b2b[:, bass.ds(e * D, D)], ALU.add))
                    wait(v, stored[par], 8 * (sl - par))
                    v.scalar_tensor_tensor(out=yo[par][:, :], in0=yb[par][:, :], scalar=xs[n][:, 2 * D:2 * D + 1],
                                           in1=xs[n][:, 0:D], op0=ALU.mult, op1=ALU.add).then_inc(b["y_ready"], 1)

            slots(v, slot)

            step(v.tensor_scalar(move[:, :], tiles[:, 0:E0 - 1], float(P), -float(REGION), ALU.mult, ALU.add))
            src = place
            for e in range(1, E0):
                step(v.tensor_scalar(beyond[:, :, :], place[:, :, :], float(e * REGION), move[:, e - 1:e],
                                     ALU.is_ge, ALU.mult))
                step(v.tensor_tensor(placed[:, :, :], src[:, :, :], beyond[:, :, :], ALU.add))
                src = placed
            v.tensor_copy(placei[:, :, :], placed[:, :, :]).then_inc(routed["table"], 1)

            GATE = 21

            def gate_norm(u, step):
                v.wait_ge(f["nrm_ready"], u + 1)
                step(v.tensor_scalar(rnrm[:, :], nrm[:, :], 1e-12, None, ALU.max))
                step.free(v.reciprocal(rnrm[:, :], rnrm[:, :]))

            def gate_logits(u, step):
                v.wait_ge(s[1]["logits_in_psum"], u + 1)
                step.wait()
                for t in range(2):
                    ins = v.scalar_tensor_tensor(out=lg[:, t, :], in0=po[:, E1 * t:E1 * t + E1],
                                                 scalar=rnrm[:, t:t + 1], in1=sgate[:, :],
                                                 op0=ALU.mult, op1=ALU.subtract)
                ins.then_inc(f["gate_logits"], 1)

            def gate_top(u, step):
                v.wait_ge(f["gate_logits"], u + 1)
                apart(v)
                for t in range(2):
                    step.free(v.max(top[:, t, :], lg[:, t, :]))
                step.free(v.tensor_scalar(gm[:, :, :], lg[:, :, :], 0.0, None, ALU.is_gt))

            def gate_index(step):
                step.wait()
                apart(v)
                for t in range(2):
                    step.free(v.max_index(topi[:, t, :], top[:, t, :], lg[:, t, :]))
                step.free(v.tensor_scalar(idle[:, :], top[:, :, 0], 0.0, None, ALU.is_le))
                step.free(v.tensor_scalar(gtop[:, :], top[:, :, 0], 0.0, None, ALU.max))

            def gate_shift(step):
                step.wait()
                v.scalar_tensor_tensor(out=lg[:, :, :], in0=lg[:, :, :], scalar=0.0, in1=bcast(gtop[:, :], E1, 2),
                                       op0=ALU.max, op1=ALU.subtract).then_inc(s[1]["logits_ready"], 1)
                for k in range(2):
                    step.free(v.tensor_tensor(fb[:, k, :, :], iota[:, :, :],
                                              topi[:, :, k:k + 1].broadcast_to([P, 2, E1]), ALU.is_equal))

            def gate_mask(step):
                step.wait()
                step(v.tensor_tensor(fb[:, 0, :, :], fb[:, 0, :, :], fb[:, 1, :, :], ALU.add))
                step(v.tensor_tensor(fb[:, 0, :, :], fb[:, 0, :, :], bcast(idle[:, :], E1, 2), ALU.mult))
                step.free(v.tensor_tensor(gm[:, :, :], gm[:, :, :], fb[:, 0, :, :], ALU.add))

            def gate_softmax(u, step):
                v.wait_ge(f["wexp_ready"], u + 1)
                step.wait()
                step(v.tensor_tensor(wg[:, :, :], ex[:, :, :], gm[:, :, :], ALU.mult))
                step(v.tensor_reduce(den[:, :], wg[:, :, :], AX_X, ALU.add))
                step(v.reciprocal(gate[:, :], den[:, :]))
                step.free(v.tensor_tensor(wg[:, :, :], wg[:, :, :], bcast(gate[:, :], E1, 2), ALU.mult))

            def gate_terms(step):
                step.wait()
                step(v.tensor_copy(w3[:, :, 0, :], wg[:, :, :]))
                step(v.tensor_tensor(wres[:, :, :], wg[:, :, :], w3[:, :, 0, :], ALU.subtract))
                step(v.tensor_copy(w3[:, :, 1, :], wres[:, :, :]))
                step.end()
                v.tensor_tensor(w3[:, :, 2, :], wres[:, :, :], w3[:, :, 1, :], ALU.subtract)\
                    .then_inc(f["w3_ready"], 1)

            def body1(u, par):
                q = s[1]
                w = u - 1
                if exists(w):
                    v.wait_ge(z_used, 16 * w + 8)
                    v.tensor_copy(qkT[:, :, :], m1[:, :].rearrange("p (a n) -> p a n", a=2))\
                        .then_inc(f["qk1_ready"], 1)
                shift_quad(q, u + 1, 0)
                first_stats(1, u + 2, par)
                if exists(w):
                    v.wait_ge(f["s1_in_psum"], w + 1)
                    sc = m1[:, 0:2 * LEN].rearrange("p (t k) -> p t k", t=2)
                    step = Steps(v, f["vec_s1"], w, 1)
                    step(v.tensor_reduce(smx[:, :], sc, AX_X, ALU.max))
                    v.tensor_tensor(sd[:, :, :], sc, bcast(smx[:, :], LEN, 2), ALU.subtract)\
                        .then_inc(f["s1_ready"], 1)
                shift_quad(q, u + 1, 1)
                if exists(w):
                    v.wait_ge(f["p1_ready"], w + 1)
                    pb = pbd[:, :, :, :].rearrange("p t h k -> p t (h k)")
                    step = Steps(v, f["vec_p1"], w, 2)
                    step(v.tensor_reduce(srs[:, :], pb, AX_X, ALU.add))
                    step(v.reciprocal(srs[:, :], srs[:, :]))
                    v.tensor_tensor(pb, pb, bcast(srs[:, :], P, 2), ALU.mult).then_inc(f["pn_ready"], 1)
                shift_quad(q, u + 1, 2)
                normalise(q, u, 0)
                shift_quad(q, u + 1, 3)
                normalise(q, u, 1)
                if exists(u):
                    add_residual(1, u, par, x3[par][:, :, :])
                    second_stats(1, u, x3[par])

                def weigh(src, batch, k):
                    v.wait_ge(ring_filled, batch * 8 + k + 1)
                    wait(v, z_used, (batch - 1) * 8 + k + 1)
                    v.tensor_tensor(z[:, 2 * k:2 * k + 2, :],
                                    s_bank[k % QUADS][:, :].rearrange("p (e n) -> p e n", e=2),
                                    bcast(src, 2, 1), ALU.mult).then_inc(ring_used, 1)

                if exists(w):
                    v.wait_ge(f["o1_ready"], w + 1)
                gates = Steps(v, f["gate_steps"], u, GATE)
                for k in range(E1 // 2):
                    if exists(w):
                        weigh(ohT[:, :], 1 + 2 * w, k)
                    if exists(u):
                        if k == 1:
                            gate_norm(u, gates)
                        if k == 2:
                            gate_logits(u, gates)
                        if k == 3:
                            gate_top(u, gates)
                        if k == 4:
                            gate_index(gates)
                        if k == 5:
                            gate_shift(gates)
                        if k == 6:
                            gate_mask(gates)
                        if k == 7:
                            gate_softmax(u, gates)
                            gate_terms(gates)
                if exists(w):
                    v.wait_ge(z_used, 16 * w + 16)
                    wait(v, out_sem[1 - par], 8 * (w - 1 + par))
                    v.scalar_tensor_tensor(out=res[1 - par][:, :, :],
                                           in0=m1[:, 0:256].rearrange("p (t n) -> p t n", t=2),
                                           scalar=tg[:, 3:4], in1=x3[1 - par][:, :, :],
                                           op0=ALU.mult, op1=ALU.add).then_inc(f["res_ready"], 1)
                if exists(u):
                    v.wait_ge(q["x1T_ready"], u + 1)
                    for k in range(E1 // 2):
                        weigh(hnT[:, :], 2 * u, k)

            units(v, body1)

        @block.tensor
        def _(pe):
            pe.wait_ge(setup["consts"], 1)
            pe.wait_ge(load["attn"], 16 * 14)
            pe.wait_ge(load["small"], 16 * 15)
            for k in range(4):
                pe.transpose(s_bank[k][:, 0:P], wraw[:, 3 + k, :], ident[:, :])
            pe.transpose(po[:, 0:P], wraw[:, 7, :], ident[:, :]).then_inc(setup["tensor"], 1)
            pe.wait_ge(setup["vec_done"], 2)
            for l in range(2):
                pe.matmul(m1[:, P * l:P * l + P], bvb[:, l, :], wo[l][:, :], start=True, stop=True)
            for k in range(4):
                pe.matmul(m1[:, 300 + k:301 + k], browp[0:1, k, :], onesf[0:1, 0:1], start=True, stop=True)
            pe.matmul(m1[:, 256:256 + E1], onesf[:, :], simq[:, :], start=True, stop=True)\
                .then_inc(setup["tensor"], 1)
            pe.wait_ge(setup["vec_done"], 12)

            def m0_is_free(layer, v):
                if isinstance(v, int) and v <= 2:
                    wait(pe, s[layer]["v_ready"], v)
                elif layer == 0:
                    pe.wait_ge(s[0]["x1T_ready"], v - 2)
                else:
                    pe.wait_ge(f["o1_ready"], v - 2)

            def transpose_in(layer, v, par):
                q = s[layer]
                if exists(v):
                    m0_is_free(layer, v)
                    pe.wait_ge(ctx_loaded[layer][par], 8 * (v - par + 2))
                    pe.wait_ge(q["xn_ready"], v + 1)
                    for t in range(2):
                        pe.transpose(m0[:, P * t:P * t + P], xn[:, t, :], ident[:, :])
                    for t in range(2):
                        ins = pe.transpose(m0[:, P * (2 + t):P * (3 + t)], cin[par][:, t, :], ident[:, :])
                    ins.then_inc(q["xc_in_psum"], 1)

            def queries_keys(layer, v):
                q = s[layer]
                if exists(v):
                    if isinstance(v, int) and v <= 2:
                        wait(pe, q["qk_ready"], v)
                    elif layer == 0:
                        pe.wait_ge(route["rank_steps"], 6 * (v - 2))
                    else:
                        pe.wait_ge(f["s1_ready"], v - 2)
                    pe.wait_ge(q["xcT_ready"], v + 1)
                    pe.matmul(m1[:, 0:256], wq[layer][:, :], xcT[:, 0:2, :], start=True, stop=True)
                    pe.matmul(m1[:, 256:512], wk[layer][:, :], xcT[:, 2:4, :], start=True, stop=True)\
                        .then_inc(q["qk_in_psum"], 1)

            def values(layer, v):
                q = s[layer]
                if exists(v):
                    if exists(v - 2):
                        pe.wait_ge(q["oT_ready"], v - 1)
                    for t in range(2):
                        ins = pe.matmul(m0[:, P * t:P * t + P], xcT[:, 2 + t, :], wv[layer][:, :],
                                        start=True, stop=True)
                    ins.then_inc(q["v_in_psum"], 1)

            def scores(layer, v, par, j):
                q = s[layer]
                if exists(v):
                    if j == 0:
                        pe.wait_ge(q["qk_ready"], v + 1)
                        if layer == 1:
                            pe.wait_ge(q["pad_row_ready"], v + 1)
                            wait(pe, ring_used, 16 * v - 24)
                    wait(pe, q["scores_ready"], 4 * v - 3 + j)
                    if layer == 0:
                        mask, rows = mask_chunk, LEN
                    else:
                        mask, rows = mask_causal[par], LEN + 1
                    pe.matmul(s_bank[j][:, :], mask_rows[0:rows, :, :], mask[0:rows, :, :], start=True, stop=False,
                              skip_group_check=True)
                    quad = slice(32 * j, 32 * j + 32)
                    for r in range(2):
                        for t in range(4):
                            seq = slice(LEN * t, LEN * t + LEN)
                            col = LEN * (4 * r + t)
                            ins = pe.matmul(s_bank[j][:, col:col + LEN], qx[quad, t, 2 * r:2 * r + 2, :],
                                            kT[quad, seq], start=False, stop=True, skip_group_check=True)
                    ins.then_inc(q["scores_in_psum"], 1)

            def transpose_probs(q, u, j):
                if exists(u):
                    pe.wait_ge(q["exp_ready"], 4 * u + j + 1)
                    wait(pe, q["probT_ready"], 4 * u + j)
                    for r in range(2):
                        for t in range(2):
                            col = P * (2 * r + t)
                            ins = pe.transpose(tb[:, col:col + P], prob[j][:, r, 2 * t:2 * t + 2, :], ident[:, :])
                    ins.then_inc(q["probT_in_psum"], 1)

            def weigh_values(q, u, par, j):
                if exists(u):
                    pe.wait_ge(q["probT_ready"], 4 * u + j + 1)
                    if j == 0:
                        pe.wait_ge(q["v_ready"], u + 1)
                        if q is s[1]:
                            wait(pe, f["gate_logits"], u)
                    if j % 2 == 0:
                        wait(pe, q["heads_ready"], 2 * u + j // 2)
                    for r in range(2):
                        for t in range(2):
                            col = 2 * VW * (2 * (2 * (j % 2) + r) + t)
                            ins = pe.matmul(po[:, col:col + 2 * VW], pT[j % 2][:, r, t, :],
                                            vb[par][:, t, 2 * j + r, :, :], start=True, stop=True,
                                            skip_group_check=True)
                    ins.then_inc(q["pv_in_psum"], 1)

            def transpose_heads(layer, u):
                q = s[layer]
                if exists(u):
                    if exists(u + 2):
                        pe.wait_ge(q["xcT_ready"], u + 3)
                    elif layer == 0:
                        pe.wait_ge(q["x1T_ready"], u)
                    else:
                        pe.wait_ge(f["o1_ready"], u)
                    pe.wait_ge(q["heads_ready"], 2 * u + 2)
                    for t in range(2):
                        ins = pe.transpose(m0[:, P * t:P * t + P], on[:, 2 * t:2 * t + 2, :, :], ident[:, :])
                    ins.then_inc(q["oT_in_psum"], 1)

            def output(layer, u):
                q = s[layer]
                if exists(u):
                    pe.wait_ge(q["oT_ready"], u + 1)
                    if exists(u + 2):
                        pe.wait_ge(q["qk_ready"], u + 3)
                    elif layer == 0:
                        pe.wait_ge(route["rank_steps"], 6 * u)
                    else:
                        pe.wait_ge(f["s1_ready"], u)
                    for t in range(2):
                        for h in range(2):
                            ins = pe.matmul(m1[:, P * t:P * t + P], oT[:, t, h, :, :], wos[layer][:, h, :],
                                            start=(h == 0), stop=(h == 1))
                    ins.then_inc(q["y_in_psum"], 1)

            def normed_transpose(layer, w, src):
                q = s[layer]
                pe.wait_ge(q["oT_ready"], w + 1)
                if exists(w + 2):
                    pe.wait_ge(q["v_ready"], w + 3)
                pe.wait_ge(q["xn2_ready"], w + 1)
                for t in range(2):
                    ins = pe.transpose(m0[:, P * t:P * t + P], src(t), ident[:, :])
                ins.then_inc(q["x1T_in_psum"], 1)

            def body0(u, par):
                q = s[0]
                w = u - 1
                scores(0, u + 1, 1 - par, 0)
                transpose_probs(q, u, 0)
                if exists(w):
                    normed_transpose(0, w, lambda t: xr[1 - par][:, t, D:2 * D])
                scores(0, u + 1, 1 - par, 1)
                transpose_probs(q, u, 1)
                weigh_values(q, u, par, 0)
                if exists(w):
                    pe.wait_ge(q["x1T_ready"], w + 1)
                    pe.wait_ge(q["x_mid_ready"], w + 1)
                    for t in range(2):
                        ins = pe.matmul(m1[:, E0 * t:E0 * t + E0], x1T[:, t, :], wr[:, :], start=True, stop=True)
                    ins.then_inc(q["logits_in_psum"], 1)
                scores(0, u + 1, 1 - par, 2)
                transpose_probs(q, u, 2)
                weigh_values(q, u, par, 1)
                scores(0, u + 1, 1 - par, 3)
                transpose_probs(q, u, 3)
                weigh_values(q, u, par, 2)
                transpose_in(0, u + 2, par)
                if exists(w):
                    pe.wait_ge(route["onehot_ready"], 2 * w + 2)
                    for t in range(2):
                        pe.matmul(m1[:, E0 * t:E0 * t + E0], earlier[:, :], onehot[:, t, :], start=True, stop=False)
                        ins = pe.matmul(m1[:, E0 * t:E0 * t + E0], onesb[:, :], seen[:, t, :], start=False, stop=True)
                    ins.then_inc(route["rank_in_psum"], 1)
                weigh_values(q, u, par, 3)
                queries_keys(0, u + 2)
                transpose_heads(0, u)
                values(0, u + 2)
                output(0, u)

            units(pe, body0)

            pe.wait_ge(route["pos_ready"], UNITS)
            pe.matmul(m1[:, 0:E0], onesb[:, :], seen[:, 0, :], start=True, stop=True)
            pe.matmul(m1[:, 64:65], earlier[:, :], onesb[:, 0:1], start=True, stop=True)\
                .then_inc(routed["count_in_psum"], 1)
            pe.wait_ge(routed["table"], 2)
            pe.wait_ge(load["moe"], 16 * 4)

            def expert_of(sl):
                return pe.value_load(slot_e[0:1, bass.ds(sl, 1)], min_val=0, max_val=E0 - 1)

            def slot(sl, n, par, rnd):
                if slot_exists(sl):
                    wait(pe, b["hT_ready"], sl)
                    pe.wait_ge(b["gelu_ready"], sl + 1)
                    for j in range(FJ):
                        ins = pe.transpose(tb[:, P * j:P * j + P], hb[par][:, P * j:P * j + P], ident[:, :])
                    ins.then_inc(b["hT_in_psum"], 1)
                if slot_exists(sl + 2):
                    e = expert_of(sl + 2)
                    wait(pe, b["h_ready"], sl + 1)
                    pe.wait_ge(b["xT_ready"], sl + 3)
                    pe.matmul(s_bank[par][:, :], xsT[par][:, :], w1[:, bass.ds(e * F0, F0)], start=True, stop=True)\
                        .then_inc(b["h_in_psum"], 1)
                if slot_exists(sl + 3):
                    nx = (n + 3) % RING0
                    pe.wait_ge(slot_loaded[nx], 16 * (rnd + (n + 3) // RING0 + 1))
                    pe.transpose(m0[:, 0:P], xs[nx][:, D:2 * D], ident[:, :]).then_inc(b["xT_in_psum"], 1)
                if slot_exists(sl):
                    e = expert_of(sl)
                    wait(pe, b["vec_y"], sl)
                    pe.wait_ge(b["hT_ready"], sl + 1)
                    for j in range(FJ):
                        ins = pe.matmul(po[:, 0:D], hT[par][:, P * j:P * j + P],
                                        w2[:, bass.ds((e * FJ + j) * D, D)], start=(j == 0), stop=(j == FJ - 1))
                    ins.then_inc(b["y_in_psum"], 1)

            slots(pe, slot)
            pe.wait_ge(load["experts1"], 16 * 4)
            pe.wait_ge(b["y_ready"], SLOTS)

            def spread(batch, k):
                wait(pe, ring_used, batch * 8 + k - QUADS + 1)
                for e in range(2):
                    ins = pe.matmul(s_bank[k % QUADS][:, 256 * e:256 * e + 256], term_sel[:, 2 * k + e, :],
                                    w3T[:, :], start=True, stop=True)
                ins.then_inc(ring_filled, 1)

            def body1(u, par):
                q = s[1]
                w = u - 1
                scores(1, u + 1, 1 - par, 0)
                transpose_probs(q, u, 0)
                if exists(w):
                    pe.wait_ge(f["qk1_ready"], w + 1)
                    apart(pe)
                    for t in range(2):
                        for half in range(2):
                            seq = slice(LEN * (2 * t + half), LEN * (2 * t + half) + LEN)
                            ins = pe.matmul(m1[64 * half:64 * half + 64, LEN * t:LEN * t + LEN], qkT[:, 0, seq],
                                            qkT[:, 1, seq], start=True, stop=True, skip_group_check=True)
                    ins.then_inc(f["s1_in_psum"], 1)
                scores(1, u + 1, 1 - par, 1)
                transpose_probs(q, u, 1)
                weigh_values(q, u, par, 0)
                scores(1, u + 1, 1 - par, 2)
                if exists(w):
                    if exists(u):
                        pe.wait_ge(q["probT_ready"], 4 * u + 2)
                    pe.wait_ge(f["pn_ready"], w + 1)
                    for t in range(2):
                        ins = pe.transpose(tb[:, P * t:P * t + P], pbd[:, t, :, :], ident[:, :])
                    ins.then_inc(f["pT_in_psum"], 1)
                    if exists(u):
                        pe.wait_ge(f["pT_ready"], w + 1)
                transpose_probs(q, u, 2)
                weigh_values(q, u, par, 1)
                if exists(w):
                    pe.wait_ge(f["v1_ready"], w + 1)
                    pe.wait_ge(f["pT_ready"], w + 1)
                    for t in range(2):
                        ins = pe.matmul(m0[:, P * t:P * t + P], vh[:, t, :], pbT[:, P * t:P * t + P],
                                        start=True, stop=True)
                    ins.then_inc(f["o1_in_psum"], 1)
                scores(1, u + 1, 1 - par, 3)
                transpose_probs(q, u, 3)
                weigh_values(q, u, par, 2)
                transpose_in(1, u + 2, par)
                weigh_values(q, u, par, 3)
                queries_keys(1, u + 2)
                transpose_heads(1, u)
                values(1, u + 2)
                output(1, u)

                if exists(w):
                    if exists(u + 1):
                        pe.wait_ge(q["scores_ready"], 4 * u + 8)
                    if exists(u):
                        pe.wait_ge(q["x_mid_ready"], u + 1)
                    for k in range(QUADS - 1):
                        spread(1 + 2 * w, k)
                for k in range(E1 // 2):
                    if exists(w):
                        if k + QUADS - 1 < E1 // 2:
                            spread(1 + 2 * w, k + QUADS - 1)
                        pe.wait_ge(ring_used, (1 + 2 * w) * 8 + k + 1)
                        for e in range(2 * k, 2 * k + 2):
                            for t in range(2):
                                ins = pe.matmul(m1[:, P * t:P * t + P], z[:, e, P * t:P * t + P], proj[:, 3, e, :],
                                                start=(e == 0 and t == 0), stop=(e == E1 - 1),
                                                skip_group_check=True)
                        ins.then_inc(z_used, 1)
                    if exists(u) and k == 1:
                        normed_transpose(1, u, lambda t: hn[:, t, :])
                    if exists(u) and k == 2:
                        pe.wait_ge(q["x1T_ready"], u + 1)
                        pe.wait_ge(q["heads_ready"], 2 * u + 2)
                        for t in range(2):
                            ins = pe.matmul(po[:, E1 * t:E1 * t + E1], hnT[:, P * t:P * t + P], simn[:, :],
                                            start=True, stop=True)
                        ins.then_inc(q["logits_in_psum"], 1)
                if exists(u):
                    pe.wait_ge(f["w3_ready"], u + 1)
                    apart(pe)
                    for t in range(2):
                        ins = pe.transpose(m0_bf[0:3 * E1, P * t:P * t + P], w3[:, t, :, :], identb[:, :])
                    ins.then_inc(f["w3T_in_psum"], 1)
                    pe.wait_ge(f["w3T_ready"], u + 1)
                    for k in range(QUADS - 1):
                        spread(2 * u, k)
                    for k in range(E1 // 2):
                        if k + QUADS - 1 < E1 // 2:
                            spread(2 * u, k + QUADS - 1)
                        if k == 0 and exists(w):
                            pe.wait_ge(f["res_ready"], w + 1)
                        pe.wait_ge(ring_used, 2 * u * 8 + k + 1)
                        for e in range(2 * k, 2 * k + 2):
                            first, last = e == 0, e == E1 - 1
                            for c in range(2):
                                pe.matmul(m1[:, 256 * c:256 * c + 256], proj[:, c, e, :], z[:, e, :],
                                          start=(first and c == 0), stop=last, skip_group_check=True)
                            for t in range(2):
                                ins = pe.matmul(m0[:, P * t:P * t + P], z[:, e, P * t:P * t + P], proj[:, 2, e, :],
                                                start=(first and t == 0), stop=last, skip_group_check=True)
                        ins.then_inc(z_used, 1)

            units(pe, body1)


def kernel(**inputs):
    import numpy as _np
    import concourse.bacc as _bacc
    from concourse import mybir as _mybir
    from concourse.bass_utils import run_bass_kernel_spmd as _run

    nc = _bacc.Bacc("TRN2", target_bir_lowering=False, num_devices=1)
    arrays, args = {}, {}
    for name in inputs:
        x = _np.ascontiguousarray(inputs[name])
        if name in ("x", "ctx_1024"):
            x = x.reshape(-1, x.shape[-1])
        arrays[f"in_{name}"] = x
        args[name] = nc.dram_tensor(f"in_{name}", x.shape, _mybir.dt.from_np(x.dtype), kind="ExternalInput").ap()
    shape = _np.shape(inputs["x"])
    out = nc.dram_tensor("out_x", (shape[0] * shape[1], shape[2]), _mybir.dt.float32, kind="ExternalOutput").ap()
    flamingo(nc, args, out)
    r = _run(nc, [arrays], core_ids=[0])
    return r.results[0]["out_x"].reshape(shape)
```

```python
from contextlib import ExitStack

import numpy as np
import concourse.bass as bass
from concourse import mybir

ALU = mybir.AluOpType
ACT = mybir.ActivationFunctionType
AX_X = mybir.AxisListType.X
F32 = mybir.dt.float32
BF16 = mybir.dt.bfloat16
I32 = mybir.dt.int32
U32 = mybir.dt.uint32
U8 = mybir.dt.uint8

P = 128
SEQS, LEN, D = 128, 64, 128
N = SEQS * LEN
HEADS, HD = 16, 8
UNIT = 256
UNITS = N // UNIT
QUADS = 4
E0, F0 = 8, 512
E1 = 16
FJ = F0 // P
RING0 = 6
SLOTS = N // P + E0
REGION = N + (E0 + 2) * P
ROWW = 2 * D + 1
CHUNK = 32
MASKED = -(2.0 ** 126)
EPS = 1e-5
SCALE = float(np.float32(1.0) / np.sqrt(np.float32(HD)))
SCALE_H = float(1.0 / np.sqrt(np.float32(D)))
VW = HD + 1


class Steps:

    def __init__(self, eng, sem, unit, per_unit):
        self.eng, self.sem, self.unit, self.per_unit, self.n = eng, sem, unit, per_unit, 0

    def free(self, ins):
        self.n += 1
        ins.then_inc(self.sem, 1)

    def wait(self):
        self.eng.wait_ge(self.sem, self.unit * self.per_unit + self.n)

    def __call__(self, ins):
        self.free(ins)
        self.wait()

    def end(self):
        assert self.n == self.per_unit, (self.n, self.per_unit)


def bcast(ap, n, at):
    return ap.unsqueeze(at).broadcast_to(list(ap.shape[:at]) + [n] + list(ap.shape[at:]))


def flamingo(nc, a, out):
    ctx = ExitStack()
    with ctx:
        ctx.enter_context(nc.allow_non_contiguous_dma("small constant loads"))

        def sb(name, shape, dt=F32):
            return ctx.enter_context(nc.sbuf_tensor(name, shape, dt))

        def bank(name):
            return ctx.enter_context(nc.psum_tensor(name, [P, 512], F32))

        def sem(name):
            return ctx.enter_context(nc.semaphore(name))

        sorted_in = nc.dram_tensor("sorted_in", (E0 * REGION, ROWW), F32, kind="Internal").ap()
        sorted_out = nc.dram_tensor("sorted_out", (SLOTS * P, D), F32, kind="Internal").ap()

        ident = sb("ident", [P, P])
        identb = sb("identb", [P, P], BF16)
        onesf = sb("onesf", [P, P])
        onesb = sb("onesb", [P, P], BF16)
        earlier = sb("earlier", [P, P], BF16)
        mask_rows = sb("mask_rows", [LEN + 2, 2, LEN], BF16)
        mask_chunk = sb("mask_chunk", [LEN, 8, LEN], BF16)
        mask_causal = [sb(f"mask_causal{b}", [LEN + 2, 8, LEN], BF16) for b in range(2)]
        head_blk = sb("head_blk", [P, HEADS])
        head_of = sb("head_of", [P, 4])
        term_sel = sb("term_sel", [3 * E1, E1, P], BF16)
        iota = sb("iota", [P, 2, E1])
        region0 = sb("region0", [P, E0])
        slot_no = sb("slot_no", [1, SLOTS])
        half_neg = sb("half_neg", [P, 2])
        eps = sb("eps", [P, 2])
        masked = sb("masked", [LEN + 2, LEN])
        half_pos = sb("half_pos", [P, E1])
        pad_u8 = sb("pad_u8", [LEN + 2, 2 * UNITS, LEN], U8)
        pad_unit = sb("pad_unit", [LEN + 2, 2, LEN])
        wraw = sb("wraw", [P, 4, P])
        wq = [sb(f"wq{l}", [P, P]) for l in range(2)]
        wk = [sb(f"wk{l}", [P, P]) for l in range(2)]
        wv = [sb(f"wv{l}", [P, P]) for l in range(2)]
        wo = [sb(f"wo{l}", [P, P]) for l in range(2)]
        bcol = sb("bcol", [P, 4])
        bvcol = sb("bvcol", [P, 2])
        bvb = sb("bvb", [P, 2, P])
        bo_b = sb("bo_b", [P, 2, P])
        gbo = sb("gbo", [P, 2, P])
        graw = sb("graw", [P, 4])
        tg = sb("tg", [P, 4])
        w1 = sb("w1", [P, E0 * F0])
        w2 = sb("w2", [P, E0 * FJ * D])
        b1b = sb("b1b", [P, E0 * F0])
        b2b = sb("b2b", [P, E0 * D])
        wr = sb("wr", [P, E0])
        brb = sb("brb", [P, E0])
        proj = sb("proj", [P, 4, E1, D])
        simm = sb("simm", [P, E1])
        simq = sb("simq", [P, E1])
        simn = sb("simn", [P, E1])
        sgate = sb("sgate", [P, E1])

        xin = [sb(f"xin{b}", [P, 2, D]) for b in range(2)]
        cin = [sb(f"cin{b}", [P, 2, D]) for b in range(2)]
        st6 = sb("st6", [P, 2, 6])
        mv = sb("mv", [P, 2, 2])
        rstd = sb("rstd", [P, 2])
        vare = sb("vare", [P, 2])
        xn = sb("xn", [P, 2, D])
        xb = [sb(f"xb{b}", [P, 2, D]) for b in range(2)]
        xT = sb("xT", [P, UNIT])
        cT = sb("cT", [P, 4, 2, LEN])
        qT = sb("qT", [P, UNIT])
        kx = sb("kx", [P, 4, UNIT])
        vb = [sb(f"vb{b}", [P, 4, 8, 2, VW]) for b in range(2)]
        mx = sb("mx", [P, QUADS, 8])
        prob = [sb(f"prob{j}", [P, 2, 4, LEN]) for j in range(QUADS)]
        pT = [sb(f"pT{b}", [P, 2, 2, P]) for b in range(2)]
        rden = sb("rden", [P, 2 * HEADS])
        on = sb("on", [P, 2, D])
        oT = sb("oT", [P, 2, P])
        xr = [sb(f"xr{b}", [P, 2, ROWW + 7]) for b in range(2)]
        st6b = sb("st6b", [P, 2, 6])
        mvb = sb("mvb", [P, 2, 2])
        vareb = sb("vareb", [P, 2])
        rstdb = sb("rstdb", [P, 2])
        x1T = sb("x1T", [P, 2, P])
        lg = sb("lg", [P, 2, E1])
        top = sb("top", [P, 2, 8])
        topi = sb("topi", [P, 2, 8], U32)
        onehot = sb("onehot", [P, 2, E0], BF16)
        seen = sb("seen", [P, 2, E0], BF16)
        ex = sb("ex", [P, 2, E1])
        den = sb("den", [P, 2])
        gate = sb("gate", [P, 2])
        rank = sb("rank", [P, 2, E0])
        rsel = sb("rsel", [P, 2, E0])
        posf = sb("posf", [P, 2])
        posi = [sb(f"posi{b}", [P, 2], I32) for b in range(2)]
        place = sb("place", [P, UNITS, 2])
        beyond = sb("beyond", [P, UNITS, 2])
        placed = sb("placed", [P, UNITS, 2])
        move = sb("move", [P, E0 - 1])
        placei = sb("placei", [P, UNITS, 2], I32)
        gidx = [sb(f"gidx{b}", [P, 2], I32) for b in range(2)]
        count = sb("count", [P, E0])
        tiles = sb("tiles", [P, E0])
        tilesi = sb("tilesi", [P, E0], I32)
        tend = sb("tend", [1, E0])
        full = sb("full", [1, SLOTS, E0 - 1])
        fullt = sb("fullt", [1, SLOTS, E0 - 1])
        slotf = sb("slotf", [1, 5, SLOTS])
        slot_e = sb("slot_e", [1, SLOTS], I32)
        slot_row = sb("slot_row", [1, SLOTS], I32)
        padf = sb("padf", [P, 2 * E0])
        padi = sb("padi", [P, 2 * E0 + 2], I32)
        zrow = sb("zrow", [P, ROWW])
        xs = [sb(f"xs{b}", [P, ROWW]) for b in range(RING0)]
        xsT = [sb(f"xsT{b}", [P, P]) for b in range(2)]
        hb = [sb(f"hb{b}", [P, F0]) for b in range(2)]
        hT = [sb(f"hT{b}", [P, F0]) for b in range(2)]
        yb = [sb(f"yb{b}", [P, D]) for b in range(2)]
        yo = [sb(f"yo{b}", [P, D]) for b in range(2)]
        x3 = [sb(f"x3{b}", [P, 2, D]) for b in range(2)]
        hn = sb("hn", [P, 2, D])
        width = sb("width", [P, 2])
        dvar = sb("dvar", [P, 2])
        dnorm = sb("dnorm", [P, 2])
        nrm = sb("nrm", [P, 2])
        rnrm = sb("rnrm", [P, 2])
        hnT = sb("hnT", [P, UNIT])
        gm = sb("gm", [P, 2, E1])
        fb = sb("fb", [P, 2, 2, E1])
        idle = sb("idle", [P, 2])
        gtop = sb("gtop", [P, 2])
        wg = sb("wg", [P, 2, E1])
        wres = sb("wres", [P, 2, E1])
        w3 = sb("w3", [P, 2, 3, E1], BF16)
        w3T = sb("w3T", [3 * E1, UNIT], BF16)
        z = w1[:, :].rearrange("p (e n) -> p e n", e=E1)
        qkT = sb("qkT", [P, 2, UNIT])
        vh = sb("vh", [P, 2, D])
        smx = sb("smx", [P, 2])
        sd = sb("sd", [P, 2, LEN])
        pbd = sb("pbd", [P, 2, 2, LEN])
        srs = sb("srs", [P, 2])
        pbT = sb("pbT", [P, UNIT])
        ohT = sb("ohT", [P, UNIT])
        res = [sb(f"res{b}", [P, 2, D]) for b in range(2)]

        m0 = bank("m0")
        m1 = bank("m1")
        s_bank = [bank(f"s_bank{j}") for j in range(QUADS)]
        tb = bank("tb")
        po = bank("po")
        m0_bf = m0[:, :].bitcast(BF16)

        names = ("vec_ln", "pool_ln", "rstd_ready", "xn_ready", "residual_ready",
                 "xc_in_psum", "xcT_ready", "qk_in_psum", "qk_ready", "v_in_psum", "v_ready", "scores_in_psum",
                 "vec_max", "scores_ready", "exp_ready", "probT_in_psum", "probT_ready", "pv_in_psum",
                 "vec_rden", "heads_ready", "oT_in_psum", "oT_ready", "y_in_psum", "x_mid_ready", "pad_row_ready",
                 "pool_pad", "vec_ln2", "pool_ln2", "rstd2_ready", "xn2_ready", "x1T_in_psum", "x1T_ready",
                 "logits_in_psum", "logits_ready", "exp8_ready", "idx_ready")
        s = [{n: sem(f"{n}_{l}") for n in names} for l in range(2)]
        rnames = ("router_steps", "onehot_ready", "rank_in_psum", "rank_steps", "pos_ready")
        route = {n: sem(n) for n in rnames}
        x_loaded = [[sem(f"x_loaded_{l}_{par}") for par in range(2)] for l in range(2)]
        ctx_loaded = [[sem(f"ctx_loaded_{l}_{par}") for par in range(2)] for l in range(2)]
        slot_loaded = [sem(f"slot_loaded_{n}") for n in range(RING0)]
        stored = [sem(f"stored_{par}") for par in range(2)]
        scattered = [sem(f"scattered_{par}") for par in range(2)]
        ring_filled = sem("ring_filled")
        ring_used = sem("ring_used")
        z_used = sem("z_used")
        fnames = ("nrm_steps", "nrm_ready", "gate_steps", "gate_logits", "wexp_ready", "w3_ready",
                  "w3T_in_psum", "w3T_ready", "qk1_ready", "v1_ready", "s1_in_psum", "s1_ready",
                  "p1_ready", "vec_s1", "vec_p1", "pn_ready", "pT_in_psum", "pT_ready", "o1_in_psum", "o1_ready",
                  "res_ready")
        f = {n: sem(f"f_{n}") for n in fnames}
        load = {n: sem(f"load_{n}") for n in ("attn", "moe", "experts1", "small", "swap")}
        setup = {n: sem(f"setup_{n}") for n in ("pool", "tensor", "scalar", "vector", "consts", "vec_done")}
        routed = {n: sem(f"routed_{n}") for n in ("count_in_psum", "vector", "table", "padded", "zero")}
        passed = sem("passed")
        out_sem = [sem(f"out_sem_{par}") for par in range(2)]
        b = {n: sem(f"moe_{n}") for n in ("xT_in_psum", "xT_ready", "h_in_psum", "h_ready", "gelu_ready",
                                          "hT_in_psum", "hT_ready", "y_in_psum", "vec_y", "y_ready")}

        def apart(eng):
            eng.sem_inc(passed, 1)

        block = ctx.enter_context(nc.Block())

        def exists(unit):
            return not isinstance(unit, int) or 0 <= unit < UNITS

        def wait(eng, semaphore, count):
            if not isinstance(count, int) or count > 0:
                eng.wait_ge(semaphore, count)

        def units(eng, body):
            for u in range(-2, 2):
                body(u, u % 2)
            with eng.Fori(1, UNITS // 2 - 2) as i:
                for par in range(2):
                    body(i * 2 + par, par)
            for u in range(UNITS - 4, UNITS + 2):
                body(u, u % 2)

        def slots(eng, body):
            for sl in range(-3, RING0):
                body(sl, sl % RING0, sl % 2, sl // RING0)
            with eng.Fori(1, SLOTS // RING0 - 1) as i:
                for n in range(RING0):
                    body(i * RING0 + n, n, n % 2, i)
            for sl in range(SLOTS - RING0, SLOTS):
                body(sl, sl % RING0, sl % 2, sl // RING0)

        def slot_exists(sl):
            return not isinstance(sl, int) or 0 <= sl < SLOTS

        @block.sync
        def _(sp):
            def tokens(ap, u):
                return ap[bass.ds(u * UNIT, UNIT), :].rearrange("(t p) d -> p t d", p=P)

            def load_unit(layer, v, par):
                if layer == 0:
                    sp.dma_start(xin[par][:, :, :], tokens(a["x"], v)).then_inc(x_loaded[0][par], 16)
                sp.dma_start(cin[par][:, :, :], tokens(a["ctx_1024"], v)).then_inc(ctx_loaded[layer][par], 16)

            def body(layer, u, par):
                q = s[layer]
                if exists(u + 3) and not (isinstance(u, int) and u < -1):
                    if layer == 0:
                        wait(sp, q["residual_ready"], u + 2)
                    wait(sp, q["xc_in_psum"], u + 2)
                    load_unit(layer, u + 3, 1 - par)
                if layer == 1 and exists(u - 2):
                    wait(sp, f["res_ready"], u - 1)
                    sp.dma_start(tokens(out, u - 2), res[par][:, :, :]).then_inc(out_sem[par], 16)

            load_unit(0, 0, 0)
            for w, n in ((wq, "q"), (wk, "k"), (wv, "v"), (wo, "o")):
                sp.dma_start(w[0][:, :], a[f"L0_xattn_W{n}"]).then_inc(load["attn"], 16)
            for k, n in enumerate("qkvo"):
                sp.dma_start(wraw[:, k, :], a[f"L1_xattn_W{n}"]).then_inc(load["attn"], 16)
            for k, n in enumerate(("L0_xattn_bq", "L0_xattn_bk", "L1_xattn_bq", "L1_xattn_bk")):
                sp.dma_start(bcol[:, k:k + 1], a[n].unsqueeze(1)).then_inc(load["small"], 16)
            for l in range(2):
                sp.dma_start(bvcol[:, l:l + 1], a[f"L{l}_xattn_bv"].unsqueeze(1)).then_inc(load["small"], 16)
                sp.dma_start(bo_b[:, l, :], a[f"L{l}_xattn_bo"].partition_broadcast(P)).then_inc(load["small"], 16)
            sp.dma_start(graw[:, 0:2], a["g_xattn"].partition_broadcast(P)).then_inc(load["small"], 16)
            sp.dma_start(graw[:, 2:4], a["g_ffn"].partition_broadcast(P)).then_inc(load["small"], 16)
            sp.dma_start(wr[:, :], a["L0_ffn_Wr"]).then_inc(load["small"], 16)
            sp.dma_start(brb[:, :], a["L0_ffn_br"].partition_broadcast(P)).then_inc(load["small"], 16)
            sp.dma_start(simm[:, :], a["L1_ffn_sim_matrix"]).then_inc(load["small"], 16)
            sp.dma_start(sgate[:, :], a["L1_ffn_gates"].partition_broadcast(P)).then_inc(load["small"], 16)
            sp.dma_start(pad_u8[LEN:LEN + 2, :, :], a["mask_BxS2_bf0"].rearrange("(g s) k -> s g k", s=2))\
                .then_inc(load["small"], 16)
            load_unit(0, 1, 1)
            sp.dma_start(w1[:, :].rearrange("c (e n) -> c e n", e=E0), a["L0_ffn_W1"].rearrange("e c n -> c e n"))\
                .then_inc(load["moe"], 16)
            sp.dma_start(w2[:, :].rearrange("c (e n) -> c e n", n=D),
                         a["L0_ffn_W2"].rearrange("e (j c) n -> c (e j) n", c=P)).then_inc(load["moe"], 16)
            sp.dma_start(b1b[:, :], a["L0_ffn_b1"].rearrange("e n -> (e n)").partition_broadcast(P))\
                .then_inc(load["moe"], 16)
            sp.dma_start(b2b[:, :], a["L0_ffn_b2"].rearrange("e n -> (e n)").partition_broadcast(P))\
                .then_inc(load["moe"], 16)
            for k, n in enumerate("qkvo"):
                sp.dma_start(proj[:, k, :, :], a[f"L1_ffn_{n}_proj"].rearrange("e c n -> c e n"))\
                    .then_inc(load["experts1"], 16)
            units(sp, lambda u, par: body(0, u, par))

            sp.wait_ge(routed["table"], 2)
            sp.wait_ge(routed["padded"], 16 * 2 * (E0 + 1))
            for par in range(2):
                sp.wait_ge(scattered[par], 16 * UNITS)

            def load_slot(sl, n):
                row = sp.value_load(slot_row[0:1, bass.ds(sl, 1)], min_val=0, max_val=E0 * REGION - P)
                sp.dma_start(xs[n][:, :], sorted_in[bass.ds(row, P), :]).then_inc(slot_loaded[n], 16)

            def slot(sl, n, par, rnd):
                if slot_exists(sl):
                    sp.wait_ge(b["y_ready"], sl + 1)
                    sp.dma_start(sorted_out[bass.ds(sl * P, P), :], yo[par][:, :]).then_inc(stored[par], 16)
                    if slot_exists(sl + RING0):
                        load_slot(sl + RING0, n)

            for sl in range(RING0):
                load_slot(sl, sl)
            slots(sp, slot)

            load_unit(1, 0, 0)
            load_unit(1, 1, 1)
            units(sp, lambda u, par: body(1, u, par))
            for par in range(2):
                sp.wait_ge(out_sem[par], 8 * UNITS)

        @block.gpsimd
        def _(g):
            done = Steps(g, setup["pool"], 0, 0)
            for t, v in ((ident[:, :], 0.0), (identb[:, :], 0.0), (onesf[:, :], 1.0), (onesb[:, :], 1.0),
                         (earlier[:, :], 1.0), (mask_rows[:, :, :], 0.0), (mask_chunk[:, :, :], 0.0),
                         (mask_causal[0][:, :, :], 0.0), (mask_causal[1][:, :, :], 0.0), (head_blk[:, :], 1.0),
                         (term_sel[:, :, :], 0.0), (half_neg[:, :], -0.5), (half_pos[:, :], 0.5),
                         (eps[:, :], EPS), (masked[:, :], MASKED), (width[:, :], float(D)),
                         (zrow[:, :], 0.0), (pbd[:, :, :, :], 0.0), (vb[0][:, :, :, :, :], 0.0),
                         (vb[1][:, :, :, :, :], 0.0), (seen[:, 0, :], 0.0)):
                done.free(g.memset(t, v))
            g.wait_ge(setup["pool"], done.n)
            for t in (ident, identb):
                done.free(g.affine_select(out=t[:, :], in_=t[:, :], compare_op=ALU.not_equal, fill=1.0, base=0,
                                          pattern=[[-1, P]], channel_multiplier=1))
            done.free(g.affine_select(out=earlier[:, :], in_=earlier[:, :], compare_op=ALU.is_gt, fill=0.0, base=0,
                                      pattern=[[1, P]], channel_multiplier=-1))
            done(g.affine_select(out=mask_rows[:, :, :], in_=mask_rows[:, :, :], compare_op=ALU.not_equal,
                                 fill=1.0, base=0, pattern=[[0, 2], [-1, LEN]], channel_multiplier=1))
            done(g.affine_select(out=mask_rows[:, :, :], in_=mask_rows[:, :, :], compare_op=ALU.not_equal,
                                 fill=1.0, base=-LEN, pattern=[[-1, 2], [0, LEN]], channel_multiplier=1))
            done(g.memset(mask_chunk[0:CHUNK, :, CHUNK:LEN], MASKED))
            for m in mask_causal:
                done.free(g.affine_select(out=m[0:LEN], in_=m[0:LEN], compare_op=ALU.is_ge, fill=MASKED, base=0,
                                          pattern=[[0, 8], [-1, LEN]], channel_multiplier=1))
            done(g.affine_select(out=head_blk[:, :], in_=head_blk[:, :], compare_op=ALU.is_ge, fill=0.0, base=0,
                                 pattern=[[-HD, HEADS]], channel_multiplier=1))
            done(g.affine_select(out=head_blk[:, :], in_=head_blk[:, :], compare_op=ALU.is_ge, fill=0.0,
                                 base=HD - 1, pattern=[[HD, HEADS]], channel_multiplier=-1))
            for t in range(3):
                done(g.affine_select(out=term_sel[:, :, :], in_=term_sel[:, :, :], compare_op=ALU.not_equal,
                                     fill=1.0, base=-E1 * t, pattern=[[-1, E1], [0, P]], channel_multiplier=1))
            for v in vb:
                for h in range(2):
                    done(g.memset(v[64 * h:64 * h + 64, :, :, h, HD:VW], 1.0))
            done(g.iota(iota[:, :, :], pattern=[[0, 2], [1, E1]], base=0, channel_multiplier=0,
                        allow_small_or_imprecise_dtypes=True))
            done(g.iota(slot_no[:, :], pattern=[[1, SLOTS]], base=0, channel_multiplier=0,
                        allow_small_or_imprecise_dtypes=True))
            done(g.tensor_scalar(region0[:, :], iota[:, 0, 0:E0], float(REGION), None, ALU.mult))
            g.memset(half_neg[:, :], -0.5).then_inc(setup["consts"], 1)
            g.wait_ge(setup["vector"], 1)
            g.tensor_tensor(simn[:, :], simq[:, :], half_pos[:, :], ALU.pow).then_inc(setup["consts"], 1)
            g.wait_ge(setup["vec_done"], 5)

            def gather(v, par):
                q = s[1]
                if exists(v - 2):
                    g.wait_ge(q["residual_ready"], v - 1)
                wait(g, q["pad_row_ready"], v)
                apart(g)
                g.tensor_copy(gidx[par][:, :], placei[:, bass.ds(v, 1), :].rearrange("p a t -> p (a t)"))\
                    .then_inc(q["idx_ready"], 1)
                g.wait_ge(q["idx_ready"], v + 1)
                apart(g)
                for t in range(2):
                    g.indirect_dma_start(
                        out=xin[par][:, t, :], out_offset=None, in_=sorted_out[:, :],
                        in_offset=bass.IndirectOffsetOnAxis(ap=gidx[par][:, t:t + 1], axis=0),
                        bounds_check=SLOTS * P - 1, oob_is_err=True).then_inc(x_loaded[1][par], 16)

            def pad_row(v, par):
                q = s[1]
                wait(g, q["scores_in_psum"], 4 * v - 4)
                g.wait_ge(x_loaded[1][par], 16 * (v - par + 2))
                wait(g, q["residual_ready"], v - 1)
                step = Steps(g, q["pool_pad"], v, 1)
                step(g.tensor_copy(pad_unit[LEN:LEN + 2, :, :], pad_u8[LEN:LEN + 2, bass.ds(v * 2, 2), :]))
                step.end()
                g.tensor_tensor(mask_causal[par][LEN:LEN + 2, :, :].rearrange("p (t h) k -> p t h k", t=2),
                                bcast(pad_unit[LEN:LEN + 2, :, :], 4, 2),
                                bcast(bcast(masked[LEN:LEN + 2, :], 4, 1), 2, 1), ALU.mult)\
                    .then_inc(q["pad_row_ready"], 1)

            def norm(layer, v, par):
                q = s[layer]
                g.wait_ge(q["vec_ln"], 4 * v + 4)
                if layer == 1:
                    g.wait_ge(q["pad_row_ready"], v + 1)
                step = Steps(g, q["pool_ln"], v, 2)
                step(g.tensor_tensor(vare[:, :], mv[:, :, 1], eps[:, :], ALU.add))
                step(g.tensor_tensor(rstd[:, :], vare[:, :], half_neg[:, :], ALU.pow))
                step.end()
                wait(g, q["xc_in_psum"], v)
                apart(g)
                for t in range(2):
                    ins = g.tensor_scalar(xn[:, t, :], xin[par][:, t, :], mv[:, t, 0:1], rstd[:, t:t + 1],
                                          ALU.subtract, ALU.mult)
                ins.then_inc(q["xn_ready"], 1)

            def residual(layer, v, par):
                q = s[layer]
                g.wait_ge(x_loaded[layer][par], (8 + 8 * layer) * (v - par + 2))
                wait(g, q["x_mid_ready"], v - 1)
                g.tensor_tensor(xb[par][:, :, :], xin[par][:, :, :], bcast(gbo[:, layer, :], 2, 1), ALU.add)\
                    .then_inc(q["residual_ready"], 1)

            def second_norm(layer, u, src, dst):
                q = s[layer]
                g.wait_ge(q["vec_ln2"], 4 * u + 4)
                step = Steps(g, q["pool_ln2"], u, 2)
                step(g.tensor_tensor(vareb[:, :], mvb[:, :, 1], eps[:, :], ALU.add))
                step(g.tensor_tensor(rstdb[:, :], vareb[:, :], half_neg[:, :], ALU.pow))
                step.end()
                if layer == 1:
                    wait(g, q["x1T_in_psum"], u)
                apart(g)
                for t in range(2):
                    ins = g.tensor_scalar(dst(t), src(t), mvb[:, t, 0:1], rstdb[:, t:t + 1], ALU.subtract, ALU.mult)
                ins.then_inc(q["xn2_ready"], 1)

            def body0(u, par):
                if exists(u + 2):
                    norm(0, u + 2, par)
                if exists(u - 1):
                    second_norm(0, u - 1, lambda t: xr[1 - par][:, t, 0:D], lambda t: xr[1 - par][:, t, D:2 * D])
                if exists(u + 1):
                    residual(0, u + 1, 1 - par)
                if exists(u - 2):
                    g.wait_ge(route["pos_ready"], u - 1)
                    apart(g)
                    for t in range(2):
                        g.indirect_dma_start(
                            out=sorted_in[:, :],
                            out_offset=bass.IndirectOffsetOnAxis(ap=posi[par][:, t:t + 1], axis=0),
                            in_=xr[par][:, t, 0:ROWW], in_offset=None,
                            bounds_check=E0 * REGION - 1, oob_is_err=True).then_inc(scattered[par], 16)

            units(g, body0)

            g.wait_ge(routed["zero"], 1)
            for k in range(2 * E0 + 2):
                g.indirect_dma_start(
                    out=sorted_in[:, :], out_offset=bass.IndirectOffsetOnAxis(ap=padi[:, k:k + 1], axis=0),
                    in_=zrow[:, :], in_offset=None,
                    bounds_check=E0 * REGION - 1, oob_is_err=True).then_inc(routed["padded"], 16)

            g.wait_ge(routed["table"], 3)
            for par in range(2):
                g.wait_ge(stored[par], 8 * SLOTS)

            def body1(u, par):
                if exists(u + 2):
                    pad_row(u + 2, par)
                    norm(1, u + 2, par)
                w = u - 1
                if exists(w):
                    second_norm(1, w, lambda t: x3[1 - par][:, t, :], lambda t: hn[:, t, :])
                    step = Steps(g, f["nrm_steps"], w, 2)
                    step(g.tensor_tensor(dvar[:, :], mvb[:, :, 1], width[:, :], ALU.mult))
                    step(g.tensor_tensor(dnorm[:, :], dvar[:, :], half_pos[:, 0:2], ALU.pow))
                    step.end()
                    g.tensor_tensor(nrm[:, :], dnorm[:, :], rstdb[:, :], ALU.mult).then_inc(f["nrm_ready"], 1)
                if exists(u + 1):
                    residual(1, u + 1, 1 - par)
                if exists(u + 3):
                    gather(u + 3, 1 - par)

            gather(0, 0)
            units(g, body1)

        @block.scalar
        def _(act):
            act.wait_ge(load["small"], 16 * 15)
            act.activation(tg[:, :], graw[:, :], ACT.Tanh).then_inc(setup["scalar"], 1)
            act.activation(sgate[:, :], sgate[:, :], ACT.Exp, scale=-1.0).then_inc(setup["scalar"], 1)
            act.wait_ge(setup["vec_done"], 1)

            def copy_xcT(q, v):
                if exists(v):
                    act.wait_ge(q["xc_in_psum"], v + 1)
                    wait(act, q["v_in_psum"], v)
                    act.activation(xT[:, :], m0[:, 0:256], ACT.Copy)
                    act.activation(cT[:, :, :, :], bcast(m0[:, 256:512].rearrange("p (s k) -> p s k", s=4), 2, 2),
                                   ACT.Copy).then_inc(q["xcT_ready"], 1)

            def copy_v(q, v, par):
                if exists(v):
                    act.wait_ge(q["v_in_psum"], v + 1)
                    wait(act, q["pv_in_psum"], 4 * v - 4)
                    for half in range(2):
                        rows = slice(64 * half, 64 * half + 64)
                        ins = act.activation(
                            vb[par][rows, :, :, half, 0:HD],
                            m0[rows, :].rearrange("p (s r h d) -> p s r h d", s=4, r=8, h=2)[:, :, :, half, :],
                            ACT.Copy)
                    ins.then_inc(q["v_ready"], 1)

            def exp_quad(q, v, j):
                if exists(v):
                    act.wait_ge(q["scores_ready"], 4 * v + j + 1)
                    act.activation(prob[j][:, :, :, :], prob[j][:, :, :, :], ACT.Exp, scale=SCALE)\
                        .then_inc(q["exp_ready"], 1)

            def copy_pT(q, u, j):
                if exists(u):
                    act.wait_ge(q["probT_in_psum"], 4 * u + j + 1)
                    wait(act, q["pv_in_psum"], 4 * u + j - 1)
                    act.activation(pT[j % 2][:, :, :, :], tb[:, :].rearrange("p (r t n) -> p r t n", r=2, t=2),
                                   ACT.Copy).then_inc(q["probT_ready"], 1)

            def copy_oT(q, u):
                if exists(u):
                    act.wait_ge(q["oT_in_psum"], u + 1)
                    wait(act, q["y_in_psum"], u)
                    act.activation(oT[:, :, :], m0[:, 0:256].rearrange("p (t n) -> p t n", t=2), ACT.Copy)\
                        .then_inc(q["oT_ready"], 1)

            def body0(u, par):
                q = s[0]
                copy_pT(q, u, 0)
                copy_oT(q, u - 1)
                exp_quad(q, u + 1, 0)
                copy_pT(q, u, 1)
                if exists(u - 2):
                    act.wait_ge(q["logits_ready"], u - 1)
                    act.activation(ex[:, :, 0:E0], lg[:, :, 0:E0], ACT.Exp).then_inc(q["exp8_ready"], 1)
                copy_xcT(q, u + 2)
                exp_quad(q, u + 1, 1)
                copy_pT(q, u, 2)
                exp_quad(q, u + 1, 2)
                copy_pT(q, u, 3)
                if exists(u - 1):
                    act.wait_ge(q["x1T_in_psum"], u)
                    act.activation(x1T[:, :, :], m0[:, 0:256].rearrange("p (t n) -> p t n", t=2), ACT.Copy)\
                        .then_inc(q["x1T_ready"], 1)
                copy_v(q, u + 2, par)
                exp_quad(q, u + 1, 3)

            units(act, body0)

            def slot(sl, n, par, rnd):
                if slot_exists(sl):
                    act.wait_ge(b["hT_in_psum"], sl + 1)
                    act.activation(hT[par][:, :], tb[:, :], ACT.Copy).then_inc(b["hT_ready"], 1)
                if slot_exists(sl + 2):
                    act.wait_ge(b["h_ready"], sl + 3)
                    act.activation(hb[par][:, :], hb[par][:, :], ACT.Gelu).then_inc(b["gelu_ready"], 1)
                if slot_exists(sl + 3):
                    act.wait_ge(b["xT_in_psum"], sl + 4)
                    act.activation(xsT[1 - par][:, :], m0[:, 0:P], ACT.Copy).then_inc(b["xT_ready"], 1)

            slots(act, slot)

            def body1(u, par):
                q = s[1]
                w = u - 2
                if exists(w):
                    act.wait_ge(z_used, 16 * w + 8)
                    act.activation(vh[:, :, :], m0[:, 0:256].rearrange("p (t n) -> p t n", t=2), ACT.Copy)\
                        .then_inc(f["v1_ready"], 1)
                copy_pT(q, u, 0)
                copy_oT(q, u - 1)
                exp_quad(q, u + 1, 0)
                if exists(w):
                    act.wait_ge(f["s1_ready"], w + 1)
                    for half in range(2):
                        rows = slice(64 * half, 64 * half + 64)
                        ins = act.activation(pbd[rows, :, half, :], sd[rows, :, :], ACT.Exp, scale=SCALE_H)
                    ins.then_inc(f["p1_ready"], 1)
                copy_pT(q, u, 1)
                copy_xcT(q, u + 2)
                exp_quad(q, u + 1, 1)
                copy_pT(q, u, 2)
                exp_quad(q, u + 1, 2)
                if exists(w):
                    act.wait_ge(f["pT_in_psum"], w + 1)
                    act.activation(pbT[:, :], tb[:, 0:256], ACT.Copy).then_inc(f["pT_ready"], 1)
                if exists(u - 1):
                    act.wait_ge(q["x1T_in_psum"], u)
                    act.activation(hnT[:, :], m0[:, 0:256], ACT.Copy).then_inc(q["x1T_ready"], 1)
                copy_pT(q, u, 3)
                if exists(w):
                    act.wait_ge(f["o1_in_psum"], w + 1)
                    act.activation(ohT[:, :], m0[:, 0:256], ACT.Copy).then_inc(f["o1_ready"], 1)
                copy_v(q, u + 2, par)
                exp_quad(q, u + 1, 3)
                if exists(u - 1):
                    act.wait_ge(q["logits_ready"], u)
                    act.activation(ex[:, :, :], lg[:, :, :], ACT.Exp).then_inc(f["wexp_ready"], 1)
                    act.wait_ge(f["w3T_in_psum"], u)
                    act.activation(w3T[:, :], m0_bf[0:3 * E1, 0:256], ACT.Copy).then_inc(f["w3T_ready"], 1)

            units(act, body1)

        @block.vector
        def _(v):
            v.wait_ge(setup["consts"], 1)
            v.wait_ge(load["attn"], 16 * 8)
            v.wait_ge(load["small"], 16 * 15)
            v.tensor_reduce(head_of[:, :], head_blk[:, :].rearrange("p (j r) -> p r j", r=4), AX_X, ALU.add)
            for l in range(2):
                v.tensor_scalar(bvb[:, l, :], onesf[:, :], bvcol[:, l:l + 1], None, ALU.mult)
            v.tensor_tensor(simq[:, :], simm[:, :], simm[:, :], ALU.mult).then_inc(setup["vec_done"], 1)
            v.wait_ge(setup["tensor"], 1)
            for k, w in enumerate((wq, wk, wv, wo)):
                ins = v.tensor_copy(w[1][:, :], s_bank[k][:, 0:P])
            ins.then_inc(setup["vec_done"], 1)
            v.wait_ge(setup["tensor"], 2)
            v.tensor_copy(simq[:, :], m1[:, 256:256 + E1]).then_inc(setup["vector"], 1)
            v.wait_ge(setup["scalar"], 2)
            step = Steps(v, setup["vec_done"], 0, 0)
            step.n = 2
            step(v.tensor_tensor(bo_b[:, :, :], m1[:, 0:256].rearrange("p (l n) -> p l n", l=2), bo_b[:, :, :], ALU.add))
            for l in range(2):
                step(v.tensor_scalar(gbo[:, l, :], bo_b[:, l, :], tg[:, l:l + 1], None, ALU.mult))
            step(v.tensor_scalar(sgate[:, :], sgate[:, :], 1.0, None, ALU.add))
            step(v.reciprocal(sgate[:, :], sgate[:, :]))
            v.wait_ge(setup["consts"], 2)
            step(v.tensor_scalar(simn[:, :], simn[:, :], 1e-12, None, ALU.max))
            step(v.reciprocal(simn[:, :], simn[:, :]))
            step(v.tensor_tensor(simn[:, :], simm[:, :], simn[:, :], ALU.mult))

            def stats(sm, u, x, six, two):
                step = Steps(v, sm, u, 4)
                step.free(v.bn_stats(six[:, 0, :], x[:, 0, 0:D]))
                step(v.bn_stats(six[:, 1, :], x[:, 1, 0:D]))
                apart(v)
                for t in range(2):
                    step.free(v.bn_aggr(two[:, t, :], six[:, t, :]))
                step.end()

            def first_stats(layer, w, par):
                q = s[layer]
                if exists(w):
                    v.wait_ge(x_loaded[layer][par], (8 + 8 * layer) * (w - par + 2))
                    wait(v, q["xn_ready"], w)
                    apart(v)
                    stats(q["vec_ln"], w, xin[par], st6, mv)

            def second_stats(layer, u, x):
                q = s[layer]
                v.wait_ge(q["x_mid_ready"], u + 1)
                wait(v, q["xn2_ready"] if layer == 0 else f["nrm_ready"], u)
                apart(v)
                stats(q["vec_ln2"], u, x, st6b, mvb)

            def shift_quad(q, w, j):
                if exists(w):
                    v.wait_ge(q["scores_in_psum"], 4 * w + j + 1)
                    step = Steps(v, q["vec_max"], w * QUADS + j, 1)
                    sc = s_bank[j][:, :].rearrange("p (a k) -> p a k", k=LEN)
                    step(v.tensor_reduce(mx[:, j, :], sc, AX_X, ALU.max))
                    wait(v, q["probT_in_psum"], 4 * w - 3 + j)
                    v.scalar_tensor_tensor(out=prob[j][:, :, :, :].rearrange("p r t k -> p (r t) k"), in0=sc,
                                           scalar=MASKED, in1=bcast(mx[:, j, :], LEN, 2),
                                           op0=ALU.max, op1=ALU.subtract).then_inc(q["scores_ready"], 1)

            def copy_qk(layer, w):
                q = s[layer]
                if exists(w):
                    v.wait_ge(q["qk_in_psum"], w + 1)
                    wait(v, q["scores_in_psum"], 4 * w)
                    v.tensor_scalar(qT[:, :], m1[:, 0:256], bcol[:, 2 * layer:2 * layer + 1], None, ALU.add)
                    v.scalar_tensor_tensor(out=kx[:, :, :], in0=bcast(m1[:, 256:512], 4, 1),
                                           scalar=bcol[:, 2 * layer + 1:2 * layer + 2],
                                           in1=bcast(head_of[:, :], UNIT, 2), op0=ALU.add, op1=ALU.mult)\
                        .then_inc(q["qk_ready"], 1)

            def normalise(q, u):
                if exists(u):
                    v.wait_ge(q["pv_in_psum"], 4 * u + 4)
                    step = Steps(v, q["vec_rden"], u, 1)
                    o = po[:, 0:2 * HEADS * VW].rearrange("p (a c) -> p a c", c=VW)
                    step(v.reciprocal(rden[:, :], o[:, :, HD]))
                    wait(v, q["oT_in_psum"], u)
                    v.tensor_tensor(on[:, :, :].rearrange("p t (h d) -> p (t h) d", d=HD), o[:, :, 0:HD],
                                    bcast(rden[:, :], HD, 2), ALU.mult).then_inc(q["heads_ready"], 1)

            def add_residual(layer, u, par, dst):
                q = s[layer]
                v.wait_ge(q["y_in_psum"], u + 1)
                v.wait_ge(q["residual_ready"], u + 1)
                v.scalar_tensor_tensor(out=dst, in0=m1[:, 0:256].rearrange("p (t n) -> p t n", t=2),
                                       scalar=tg[:, layer:layer + 1], in1=xb[par][:, :, :],
                                       op0=ALU.mult, op1=ALU.add).then_inc(q["x_mid_ready"], 1)

            ROUTER, RANK = 5, 6

            def router_logits(w):
                if exists(w):
                    v.wait_ge(s[0]["logits_in_psum"], w + 1)
                    step = Steps(v, route["router_steps"], w, ROUTER)
                    step(v.tensor_tensor(lg[:, :, 0:E0], m1[:, 0:2 * E0].rearrange("p (t e) -> p t e", t=2),
                                         bcast(brb[:, :], 2, 1), ALU.add))
                    apart(v)
                    for t in range(2):
                        step.free(v.max(top[:, t, :], lg[:, t, 0:E0]))

            def router_choice(w):
                if exists(w):
                    v.wait_ge(route["router_steps"], ROUTER * w + 3)
                    apart(v)
                    for t in range(2):
                        ins = v.max_index(topi[:, t, :], top[:, t, :], lg[:, t, 0:E0])
                        ins.then_inc(route["router_steps"], 1)

            def router_onehot(w):
                if exists(w):
                    v.wait_ge(route["router_steps"], ROUTER * w + ROUTER)
                    v.tensor_tensor(onehot[:, :, :], iota[:, :, 0:E0], topi[:, :, 0:1].broadcast_to([P, 2, E0]),
                                    ALU.is_equal).then_inc(route["onehot_ready"], 1)
                    v.tensor_tensor(lg[:, :, 0:E0], lg[:, :, 0:E0], top[:, :, 0:1].broadcast_to([P, 2, E0]),
                                    ALU.subtract).then_inc(s[0]["logits_ready"], 1)
                    v.wait_ge(route["onehot_ready"], 2 * w + 1)
                    v.tensor_tensor(seen[:, 1, :], seen[:, 0, :], onehot[:, 0, :], ALU.add)\
                        .then_inc(route["onehot_ready"], 1)

            def router_rank(w):
                if exists(w):
                    v.wait_ge(route["rank_in_psum"], w + 1)
                    v.wait_ge(s[0]["exp8_ready"], w + 1)
                    step = Steps(v, route["rank_steps"], w, RANK)
                    step.free(v.tensor_tensor(seen[:, 0, :], seen[:, 1, :], onehot[:, 1, :], ALU.add))
                    step.free(v.tensor_tensor(rank[:, :, :], m1[:, 0:2 * E0].rearrange("p (t e) -> p t e", t=2),
                                              bcast(region0[:, :], 2, 1), ALU.add))
                    step(v.tensor_reduce(den[:, :], ex[:, :, 0:E0], AX_X, ALU.add))
                    step.free(v.tensor_tensor(rsel[:, :, :], rank[:, :, :], onehot[:, :, :], ALU.mult))
                    step(v.reciprocal(gate[:, :], den[:, :]))
                    step.free(v.tensor_reduce(posf[:, :], rsel[:, :, :], AX_X, ALU.add))
                    step.end()

            def router_place(w, par):
                if exists(w):
                    v.tensor_scalar(xr[par][:, :, 2 * D], gate[:, :], tg[:, 2:3], None, ALU.mult)
                    v.wait_ge(route["rank_steps"], RANK * w + RANK)
                    v.tensor_copy(place[:, bass.ds(w, 1), :], posf[:, :].unsqueeze(1))
                    v.tensor_copy(posi[par][:, :], posf[:, :]).then_inc(route["pos_ready"], 1)

            def body0(u, par):
                q = s[0]
                first_stats(0, u + 2, par)
                shift_quad(q, u + 1, 0)
                router_logits(u - 2)
                router_choice(u - 2)
                router_onehot(u - 2)
                shift_quad(q, u + 1, 1)
                if exists(u - 1):
                    wait(v, scattered[1 - par], 16 * (u - 2 + par))
                    add_residual(0, u - 1, 1 - par, xr[1 - par][:, :, 0:D])
                    second_stats(0, u - 1, xr[1 - par])
                router_rank(u - 2)
                shift_quad(q, u + 1, 2)
                router_place(u - 2, par)
                copy_qk(0, u + 2)
                shift_quad(q, u + 1, 3)
                normalise(q, u)

            units(v, body0)

            v.wait_ge(routed["count_in_psum"], 1)
            step = Steps(v, routed["vector"], 0, 0)
            step(v.tensor_copy(count[:, :], m1[:, 0:E0]))
            step(v.tensor_tensor(padf[:, 0:E0], count[:, :], region0[:, :], ALU.add))
            step(v.tensor_scalar(padf[:, 0:E0], padf[:, 0:E0], m1[:, 64:65], None, ALU.add))
            for k in range(E0 + 2):
                step.free(v.tensor_scalar(padi[:, E0 + k:E0 + k + 1], padf[:, E0 - 1:E0], float(P * (k + 1)), None,
                                          ALU.add))
            v.wait_ge(routed["vector"], step.n)
            v.tensor_copy(padi[:, 0:E0], padf[:, 0:E0]).then_inc(routed["zero"], 1)
            step(v.tensor_scalar(tilesi[:, :], count[:, :], P / 2 - 0.5, 1.0 / P, ALU.add, ALU.mult))
            step(v.tensor_copy(tiles[:, :], tilesi[:, :]))
            step(v.tensor_copy(tend[:, 0:1], tiles[0:1, 0:1]))
            for e in range(1, E0):
                step(v.tensor_tensor(tend[:, e:e + 1], tend[:, e - 1:e], tiles[0:1, e:e + 1], ALU.add))
            step(v.tensor_tensor(full[:, :, :], bcast(tend[:, 0:E0 - 1], SLOTS, 1), bcast(slot_no[:, :], E0 - 1, 2),
                                 ALU.is_le))
            step(v.tensor_reduce(slotf[:, 0, :], full[:, :, :], AX_X, ALU.add))
            step(v.tensor_tensor(fullt[:, :, :], full[:, :, :], bcast(tend[:, 0:E0 - 1], SLOTS, 1), ALU.mult))
            step(v.tensor_reduce(slotf[:, 1, :], fullt[:, :, :], AX_X, ALU.max))
            step(v.tensor_tensor(slotf[:, 2, :], slot_no[:, :], slotf[:, 1, :], ALU.subtract))
            step(v.tensor_scalar(slotf[:, 3, :], slotf[:, 2, :], float(P), None, ALU.mult))
            step(v.scalar_tensor_tensor(out=slotf[:, 4, :], in0=slotf[:, 0, :], scalar=float(REGION),
                                        in1=slotf[:, 3, :], op0=ALU.mult, op1=ALU.add))
            v.tensor_copy(slot_e[:, :], slotf[:, 0, :]).then_inc(routed["table"], 1)
            v.tensor_copy(slot_row[:, :], slotf[:, 4, :]).then_inc(routed["table"], 1)
            v.wait_ge(routed["table"], 2)
            v.wait_ge(load["moe"], 16 * 4)

            def expert_of(sl):
                return v.value_load(slot_e[0:1, bass.ds(sl, 1)], min_val=0, max_val=E0 - 1)

            def slot(sl, n, par, rnd):
                if slot_exists(sl + 2):
                    e = expert_of(sl + 2)
                    v.wait_ge(b["h_in_psum"], sl + 3)
                    wait(v, b["hT_in_psum"], sl + 1)
                    v.tensor_tensor(hb[par][:, :], s_bank[par][:, :], b1b[:, bass.ds(e * F0, F0)], ALU.add)\
                        .then_inc(b["h_ready"], 1)
                if slot_exists(sl):
                    e = expert_of(sl)
                    v.wait_ge(b["y_in_psum"], sl + 1)
                    step = Steps(v, b["vec_y"], sl, 1)
                    step(v.tensor_tensor(yb[par][:, :], po[:, 0:D], b2b[:, bass.ds(e * D, D)], ALU.add))
                    wait(v, stored[par], 8 * (sl - par))
                    v.scalar_tensor_tensor(out=yo[par][:, :], in0=yb[par][:, :], scalar=xs[n][:, 2 * D:2 * D + 1],
                                           in1=xs[n][:, 0:D], op0=ALU.mult, op1=ALU.add).then_inc(b["y_ready"], 1)

            slots(v, slot)

            step(v.tensor_scalar(move[:, :], tiles[:, 0:E0 - 1], float(P), -float(REGION), ALU.mult, ALU.add))
            src = place
            for e in range(1, E0):
                step(v.tensor_scalar(beyond[:, :, :], place[:, :, :], float(e * REGION), move[:, e - 1:e],
                                     ALU.is_ge, ALU.mult))
                step(v.tensor_tensor(placed[:, :, :], src[:, :, :], beyond[:, :, :], ALU.add))
                src = placed
            v.tensor_copy(placei[:, :, :], placed[:, :, :]).then_inc(routed["table"], 1)

            GATE = 21

            def gate_norm(u, step):
                v.wait_ge(f["nrm_ready"], u + 1)
                step(v.tensor_scalar(rnrm[:, :], nrm[:, :], 1e-12, None, ALU.max))
                step.free(v.reciprocal(rnrm[:, :], rnrm[:, :]))

            def gate_logits(u, step):
                v.wait_ge(s[1]["logits_in_psum"], u + 1)
                step.wait()
                for t in range(2):
                    ins = v.scalar_tensor_tensor(out=lg[:, t, :], in0=s_bank[0][:, E1 * t:E1 * t + E1],
                                                 scalar=rnrm[:, t:t + 1], in1=sgate[:, :],
                                                 op0=ALU.mult, op1=ALU.subtract)
                ins.then_inc(f["gate_logits"], 1)

            def gate_top(u, step):
                v.wait_ge(f["gate_logits"], u + 1)
                apart(v)
                for t in range(2):
                    step.free(v.max(top[:, t, :], lg[:, t, :]))
                step.free(v.tensor_scalar(gm[:, :, :], lg[:, :, :], 0.0, None, ALU.is_gt))

            def gate_index(step):
                step.wait()
                apart(v)
                for t in range(2):
                    step.free(v.max_index(topi[:, t, :], top[:, t, :], lg[:, t, :]))
                step.free(v.tensor_scalar(idle[:, :], top[:, :, 0], 0.0, None, ALU.is_le))
                step.free(v.tensor_scalar(gtop[:, :], top[:, :, 0], 0.0, None, ALU.max))

            def gate_shift(step):
                step.wait()
                v.scalar_tensor_tensor(out=lg[:, :, :], in0=lg[:, :, :], scalar=0.0, in1=bcast(gtop[:, :], E1, 2),
                                       op0=ALU.max, op1=ALU.subtract).then_inc(s[1]["logits_ready"], 1)
                for k in range(2):
                    step.free(v.tensor_tensor(fb[:, k, :, :], iota[:, :, :],
                                              topi[:, :, k:k + 1].broadcast_to([P, 2, E1]), ALU.is_equal))

            def gate_mask(step):
                step.wait()
                step(v.tensor_tensor(fb[:, 0, :, :], fb[:, 0, :, :], fb[:, 1, :, :], ALU.add))
                step(v.tensor_tensor(fb[:, 0, :, :], fb[:, 0, :, :], bcast(idle[:, :], E1, 2), ALU.mult))
                step.free(v.tensor_tensor(gm[:, :, :], gm[:, :, :], fb[:, 0, :, :], ALU.add))

            def gate_softmax(u, step):
                v.wait_ge(f["wexp_ready"], u + 1)
                step.wait()
                step(v.tensor_tensor(wg[:, :, :], ex[:, :, :], gm[:, :, :], ALU.mult))
                step(v.tensor_reduce(den[:, :], wg[:, :, :], AX_X, ALU.add))
                step(v.reciprocal(gate[:, :], den[:, :]))
                step.free(v.tensor_tensor(wg[:, :, :], wg[:, :, :], bcast(gate[:, :], E1, 2), ALU.mult))

            def gate_terms(step):
                step.wait()
                step(v.tensor_copy(w3[:, :, 0, :], wg[:, :, :]))
                step(v.tensor_tensor(wres[:, :, :], wg[:, :, :], w3[:, :, 0, :], ALU.subtract))
                step(v.tensor_copy(w3[:, :, 1, :], wres[:, :, :]))
                step.end()
                v.tensor_tensor(w3[:, :, 2, :], wres[:, :, :], w3[:, :, 1, :], ALU.subtract)\
                    .then_inc(f["w3_ready"], 1)

            def body1(u, par):
                q = s[1]
                w = u - 2
                if exists(w):
                    v.wait_ge(z_used, 16 * w + 8)
                    v.tensor_copy(qkT[:, :, :], m1[:, :].rearrange("p (a n) -> p a n", a=2))\
                        .then_inc(f["qk1_ready"], 1)
                first_stats(1, u + 2, par)
                shift_quad(q, u + 1, 0)
                if exists(w):
                    v.wait_ge(f["s1_in_psum"], w + 1)
                    sc = m1[:, 0:2 * LEN].rearrange("p (t k) -> p t k", t=2)
                    step = Steps(v, f["vec_s1"], w, 1)
                    step(v.tensor_reduce(smx[:, :], sc, AX_X, ALU.max))
                    v.tensor_tensor(sd[:, :, :], sc, bcast(smx[:, :], LEN, 2), ALU.subtract)\
                        .then_inc(f["s1_ready"], 1)
                shift_quad(q, u + 1, 1)
                if exists(u - 1):
                    add_residual(1, u - 1, 1 - par, x3[1 - par][:, :, :])
                    second_stats(1, u - 1, x3[1 - par])
                if exists(w):
                    v.wait_ge(f["p1_ready"], w + 1)
                    pb = pbd[:, :, :, :].rearrange("p t h k -> p t (h k)")
                    step = Steps(v, f["vec_p1"], w, 2)
                    step(v.tensor_reduce(srs[:, :], pb, AX_X, ALU.add))
                    step(v.reciprocal(srs[:, :], srs[:, :]))
                    v.tensor_tensor(pb, pb, bcast(srs[:, :], P, 2), ALU.mult).then_inc(f["pn_ready"], 1)
                shift_quad(q, u + 1, 2)
                copy_qk(1, u + 2)
                shift_quad(q, u + 1, 3)
                gates = Steps(v, f["gate_steps"], u - 1, GATE)
                if exists(u - 1):
                    gate_norm(u - 1, gates)
                    gate_logits(u - 1, gates)
                    gate_top(u - 1, gates)
                normalise(q, u)
                if exists(u - 1):
                    gate_index(gates)

                def weigh(src, batch, k):
                    v.wait_ge(ring_filled, batch * 8 + k + 1)
                    wait(v, z_used, (batch - 1) * 8 + k + 1)
                    v.tensor_tensor(z[:, 2 * k:2 * k + 2, :],
                                    s_bank[k % QUADS][:, :].rearrange("p (e n) -> p e n", e=2),
                                    bcast(src, 2, 1), ALU.mult).then_inc(ring_used, 1)

                if exists(w):
                    v.wait_ge(f["o1_ready"], w + 1)
                for k in range(E1 // 2):
                    if exists(u - 1):
                        if k == 1:
                            gate_shift(gates)
                        if k == 2:
                            gate_mask(gates)
                        if k == 3:
                            gate_softmax(u - 1, gates)
                        if k == 4:
                            gate_terms(gates)
                    if exists(w):
                        weigh(ohT[:, :], 1 + 2 * w, k)
                if exists(u - 1):
                    v.wait_ge(q["x1T_ready"], u)
                for k in range(E1 // 2):
                    if exists(u - 1):
                        weigh(hnT[:, :], 2 * (u - 1), k)
                    if k == 2 and exists(w):
                        v.wait_ge(z_used, 16 * w + 16)
                        wait(v, out_sem[par], 8 * (w - par))
                        v.scalar_tensor_tensor(out=res[par][:, :, :],
                                               in0=po[:, 0:256].rearrange("p (t n) -> p t n", t=2),
                                               scalar=tg[:, 3:4], in1=x3[par][:, :, :],
                                               op0=ALU.mult, op1=ALU.add).then_inc(f["res_ready"], 1)

            units(v, body1)

        @block.tensor
        def _(pe):
            pe.wait_ge(setup["consts"], 1)
            pe.wait_ge(load["attn"], 16 * 8)
            pe.wait_ge(load["small"], 16 * 15)
            for k in range(4):
                ins = pe.transpose(s_bank[k][:, 0:P], wraw[:, k, :], ident[:, :])
            ins.then_inc(setup["tensor"], 1)
            pe.wait_ge(setup["vec_done"], 2)
            for l in range(2):
                pe.matmul(m1[:, P * l:P * l + P], bvb[:, l, :], wo[l][:, :], start=True, stop=True)
            pe.matmul(m1[:, 256:256 + E1], onesf[:, :], simq[:, :], start=True, stop=True)\
                .then_inc(setup["tensor"], 1)
            pe.wait_ge(setup["vec_done"], 10)

            def since(*users):
                for unit, semaphore, count in users:
                    if exists(unit):
                        pe.wait_ge(semaphore, count)
                        return

            def transpose_in(layer, v, par):
                q = s[layer]
                if exists(v):
                    since((v - 3, q["oT_ready"], v - 2), (v - 1, q["v_ready"], v))
                    pe.wait_ge(ctx_loaded[layer][par], 8 * (v - par + 2))
                    pe.wait_ge(q["xn_ready"], v + 1)
                    for t in range(2):
                        pe.transpose(m0[:, P * t:P * t + P], xn[:, t, :], ident[:, :])
                    for t in range(2):
                        ins = pe.transpose(m0[:, P * (2 + t):P * (3 + t)], cin[par][:, t, :], ident[:, :])
                    ins.then_inc(q["xc_in_psum"], 1)

            def queries_keys(layer, v):
                q = s[layer]
                if exists(v):
                    if layer == 0:
                        since((v - 4, route["rank_steps"], 6 * (v - 4) + 2), (v - 3, q["x_mid_ready"], v - 2),
                              (v - 1, q["qk_ready"], v))
                    else:
                        since((v - 3, q["x_mid_ready"], v - 2), (v - 1, q["qk_ready"], v))
                    pe.wait_ge(q["xcT_ready"], v + 1)
                    pe.matmul(m1[:, 0:256], wq[layer][:, :], xT[:, :], start=True, stop=True)
                    pe.matmul(m1[:, 256:512], wk[layer][:, :], cT[:, :, 0, :], start=True, stop=True)\
                        .then_inc(q["qk_in_psum"], 1)

            def values(layer, v):
                q = s[layer]
                if exists(v):
                    if layer == 1:
                        since((v - 4, f["o1_ready"], v - 3), (v - 3, q["x1T_ready"], v - 2),
                              (v, q["xcT_ready"], v + 1))
                    else:
                        since((v - 3, q["x1T_ready"], v - 2), (v, q["xcT_ready"], v + 1))
                    for seq in range(4):
                        ins = pe.matmul(m0[:, P * seq:P * seq + P], cT[:, seq, :, :].rearrange("c a k -> c (a k)"),
                                        wv[layer][:, :], start=True, stop=True)
                    ins.then_inc(q["v_in_psum"], 1)

            def scores(layer, v, par, j):
                q = s[layer]
                if exists(v):
                    if j == 0:
                        pe.wait_ge(q["qk_ready"], v + 1)
                        if layer == 1:
                            pe.wait_ge(q["pad_row_ready"], v + 1)
                            wait(pe, ring_used, 16 * v - 40)
                    wait(pe, q["scores_ready"], 4 * v - 3 + j)
                    if layer == 0:
                        mask, rows = mask_chunk, LEN
                    else:
                        mask, rows = mask_causal[par], LEN + 2
                    pe.matmul(s_bank[j][:, :], mask_rows[0:rows, :, :], mask[0:rows, :, :], start=True, stop=False,
                              skip_group_check=True)
                    quad = slice(32 * j, 32 * j + 32)
                    for seq in range(4):
                        t, half = divmod(seq, 2)
                        own = slice(LEN * seq, LEN * seq + LEN)
                        ins = pe.matmul(s_bank[j][64 * half:64 * half + 64, UNIT * t:UNIT * t + UNIT], qT[quad, own],
                                        kx[quad, :, own], start=False, stop=True, skip_group_check=True)
                    ins.then_inc(q["scores_in_psum"], 1)

            def transpose_probs(q, u, j):
                if exists(u):
                    pe.wait_ge(q["exp_ready"], 4 * u + j + 1)
                    wait(pe, q["probT_ready"], 4 * u + j)
                    for t in range(2):
                        for r in range(2):
                            col = P * (2 * t + r)
                            ins = pe.transpose(tb[:, col:col + P], prob[j][:, t, 2 * r:2 * r + 2, :], ident[:, :])
                    ins.then_inc(q["probT_in_psum"], 1)

            def weigh_values(q, u, par, j):
                if exists(u):
                    pe.wait_ge(q["probT_ready"], 4 * u + j + 1)
                    if j == 0:
                        pe.wait_ge(q["v_ready"], u + 1)
                        wait(pe, q["heads_ready"], u)
                    apart(pe)
                    for seq in range(4):
                        t, half = divmod(seq, 2)
                        for r in range(2):
                            col = 2 * VW * (8 * t + 2 * j + r)
                            ins = pe.matmul(po[64 * half:64 * half + 64, col:col + 2 * VW],
                                            pT[j % 2][:, t, r, 64 * half:64 * half + 64],
                                            vb[par][:, seq, 2 * j + r, :, :].rearrange("p h c -> p (h c)"),
                                            start=True, stop=True, skip_group_check=True)
                    ins.then_inc(q["pv_in_psum"], 1)

            def transpose_heads(layer, u):
                q = s[layer]
                if exists(u):
                    if layer == 0:
                        since((u + 2, q["v_ready"], u + 3), (u - 1, q["x1T_ready"], u))
                    else:
                        since((u - 1, f["v1_ready"], u), (u + 2, q["v_ready"], u + 3))
                    pe.wait_ge(q["heads_ready"], u + 1)
                    for t in range(2):
                        ins = pe.transpose(m0[:, P * t:P * t + P], on[:, t, :], ident[:, :])
                    ins.then_inc(q["oT_in_psum"], 1)

            def output(layer, u):
                q = s[layer]
                if exists(u):
                    if layer == 0:
                        since((u - 1, route["router_steps"], 5 * (u - 1) + 1), (u + 2, q["qk_ready"], u + 3))
                    else:
                        since((u - 1, f["s1_ready"], u), (u + 2, q["qk_ready"], u + 3))
                    pe.wait_ge(q["oT_ready"], u + 1)
                    for t in range(2):
                        ins = pe.matmul(m1[:, P * t:P * t + P], oT[:, t, :], wo[layer][:, :], start=True, stop=True)
                    ins.then_inc(q["y_in_psum"], 1)

            def normed_transpose(layer, w, src):
                q = s[layer]
                if exists(w):
                    since((w + 3, q["xcT_ready"], w + 4), (w, q["oT_ready"], w + 1))
                    pe.wait_ge(q["xn2_ready"], w + 1)
                    for t in range(2):
                        ins = pe.transpose(m0[:, P * t:P * t + P], src(t), ident[:, :])
                    ins.then_inc(q["x1T_in_psum"], 1)

            def router_logits(w):
                q = s[0]
                if exists(w):
                    since((w + 3, q["qk_ready"], w + 4), (w - 1, route["rank_steps"], 6 * w))
                    pe.wait_ge(q["x1T_ready"], w + 1)
                    for t in range(2):
                        ins = pe.matmul(m1[:, E0 * t:E0 * t + E0], x1T[:, t, :], wr[:, :], start=True, stop=True)
                    ins.then_inc(q["logits_in_psum"], 1)

            def router_rank(w):
                if exists(w):
                    since((w + 1, s[0]["x_mid_ready"], w + 2))
                    pe.wait_ge(route["onehot_ready"], 2 * w + 2)
                    for t in range(2):
                        pe.matmul(m1[:, E0 * t:E0 * t + E0], earlier[:, :], onehot[:, t, :], start=True, stop=False)
                        ins = pe.matmul(m1[:, E0 * t:E0 * t + E0], onesb[:, :], seen[:, t, :], start=False, stop=True)
                    ins.then_inc(route["rank_in_psum"], 1)

            def body0(u, par):
                q = s[0]
                scores(0, u + 1, 1 - par, 0)
                transpose_probs(q, u, 0)
                router_logits(u - 2)
                transpose_heads(0, u - 1)
                scores(0, u + 1, 1 - par, 1)
                transpose_probs(q, u, 1)
                weigh_values(q, u, par, 0)
                output(0, u - 1)
                transpose_in(0, u + 2, par)
                scores(0, u + 1, 1 - par, 2)
                router_rank(u - 2)
                transpose_probs(q, u, 2)
                weigh_values(q, u, par, 1)
                scores(0, u + 1, 1 - par, 3)
                queries_keys(0, u + 2)
                transpose_probs(q, u, 3)
                weigh_values(q, u, par, 2)
                normed_transpose(0, u - 1, lambda t: xr[1 - par][:, t, D:2 * D])
                weigh_values(q, u, par, 3)
                values(0, u + 2)

            units(pe, body0)

            pe.wait_ge(route["pos_ready"], UNITS)
            pe.matmul(m1[:, 0:E0], onesb[:, :], seen[:, 0, :], start=True, stop=True)
            pe.matmul(m1[:, 64:65], earlier[:, :], onesb[:, 0:1], start=True, stop=True)\
                .then_inc(routed["count_in_psum"], 1)
            pe.wait_ge(routed["table"], 2)
            pe.wait_ge(load["moe"], 16 * 4)

            def expert_of(sl):
                return pe.value_load(slot_e[0:1, bass.ds(sl, 1)], min_val=0, max_val=E0 - 1)

            def slot(sl, n, par, rnd):
                if slot_exists(sl):
                    wait(pe, b["hT_ready"], sl)
                    pe.wait_ge(b["gelu_ready"], sl + 1)
                    for j in range(FJ):
                        ins = pe.transpose(tb[:, P * j:P * j + P], hb[par][:, P * j:P * j + P], ident[:, :])
                    ins.then_inc(b["hT_in_psum"], 1)
                if slot_exists(sl + 2):
                    e = expert_of(sl + 2)
                    wait(pe, b["h_ready"], sl + 1)
                    pe.wait_ge(b["xT_ready"], sl + 3)
                    pe.matmul(s_bank[par][:, :], xsT[par][:, :], w1[:, bass.ds(e * F0, F0)], start=True, stop=True)\
                        .then_inc(b["h_in_psum"], 1)
                if slot_exists(sl + 3):
                    nx = (n + 3) % RING0
                    pe.wait_ge(slot_loaded[nx], 16 * (rnd + (n + 3) // RING0 + 1))
                    pe.transpose(m0[:, 0:P], xs[nx][:, D:2 * D], ident[:, :]).then_inc(b["xT_in_psum"], 1)
                if slot_exists(sl):
                    e = expert_of(sl)
                    wait(pe, b["vec_y"], sl)
                    pe.wait_ge(b["hT_ready"], sl + 1)
                    for j in range(FJ):
                        ins = pe.matmul(po[:, 0:D], hT[par][:, P * j:P * j + P],
                                        w2[:, bass.ds((e * FJ + j) * D, D)], start=(j == 0), stop=(j == FJ - 1))
                    ins.then_inc(b["y_in_psum"], 1)

            slots(pe, slot)
            pe.wait_ge(load["experts1"], 16 * 4)
            pe.wait_ge(b["y_ready"], SLOTS)

            def spread(batch, k):
                wait(pe, ring_used, batch * 8 + k - QUADS + 1)
                for e in range(2):
                    ins = pe.matmul(s_bank[k % QUADS][:, 256 * e:256 * e + 256], term_sel[:, 2 * k + e, :],
                                    w3T[:, :], start=True, stop=True)
                ins.then_inc(ring_filled, 1)

            def body1(u, par):
                q = s[1]
                w = u - 2
                scores(1, u + 1, 1 - par, 0)
                transpose_probs(q, u, 0)
                if exists(w):
                    pe.wait_ge(f["qk1_ready"], w + 1)
                    apart(pe)
                    for t in range(2):
                        for half in range(2):
                            seq = slice(LEN * (2 * t + half), LEN * (2 * t + half) + LEN)
                            ins = pe.matmul(m1[64 * half:64 * half + 64, LEN * t:LEN * t + LEN], qkT[:, 0, seq],
                                            qkT[:, 1, seq], start=True, stop=True, skip_group_check=True)
                    ins.then_inc(f["s1_in_psum"], 1)
                transpose_heads(1, u - 1)
                scores(1, u + 1, 1 - par, 1)
                transpose_probs(q, u, 1)
                weigh_values(q, u, par, 0)
                output(1, u - 1)
                transpose_in(1, u + 2, par)
                scores(1, u + 1, 1 - par, 2)
                transpose_probs(q, u, 2)
                weigh_values(q, u, par, 1)
                scores(1, u + 1, 1 - par, 3)
                if exists(w):
                    if exists(u):
                        pe.wait_ge(q["probT_ready"], 4 * u + 3)
                    pe.wait_ge(f["pn_ready"], w + 1)
                    for t in range(2):
                        ins = pe.transpose(tb[:, P * t:P * t + P], pbd[:, t, :, :], ident[:, :])
                    ins.then_inc(f["pT_in_psum"], 1)
                queries_keys(1, u + 2)
                normed_transpose(1, u - 1, lambda t: hn[:, t, :])
                weigh_values(q, u, par, 2)
                if exists(w):
                    pe.wait_ge(f["pT_ready"], w + 1)
                transpose_probs(q, u, 3)
                if exists(u - 1):
                    if exists(u + 1):
                        pe.wait_ge(q["scores_ready"], 4 * u + 5)
                    else:
                        pe.wait_ge(ring_used, 16 * u - 24)
                    pe.wait_ge(q["x1T_ready"], u)
                    for t in range(2):
                        ins = pe.matmul(s_bank[0][:, E1 * t:E1 * t + E1], hnT[:, P * t:P * t + P], simn[:, :],
                                        start=True, stop=True)
                    ins.then_inc(q["logits_in_psum"], 1)
                if exists(w):
                    since((u - 1, q["x1T_ready"], u), (w, f["v1_ready"], w + 1))
                    for t in range(2):
                        ins = pe.matmul(m0[:, P * t:P * t + P], vh[:, t, :], pbT[:, P * t:P * t + P],
                                        start=True, stop=True)
                    ins.then_inc(f["o1_in_psum"], 1)
                weigh_values(q, u, par, 3)
                values(1, u + 2)

                if exists(u - 1):
                    pe.wait_ge(f["gate_logits"], u)
                if exists(u + 1) and (exists(w) or exists(u - 1)):
                    pe.wait_ge(q["scores_ready"], 4 * u + 8)

                def weights_transposed():
                    since((u + 2, q["v_ready"], u + 3), (u - 2, f["o1_ready"], u - 1), (u - 1, q["x1T_ready"], u))
                    pe.wait_ge(f["w3_ready"], u)
                    apart(pe)
                    for t in range(2):
                        ins = pe.transpose(m0_bf[0:3 * E1, P * t:P * t + P], w3[:, t, :, :], identb[:, :])
                    ins.then_inc(f["w3T_in_psum"], 1)

                def first_spreads():
                    pe.wait_ge(f["w3T_ready"], u)
                    for k in range(QUADS - 1):
                        spread(2 * (u - 1), k)

                if exists(w):
                    for k in range(QUADS - 1):
                        spread(1 + 2 * w, k)
                    for k in range(E1 // 2):
                        if k + QUADS - 1 < E1 // 2:
                            spread(1 + 2 * w, k + QUADS - 1)
                        if k == 0:
                            since((u, q["heads_ready"], u + 1))
                        pe.wait_ge(ring_used, (1 + 2 * w) * 8 + k + 1)
                        for e in range(2 * k, 2 * k + 2):
                            for t in range(2):
                                ins = pe.matmul(po[:, P * t:P * t + P], z[:, e, P * t:P * t + P], proj[:, 3, e, :],
                                                start=(e == 0 and t == 0), stop=(e == E1 - 1),
                                                skip_group_check=True)
                        ins.then_inc(z_used, 1)
                        if exists(u - 1):
                            if k == E1 // 2 - 3:
                                weights_transposed()
                            if k == E1 // 2 - 2:
                                first_spreads()
                if exists(u - 1):
                    if not exists(w):
                        weights_transposed()
                        first_spreads()
                    for k in range(E1 // 2):
                        if k + QUADS - 1 < E1 // 2:
                            spread(2 * (u - 1), k + QUADS - 1)
                        if k == 0:
                            since((u + 2, q["qk_ready"], u + 3), (u - 1, q["x_mid_ready"], u))
                        pe.wait_ge(ring_used, 2 * (u - 1) * 8 + k + 1)
                        for e in range(2 * k, 2 * k + 2):
                            first, last = e == 0, e == E1 - 1
                            for c in range(2):
                                pe.matmul(m1[:, 256 * c:256 * c + 256], proj[:, c, e, :], z[:, e, :],
                                          start=(first and c == 0), stop=last, skip_group_check=True)
                            for t in range(2):
                                ins = pe.matmul(m0[:, P * t:P * t + P], z[:, e, P * t:P * t + P], proj[:, 2, e, :],
                                                start=(first and t == 0), stop=last, skip_group_check=True)
                        ins.then_inc(z_used, 1)

            units(pe, body1)


def kernel(**inputs):
    import numpy as _np
    import concourse.bacc as _bacc
    from concourse import mybir as _mybir
    from concourse.bass_utils import run_bass_kernel_spmd as _run

    nc = _bacc.Bacc("TRN2", target_bir_lowering=False, num_devices=1)
    arrays, args = {}, {}
    for name in inputs:
        x = _np.ascontiguousarray(inputs[name])
        if name in ("x", "ctx_1024"):
            x = x.reshape(-1, x.shape[-1])
        arrays[f"in_{name}"] = x
        args[name] = nc.dram_tensor(f"in_{name}", x.shape, _mybir.dt.from_np(x.dtype), kind="ExternalInput").ap()
    shape = _np.shape(inputs["x"])
    out = nc.dram_tensor("out_x", (shape[0] * shape[1], shape[2]), _mybir.dt.float32, kind="ExternalOutput").ap()
    flamingo(nc, args, out)
    r = _run(nc, [arrays], core_ids=[0])
    return r.results[0]["out_x"].reshape(shape)
```
